# Optimizing a Trainium2 kernel written in Bass

```python
import numpy as np
import jax
import jax.numpy as jnp

def _softmax(x, axis=-1):
    return jax.nn.softmax(x, axis=axis)

def _gelu(x):
    return jax.nn.gelu(x, approximate=True)

def _silu(x):
    return jax.nn.silu(x)

def _sigmoid(x):
    return jax.nn.sigmoid(x)

def _layernorm(x, axis=-1, eps=1e-05):
    m = jnp.mean(x, axis=axis, keepdims=True)
    v = jnp.var(x, axis=axis, keepdims=True)
    return (x - m) / jnp.sqrt(v + eps)

def _scatter_add(tgt, idx, src, axis=0):
    return tgt.at[idx].add(src)

def _segment_sum(src, seg, n):
    return jax.ops.segment_sum(src, seg, n)
kernel_name = 'mk_gnn_resnorm_d4_gnn_r16_6ef9b5'

def setup_inputs(seed: int=0):
    np.random.seed(seed)
    _w = jnp.asarray

    def _rec_inputs():
        import jax
        import jax.numpy as jnp
        _gk = jax.random.key(seed)
        x = -6.415e-05 + 1 * jax.random.normal(jax.random.fold_in(_gk, 1), (3125, 512), jnp.float32)
        src = jax.random.randint(jax.random.fold_in(_gk, 2), (50000,), 0, 3125, jnp.int32)
        dst = jnp.minimum((3125 * jax.random.uniform(jax.random.fold_in(_gk, 3), (50000,)) ** 2.0).astype(jnp.int32), 49999)
        _o = jnp.argsort(dst, stable=True)
        src = src[_o]
        dst = dst[_o]
        edge_attr_4 = 0.000126197 + 0.999763 * jax.random.normal(jax.random.fold_in(_gk, 11), (50000, 4), jnp.float32)
        edge_weight = jax.random.uniform(jax.random.fold_in(_gk, 13), (50000,), jnp.float32, 0.0, 0.999998)
        return (x, src, dst, edge_attr_4, edge_weight)
    x, src, dst, edge_attr_4, edge_weight = _rec_inputs()

    def _L0_gnn_setup():
        import jax, jax.numpy as jnp
        import numpy as np
        N = 1250
        E = 20000
        IN = 512
        H = 4
        C = 128
        ED = 4
        NEG_SLOPE = 0.2
        BN_EPS = 1e-05

        def _edge_gat(x, edge_index, edge_attr, W, W_edge, att_src, att_dst, att_edge, bias, gamma, beta):
            n = x.shape[0]
            loop = jnp.arange(n, dtype=edge_index.dtype)
            src = jnp.concatenate([edge_index[0], loop])
            dst = jnp.concatenate([edge_index[1], loop])
            ea = jnp.concatenate([edge_attr, jnp.broadcast_to(edge_attr.mean(0), (n, edge_attr.shape[1]))], 0)
            h = (x @ W).reshape(n, H, C)
            a_src = (h * att_src[None]).sum(-1)
            a_dst = (h * att_dst[None]).sum(-1)
            e = (ea @ W_edge).reshape(-1, H, C)
            a_edge = (e * att_edge[None]).sum(-1)
            alpha = a_src[src] + a_dst[dst] + a_edge
            alpha = jax.nn.leaky_relu(alpha, NEG_SLOPE)
            amax = jax.lax.stop_gradient(jax.ops.segment_max(alpha, dst, num_segments=n))
            ex = jnp.exp(alpha - amax[dst])
            denom = jax.ops.segment_sum(ex, dst, num_segments=n)
            att = ex / (denom[dst] + 1e-16)
            msg = h[src] * att[:, :, None]
            out = jax.ops.segment_sum(msg, dst, num_segments=n).reshape(n, H * C) + bias
            mu = out.mean(0)
            var = out.var(0)
            return (out - mu) / jnp.sqrt(var + BN_EPS) * gamma + beta
        key = jax.random.key(seed)
        ks = jax.random.split(key, 10)
        x = jax.random.normal(ks[0], (N, IN), dtype=jnp.float32)
        edge_index = jax.random.randint(ks[1], (2, E), 0, N, dtype=jnp.int64)
        edge_attr = jax.random.normal(ks[2], (E, ED), dtype=jnp.float32)
        W = jax.random.normal(ks[3], (IN, H * C), dtype=jnp.float32) / np.sqrt(IN)
        W_edge = jax.random.normal(ks[4], (ED, H * C), dtype=jnp.float32) / np.sqrt(ED)
        att_src = jax.random.normal(ks[5], (H, C), dtype=jnp.float32) / np.sqrt(C)
        att_dst = jax.random.normal(ks[6], (H, C), dtype=jnp.float32) / np.sqrt(C)
        att_edge = jax.random.normal(ks[7], (H, C), dtype=jnp.float32) / np.sqrt(C)
        bias = jnp.zeros((H * C,), dtype=jnp.float32)
        gamma = jnp.ones((H * C,), dtype=jnp.float32)
        beta = jnp.zeros((H * C,), dtype=jnp.float32)
        return {'x': x, 'edge_index': edge_index, 'edge_attr': edge_attr, 'W': W, 'W_edge': W_edge, 'att_src': att_src, 'att_dst': att_dst, 'att_edge': att_edge, 'bias': bias, 'gamma': gamma, 'beta': beta}
    _L0_gnn_all = _L0_gnn_setup()
    _L0_gnn_in = {k: v for k, v in _L0_gnn_all.items() if k in ('W', 'W_edge', 'att_src', 'att_dst', 'att_edge', 'bias', 'gamma', 'beta')}
    del _L0_gnn_all

    def _L1_gnn_setup():
        import jax, jax.numpy as jnp
        import numpy as np
        EPS = 1e-12

        def _gcn_conv(x, W, b, src, dst, w, n_nodes):
            h = x @ W
            deg = jax.ops.segment_sum(w, dst, num_segments=n_nodes)
            dinv = jnp.where(deg > 0, jax.lax.rsqrt(deg), 0.0)
            norm = dinv[src] * w * dinv[dst]
            out = jax.ops.segment_sum(h[src] * norm[:, None], dst, num_segments=n_nodes)
            return out + b
        key = jax.random.key(seed)
        ks = jax.random.split(key, 6)
        N, E, F_in, F_hid, F_out = (3125, 25000, 512, 256, 512)
        node_features = jax.random.normal(ks[0], (N, F_in), dtype=jnp.float32)
        node_features = node_features / jnp.linalg.norm(node_features, axis=-1, keepdims=True)
        edge_index = jax.random.randint(ks[1], (2, E), 0, N, dtype=jnp.int64)
        edge_weight = jax.random.uniform(ks[2], (E,), dtype=jnp.float32)
        W1 = jax.random.normal(ks[3], (F_in, F_hid), dtype=jnp.float32) / np.sqrt(F_in)
        b1 = jnp.zeros((F_hid,), dtype=jnp.float32)
        W2 = jax.random.normal(ks[4], (F_hid, F_out), dtype=jnp.float32) / np.sqrt(F_hid)
        b2 = jnp.zeros((F_out,), dtype=jnp.float32)
        return {'node_features': node_features, 'edge_index': edge_index, 'edge_weight': edge_weight, 'W1': W1, 'b1': b1, 'W2': W2, 'b2': b2}
    _L1_gnn_all = _L1_gnn_setup()
    _L1_gnn_in = {k: v for k, v in _L1_gnn_all.items() if k in ('W1', 'b1', 'W2', 'b2')}
    del _L1_gnn_all

    def _L2_gnn_setup():
        import jax, jax.numpy as jnp
        import numpy as np
        key = jax.random.key(seed)
        ks = jax.random.split(key, 8)
        n_nodes, n_edges, in_dim, out_dim = (3125, 25000, 512, 512)
        x = jax.random.normal(ks[0], (n_nodes, in_dim), dtype=jnp.float32)
        edge_index = jax.random.randint(ks[1], (2, n_edges), 0, n_nodes, dtype=jnp.int64)
        edge_weight = jax.random.uniform(ks[2], (n_edges,), dtype=jnp.float32)
        s = 1.0 / np.sqrt(in_dim)
        W_self = jax.random.uniform(ks[3], (out_dim, in_dim), minval=-s, maxval=s, dtype=jnp.float32)
        b_self = jax.random.uniform(ks[4], (out_dim,), minval=-s, maxval=s, dtype=jnp.float32)
        W_neigh = jax.random.uniform(ks[5], (out_dim, in_dim), minval=-s, maxval=s, dtype=jnp.float32)
        b_neigh = jax.random.uniform(ks[6], (out_dim,), minval=-s, maxval=s, dtype=jnp.float32)
        return {'x': x, 'edge_index': edge_index, 'edge_weight': edge_weight, 'W_self': W_self, 'b_self': b_self, 'W_neigh': W_neigh, 'b_neigh': b_neigh}
    _L2_gnn_all = _L2_gnn_setup()
    _L2_gnn_in = {k: v for k, v in _L2_gnn_all.items() if k in ('W_self', 'b_self', 'W_neigh', 'b_neigh')}
    del _L2_gnn_all

    def _L3_gnn_setup():
        import jax, jax.numpy as jnp
        import numpy as np
        N_NODES = 3125
        N_EDGES = 100000
        IN_F = 512
        OUT_F = 512
        key = jax.random.key(seed)
        k1, k2, k3, k4, k5 = jax.random.split(key, 5)
        input = jax.random.normal(k1, (N_NODES, IN_F), dtype=jnp.float32)
        edge_index = jax.random.randint(k2, (2, N_EDGES), 0, N_NODES, dtype=jnp.int64)
        edge_vals = jax.random.uniform(k3, (N_EDGES,), dtype=jnp.float32)
        stdv = 1.0 / np.sqrt(OUT_F)
        weight = jax.random.uniform(k4, (IN_F, OUT_F), dtype=jnp.float32, minval=-stdv, maxval=stdv)
        bias = jax.random.uniform(k5, (OUT_F,), dtype=jnp.float32, minval=-stdv, maxval=stdv)
        return {'input': input, 'edge_index': edge_index, 'edge_vals': edge_vals, 'weight': weight, 'bias': bias}
    _L3_gnn_all = _L3_gnn_setup()
    _L3_gnn_in = {k: v for k, v in _L3_gnn_all.items() if k in ('weight', 'bias')}
    del _L3_gnn_all
    return {'x': x, 'src': src, 'dst': dst, 'edge_attr_4': edge_attr_4, 'edge_weight': edge_weight, 'L0_gnn_W': _L0_gnn_in['W'], 'L0_gnn_W_edge': _L0_gnn_in['W_edge'], 'L0_gnn_att_src': _L0_gnn_in['att_src'], 'L0_gnn_att_dst': _L0_gnn_in['att_dst'], 'L0_gnn_att_edge': _L0_gnn_in['att_edge'], 'L0_gnn_bias': _L0_gnn_in['bias'], 'L0_gnn_gamma': _L0_gnn_in['gamma'], 'L0_gnn_beta': _L0_gnn_in['beta'], 'L1_gnn_W1': _L1_gnn_in['W1'], 'L1_gnn_b1': _L1_gnn_in['b1'], 'L1_gnn_W2': _L1_gnn_in['W2'], 'L1_gnn_b2': _L1_gnn_in['b2'], 'L2_gnn_W_self': _L2_gnn_in['W_self'], 'L2_gnn_b_self': _L2_gnn_in['b_self'], 'L2_gnn_W_neigh': _L2_gnn_in['W_neigh'], 'L2_gnn_b_neigh': _L2_gnn_in['b_neigh'], 'L3_gnn_weight': _L3_gnn_in['weight'], 'L3_gnn_bias': _L3_gnn_in['bias']}

def reference(x, src, dst, edge_attr_4, edge_weight, L0_gnn_W, L0_gnn_W_edge, L0_gnn_att_src, L0_gnn_att_dst, L0_gnn_att_edge, L0_gnn_bias, L0_gnn_gamma, L0_gnn_beta, L1_gnn_W1, L1_gnn_b1, L1_gnn_W2, L1_gnn_b2, L2_gnn_W_self, L2_gnn_b_self, L2_gnn_W_neigh, L2_gnn_b_neigh, L3_gnn_weight, L3_gnn_bias):
    import jax
    import jax.numpy as jnp

    def _L0_gnn_ref(x, edge_index, edge_attr, W, W_edge, att_src, att_dst, att_edge, bias, gamma, beta):
        import jax, jax.numpy as jnp
        import numpy as np
        N = 1250
        E = 20000
        IN = 512
        H = 4
        C = 128
        ED = 4
        NEG_SLOPE = 0.2
        BN_EPS = 1e-05

        def _edge_gat(x, edge_index, edge_attr, W, W_edge, att_src, att_dst, att_edge, bias, gamma, beta):
            n = x.shape[0]
            loop = jnp.arange(n, dtype=edge_index.dtype)
            src = jnp.concatenate([edge_index[0], loop])
            dst = jnp.concatenate([edge_index[1], loop])
            ea = jnp.concatenate([edge_attr, jnp.broadcast_to(edge_attr.mean(0), (n, edge_attr.shape[1]))], 0)
            h = (x @ W).reshape(n, H, C)
            a_src = (h * att_src[None]).sum(-1)
            a_dst = (h * att_dst[None]).sum(-1)
            e = (ea @ W_edge).reshape(-1, H, C)
            a_edge = (e * att_edge[None]).sum(-1)
            alpha = a_src[src] + a_dst[dst] + a_edge
            alpha = jax.nn.leaky_relu(alpha, NEG_SLOPE)
            amax = jax.lax.stop_gradient(jax.ops.segment_max(alpha, dst, num_segments=n))
            ex = jnp.exp(alpha - amax[dst])
            denom = jax.ops.segment_sum(ex, dst, num_segments=n)
            att = ex / (denom[dst] + 1e-16)
            msg = h[src] * att[:, :, None]
            out = jax.ops.segment_sum(msg, dst, num_segments=n).reshape(n, H * C) + bias
            mu = out.mean(0)
            var = out.var(0)
            return (out - mu) / jnp.sqrt(var + BN_EPS) * gamma + beta
        return _edge_gat(x, edge_index, edge_attr, W, W_edge, att_src, att_dst, att_edge, bias, gamma, beta)

    def _L1_gnn_ref(node_features, edge_index, edge_weight, W1, b1, W2, b2):
        import jax, jax.numpy as jnp
        import numpy as np
        EPS = 1e-12

        def _gcn_conv(x, W, b, src, dst, w, n_nodes):
            h = x @ W
            deg = jax.ops.segment_sum(w, dst, num_segments=n_nodes)
            dinv = jnp.where(deg > 0, jax.lax.rsqrt(deg), 0.0)
            norm = dinv[src] * w * dinv[dst]
            out = jax.ops.segment_sum(h[src] * norm[:, None], dst, num_segments=n_nodes)
            return out + b
        N = node_features.shape[0]
        loop = jnp.arange(N, dtype=edge_index.dtype)
        src = jnp.concatenate([edge_index[0], loop])
        dst = jnp.concatenate([edge_index[1], loop])
        w = jnp.concatenate([edge_weight, jnp.ones((N,), dtype=edge_weight.dtype)])
        x = _gcn_conv(node_features, W1, b1, src, dst, w, N)
        x = jax.nn.relu(x)
        x = _gcn_conv(x, W2, b2, src, dst, w, N)
        nrm = jnp.linalg.norm(x, axis=-1, keepdims=True)
        return x / jnp.maximum(nrm, EPS)

    def _L2_gnn_ref(x, edge_index, edge_weight, W_self, b_self, W_neigh, b_neigh):
        import jax, jax.numpy as jnp
        import numpy as np
        n_nodes = x.shape[0]
        row, col = (edge_index[0], edge_index[1])
        msg = x[row] * edge_weight[:, None]
        x_neigh = jax.ops.segment_sum(msg, col, num_segments=n_nodes)
        degree = jax.ops.segment_sum(edge_weight, col, num_segments=n_nodes)
        degree = jnp.maximum(degree, 1.0)
        x_neigh = x_neigh / degree[:, None]
        x_self = x @ W_self.T + b_self
        x_neigh = x_neigh @ W_neigh.T + b_neigh
        return x_self + x_neigh

    def _L3_gnn_ref(input, edge_index, edge_vals, weight, bias):
        import jax, jax.numpy as jnp
        import numpy as np
        N_NODES = 3125
        N_EDGES = 100000
        IN_F = 512
        OUT_F = 512
        support = jnp.matmul(input, weight)
        dst, src = (edge_index[0], edge_index[1])
        messages = support[src] * edge_vals[:, None]
        output = jax.ops.segment_sum(messages, dst, num_segments=input.shape[0])
        return output + bias
    edge_index = jnp.stack([src, dst])
    x = _layernorm(x + _L0_gnn_ref(x, edge_index, edge_attr_4, L0_gnn_W, L0_gnn_W_edge, L0_gnn_att_src, L0_gnn_att_dst, L0_gnn_att_edge, L0_gnn_bias, L0_gnn_gamma, L0_gnn_beta), axis=-1)
    x = _layernorm(x + _L1_gnn_ref(x, edge_index, edge_weight, L1_gnn_W1, L1_gnn_b1, L1_gnn_W2, L1_gnn_b2), axis=-1)
    x = _layernorm(x + _L2_gnn_ref(x, edge_index, edge_weight, L2_gnn_W_self, L2_gnn_b_self, L2_gnn_W_neigh, L2_gnn_b_neigh), axis=-1)
    x = _layernorm(x + _L3_gnn_ref(x, edge_index, edge_weight, L3_gnn_weight, L3_gnn_bias), axis=-1)
    return x

_drawn_inputs = setup_inputs


def setup_inputs(seed=0):
    import zlib

    import numpy as np

    out = dict(_drawn_inputs(seed))
    spreads = {'L0_gnn_bias': (0.0, 0.8),
     'L0_gnn_gamma': (1.0, 0.2),
     'L0_gnn_beta': (0.0, 0.1),
     'L1_gnn_b1': (0.0, 0.1),
     'L1_gnn_b2': (0.0, 0.1)}
    factors = {'L3_gnn_bias': 4.457}
    for name, (base, spread) in spreads.items():
        noise = np.random.default_rng([zlib.crc32(name.encode()), seed]).standard_normal(out[name].shape)
        drawn = base * np.exp(spread * noise) if base else spread * noise
        out[name] = jnp.asarray(drawn.astype(out[name].dtype))
    for name, factor in factors.items():
        out[name] = (out[name] * factor).astype(out[name].dtype)
    return out
```

```python
from contextlib import ExitStack

import concourse.bass as bass
from concourse import mybir

FP = mybir.dt.float32
I32 = mybir.dt.int32
BF = mybir.dt.bfloat16
ALU = mybir.AluOpType
ACT = mybir.ActivationFunctionType
AX = mybir.AxisListType

P = 128
N_NODES, F, HEADS, N_EDGES, HID = 3125, 512, 4, 50000, 256
C = F // HEADS
NT = -(-N_NODES // P)
NODES_PAD = NT * P
LAST_ROWS = N_NODES - (NT - 1) * P
BT = 8
EC = -(-N_EDGES // (P * BT)) * BT
EDGES_PAD = P * EC
TILES_USED = (N_EDGES + NT * (P - 1)) // P
TILES = -(-TILES_USED // (2 * BT)) * 2 * BT
TILES_PAD = TILES + BT
TC = TILES_PAD + -(-(EDGES_PAD - N_EDGES) // P)
REC = 8
R_LOCAL, R_OTHER, R_W, R_EA = 0, 1, 2, 4
NEG_SLOPE, EPS_BN, EPS_LN, EPS_DEN, EPS_NORM = 0.2, 1e-5, 1e-5, 1e-16, 1e-12
MASKED = -1e30
ACCW = F + BT
DEN, DEG = F, F + HEADS
TINY = 1e-30


class Chain:

    def __init__(self, eng, sem, base=0):
        self.eng, self.sem, self.base, self.n = eng, sem, base, 0

    def run(self, instruction):
        instruction.then_inc(self.sem, 1)
        self.n += 1
        self.eng.wait_ge(self.sem, self.base + self.n)


def tiles_ahead(eng, first, second):
    first(0, 0)
    with eng.Fori(0, (NT - 1) // 4) as i:
        t = i * 4
        for q in range(4):
            first(t + (q + 1), (q + 1) % 4)
            second(t + q, q)
    second(NT - 1, 0)


def batches_ahead(eng, first, second, third):
    first(0, 0)
    third(0, 0)
    with eng.Fori(0, TILES // BT // 2) as i:
        g = i * 2
        first(g + 1, 1)
        second(g, 0)
        third(g + 1, 1)
        first(g + 2, 0)
        second(g + 1, 1)
        third(g + 2, 0)


def nothing(t, q):
    pass


def uses4(t, q, each):
    return (t - q) * (each // 4) + each


def col(ap, j, n=1):
    return ap[:, bass.ds(j, n)]


def bucket_registers(nc, engine, buckets, j):
    _, values = nc.values_load_multi_w_load_instructions(
        buckets[0:1, bass.ds(j, BT)], engines=[engine], min_val=0, max_val=NT - 1,
        skip_runtime_bounds_check_because="the node tile numbers are clamped")
    return values


class Scope:

    def __init__(self, nc, name):
        self.nc, self.name, self.ctx, self.sems = nc, name, ExitStack(), []

    def __enter__(self):
        return self

    def __exit__(self, *exc):
        if self.sems and exc[0] is None:
            self.nc.clear_and_free_semaphores(self.sems)
            self.nc.all_engine_barrier(sem_only=True)
        self.ctx.close()

    def sb(self, name, shape, dt=FP):
        return self.ctx.enter_context(self.nc.sbuf_tensor(f"{self.name}_{name}", shape, dt))

    def ps(self, name, shape):
        return self.ctx.enter_context(self.nc.psum_tensor(f"{self.name}_{name}", shape, FP))

    def sem(self, name):
        self.sems.append(self.nc.alloc_semaphore(f"{self.name}_{name}"))
        return self.sems[-1]


def constants(nc, k):
    with Scope(nc, "cst") as s:
        ii = s.sb("ii", [P, P], I32)
        ic = s.sb("ic", [P, TILES_PAD], I32)
        ie = s.sb("ie", [P, EC], I32)
        pf = s.sb("pf", [P, P])
        ef = s.sb("ef", [P, EC])
        made = s.sem("made")
        own = s.sem("own")
        with nc.Block() as block:
            @block.gpsimd
            def _(pool):
                pool.iota(ii[:, :], [[0, P]], base=0, channel_multiplier=1).then_inc(made, 1)
                pool.iota(ic[:, :], [[1, TILES_PAD]], base=0, channel_multiplier=0).then_inc(made, 1)
                pool.iota(ie[:, :], [[1, EC]], base=0, channel_multiplier=EC).then_inc(made, 1)

            @block.vector
            def _(dve):
                own_chain = Chain(dve, own)
                dve.wait_ge(made, 3)
                dve.tensor_copy(pf[:, :], ii[:, :])
                dve.tensor_copy(ef[:, :], ie[:, :])
                own_chain.run(dve.tensor_copy(k.columns[:, :], ic[:, :]))
                dve.tensor_tensor(k.ident[:, :], k.columns[:, 0:P], pf[:, :], ALU.is_equal)
                dve.tensor_tensor(k.before[:, :], k.columns[:, 0:P], pf[:, :], ALU.is_gt)
                dve.memset(k.ones[:, :], 1.0)
                dve.tensor_scalar(k.last_rows[:, :], pf[:, :], float(LAST_ROWS), None, ALU.is_lt)
                own_chain.run(dve.tensor_scalar(k.pad_slot[:, :], ef[:, :], float(N_EDGES), None, ALU.is_ge))
                own_chain.run(dve.tensor_scalar(ef[:, :], ef[:, :], float(TILES_PAD * P - N_EDGES), None, ALU.add))
                dve.tensor_tensor(k.pad_slot[:, :], k.pad_slot[:, :], ef[:, :], ALU.mult)
    return


def place(nc, k, name, key_dram, slots, buckets, records, other_dram):
    with Scope(nc, name) as s:
        key, other = s.sb("key", [P, EC], I32), s.sb("other", [P, EC], I32)
        key_i, key_f, low_f = s.sb("key_i", [P, EC], I32), s.sb("key_f", [P, EC]), s.sb("low_f", [P, EC])
        ohot = s.sb("ohot", [P, NT, EC], BF)
        seen = s.sb("seen", [P, TILES_PAD * NT])
        ends, cnt = s.sb("ends", [P, NT + 1]), s.sb("cnt", [P, NT])
        tiles_i, tiles_f = s.sb("tiles_i", [P, NT], I32), s.sb("tiles_f", [P, NT])
        last, start, off = s.sb("last", [P, NT]), s.sb("start", [P, NT]), s.sb("off", [P, NT])
        tile_f = s.sb("tile_f", [P, TILES_PAD])
        p_cnt = s.ps("p_cnt", [P, 2 * NT])
        loaded, own, counted, summed = s.sem("loaded"), s.sem("own"), s.sem("counted"), s.sem("summed")
        with nc.Block() as block:
            @block.sync
            def _(sp):
                sp.dma_start(key[:, :], key_dram).then_inc(loaded, 16)
                sp.dma_start(other[:, :], other_dram).then_inc(loaded, 16)

            @block.tensor
            def _(pe):
                pe.wait_ge(counted, 1)
                pe.matmul(p_cnt[:, 0:NT], k.before[:, :], cnt[:, :], start=True, stop=True)
                pe.matmul(p_cnt[:, NT:2 * NT], k.ones[:, :], cnt[:, :], start=True, stop=True).then_inc(summed, 1)

            @block.vector
            def _(dve):
                c = Chain(dve, own)
                dve.wait_ge(loaded, 32)
                dve.tensor_copy(records[:, :, R_OTHER].bitcast(I32), other[:, :])
                c.run(dve.tensor_scalar(key_i[:, :], key[:, :], 7, None, ALU.arith_shift_right))
                c.run(dve.tensor_copy(key_f[:, :], key_i[:, :]))
                c.run(dve.tensor_scalar(key_i[:, :], key[:, :], P - 1, None, ALU.bitwise_and))
                dve.tensor_copy(records[:, :, R_LOCAL], key_i[:, :])
                c.run(dve.tensor_tensor(
                    ohot[:, :, :], key_f[:, :].unsqueeze(1).broadcast_to([P, NT, EC]),
                    k.columns[:, 0:NT].unsqueeze(2).broadcast_to([P, NT, EC]), ALU.is_equal))
                flat = ohot[:, :, :].rearrange("p b c -> p (b c)")
                c.run(dve.tensor_tensor_scan(seen[:, 0:NT * EC], flat, flat, 0.0, ALU.add, ALU.max))
                seen_bc = seen[:, 0:NT * EC].rearrange("p (b c) -> p b c", b=NT)
                dve.memset(ends[:, 0:1], 0.0)
                c.run(dve.tensor_copy(ends[:, 1:NT + 1], seen_bc[:, :, EC - 1]))
                dve.tensor_tensor(cnt[:, :], ends[:, 1:NT + 1], ends[:, 0:NT], ALU.subtract).then_inc(counted, 1)
                dve.wait_ge(summed, 1)
                c.run(dve.tensor_scalar(tiles_i[:, :], p_cnt[:, NT:2 * NT], float(P - 1), None, ALU.add))
                c.run(dve.tensor_scalar(tiles_i[:, :], tiles_i[:, :], 7, None, ALU.arith_shift_right))
                c.run(dve.tensor_copy(tiles_f[:, :], tiles_i[:, :]))
                c.run(dve.tensor_tensor_scan(last[:, :], tiles_f[:, :], tiles_f[:, :], 0.0, ALU.add, ALU.max))
                c.run(dve.tensor_tensor(start[:, :], last[:, :], tiles_f[:, :], ALU.subtract))
                c.run(dve.scalar_tensor_tensor(off[:, :], start[:, :], float(P), p_cnt[:, 0:NT], ALU.mult, ALU.add))
                c.run(dve.scalar_tensor_tensor(off[:, :], off[:, :], -1.0, ends[:, 0:NT], ALU.add, ALU.subtract))
                c.run(dve.tensor_tensor(seen_bc, seen_bc, off[:, :].unsqueeze(2).broadcast_to([P, NT, EC]), ALU.add))
                c.run(dve.tensor_tensor(seen_bc, seen_bc, ohot[:, :, :], ALU.mult))
                c.run(dve.tensor_reduce(key_f[:, :], seen_bc.rearrange("p b c -> p c b"), AX.X, ALU.add))
                c.run(dve.tensor_tensor(key_f[:, :], key_f[:, :], k.pad_slot[:, :], ALU.add))
                c.run(dve.tensor_copy(slots[:, :], key_f[:, :]))
                c.run(dve.tensor_scalar(key_i[:, :], slots[:, :], 7, None, ALU.arith_shift_right))
                c.run(dve.tensor_copy(key_f[:, :], key_i[:, :]))
                c.run(dve.tensor_scalar(slots[:, :], slots[:, :], P - 1, None, ALU.bitwise_and))
                c.run(dve.tensor_copy(low_f[:, :], slots[:, :]))
                c.run(dve.scalar_tensor_tensor(slots[:, :], low_f[:, :], float(TC), key_f[:, :], ALU.mult, ALU.add))
                ended = seen[:, 0:TILES_PAD * NT].rearrange("p (j b) -> p j b", b=NT)
                c.run(dve.tensor_tensor(
                    ended, last[:, :].unsqueeze(1).broadcast_to([P, TILES_PAD, NT]),
                    k.columns[:, :].unsqueeze(2).broadcast_to([P, TILES_PAD, NT]), ALU.is_le))
                c.run(dve.tensor_reduce(tile_f[:, :], ended, AX.X, ALU.add))
                c.run(dve.tensor_scalar(buckets[:, :], tile_f[:, :], float(NT - 1), None, ALU.min))


def scatter_records(nc, name, records, slots, table, blank):
    with Scope(nc, name) as s:
        rec = s.sb("rec", [P, 2, BT, REC])
        row = s.sb("row", [P, 2, BT], I32)
        blanked, staged = s.sem("blanked"), s.sem("staged")
        written = [s.sem(f"written{h}") for h in range(2)]
        issued = s.sem("issued")
        batches = EC // BT
        with nc.Block() as block:
            @block.sync
            def _(sp):
                sp.dma_start(table.rearrange("(l t) f -> l (t f)", l=P), blank[:, :]).then_inc(blanked, 16)

            @block.scalar
            def _(act):
                def stage(g, h, reused=True):
                    if reused:
                        act.wait_ge(written[h], (g - h) * (BT * 16 // 2))
                    act.copy(row[:, h, :], col(slots, g * BT, BT))
                    act.copy(rec[:, h, :, :], col(records, g * BT, BT)).then_inc(staged, 1)

                stage(0, 0, reused=False)
                stage(1, 1, reused=False)
                with act.Fori(1, (batches - 1) // 2) as i:
                    g = i * 2
                    stage(g, 0)
                    stage(g + 1, 1)
                stage(batches - 1, 0)

            @block.gpsimd
            def _(pool):
                pool.wait_ge(blanked, 16)

                def scatter(g, h):
                    pool.wait_ge(staged, g + 1)
                    pool.sem_inc(issued, 1)
                    for n in range(BT):
                        pool.indirect_dma_start(
                            table, bass.IndirectOffsetOnAxis(row[:, h, n:n + 1], 0),
                            rec[:, h, n, :], None).then_inc(written[h], 16)

                with pool.Fori(0, (batches - 1) // 2) as i:
                    g = i * 2
                    scatter(g, 0)
                    scatter(g + 1, 1)
                scatter(batches - 1, 0)
                pool.wait_ge(written[0], (batches + 1) // 2 * BT * 16)
                pool.wait_ge(written[1], batches // 2 * BT * 16)


def load_records(nc, name, table, rec):
    with Scope(nc, name) as s:
        loaded = s.sem("loaded")
        with nc.Block() as block:
            @block.sync
            def _(sp):
                sp.dma_start(rec[:, :, :].rearrange("p t f -> p (t f)"),
                             table.rearrange("(l t) f -> l (t f)", l=P)[:, 0:TILES_PAD * REC]).then_inc(loaded, 16)
                sp.wait_ge(loaded, 16)


def aggregate(nc, k, name, rec, buckets, table, width, acc, clear):
    RING, AHEAD = 4, 2
    with Scope(nc, name) as s:
        rows = s.sb("rows", [P, BT, width])
        index = s.sb("index", [P, 2, BT], I32)
        hot = s.sb("hot", [P, RING, P])
        part = [s.ps(f"part{i}", [P, F]) for i in range(RING)]
        gathered = [s.sem(f"gathered{n}") for n in range(BT)]
        indexed, granted, hot_ready = s.sem("indexed"), s.sem("granted"), s.sem("hot_ready")
        summed, added, cleared = s.sem("summed"), s.sem("added"), s.sem("cleared")
        other = rec[:, :, R_OTHER].bitcast(I32)
        with nc.Block() as block:
            @block.scalar
            def _(act):
                with act.Fori(0, TILES // BT // 2) as i:
                    g = i * 2
                    for h in range(2):
                        act.wait_ge(summed, g * BT + BT * (h + 1))
                        act.copy(index[:, h, :], col(other, g * BT + BT * h, BT)).then_inc(indexed, 1)

            @block.gpsimd
            def _(pool):
                with pool.Fori(0, TILES // BT // 2) as i:
                    g = i * 2
                    for h in range(2):
                        pool.wait_ge(indexed, g + (h + 1))
                        for n in range(BT):
                            pool.wait_ge(summed, g * BT + (h * BT + n + 1 + BT))
                            pool.sem_inc(granted, 1)
                            pool.indirect_dma_start(
                                rows[:, n, :], None, table,
                                bass.IndirectOffsetOnAxis(index[:, h, n:n + 1], 0)).then_inc(gathered[n], 16)

            @block.vector
            def _(dve):
                def weigh(j, n):
                    dve.tensor_scalar(hot[:, n % RING, :], k.columns[:, 0:P], col(rec[:, :, R_LOCAL], j),
                                      col(rec[:, :, R_W], j), ALU.is_equal, ALU.mult).then_inc(hot_ready, 1)

                if clear:
                    dve.memset(acc[:, :, 0:width], 0.0).then_inc(cleared, 1)
                    dve.wait_ge(cleared, 1)
                for n in range(AHEAD):
                    weigh(n, n)
                with dve.Fori(0, TILES // BT // 2) as i:
                    g = i * 2
                    for h in range(2):
                        tile = bucket_registers(nc, mybir.EngineType.DVE, buckets, g * BT + h * BT)
                        for n in range(BT):
                            u = h * BT + n
                            dve.wait_ge(summed, g * BT + (u + AHEAD - RING + 2 * BT + 1))
                            weigh(g * BT + (u + AHEAD), u + AHEAD)
                            dve.wait_ge(summed, g * BT + (u + 2 * BT + 1))
                            dve.wait_ge(added, g * BT + (u + RING))
                            here = acc[:, bass.ds(tile[n], 1), 0:width]
                            dve.tensor_tensor(here, here, part[n % RING][:, 0:width].unsqueeze(1),
                                              ALU.add).then_inc(added, 1)

            @block.tensor
            def _(pe):
                pe.sem_inc(summed, 2 * BT)
                pe.sem_inc(added, RING)
                with pe.Fori(0, TILES // BT // 2) as i:
                    g = i * 2
                    for u in range(2 * BT):
                        pe.wait_ge(hot_ready, g * BT + (u + 1))
                        pe.wait_ge(gathered[u % BT], g * 16 + (u // BT + 1) * 16)
                        pe.wait_ge(added, g * BT + (u + 1))
                        pe.matmul(part[u % RING][:, 0:width], hot[:, u % RING, :], rows[:, u % BT, :],
                                  start=True, stop=True).then_inc(summed, 1)


def setup(nc, k, inp, w, blank):
    with Scope(nc, "set") as s:
        w0 = s.sb("w0", [P, F // P, F])
        att = s.sb("att", [P, 3, F])
        w_edge = s.sb("w_edge", [P, 4, F])
        prod = s.sb("prod", [P, F // P, F])
        ea_sum, mean_ea = s.sb("ea_sum", [P, 4]), s.sb("mean_ea", [P, 4])
        tmp = s.sb("tmp", [P, HEADS, 4])
        p_ea = s.ps("p_ea", [P, 4])
        loaded, own, counted, summed = s.sem("loaded"), s.sem("own"), s.sem("counted"), s.sem("summed")
        with nc.Block() as block:
            @block.sync
            def _(sp):
                sp.dma_start(w0[:, :, :], inp["W0"].rearrange("(t p) n -> p t n", p=P)).then_inc(loaded, 16)
                for i, n in enumerate(("att_src", "att_dst", "att_edge")):
                    sp.dma_start(att[:, i, :], inp[n].partition_broadcast(P)).then_inc(loaded, 16)
                sp.dma_start(w_edge[:, :, :].rearrange("p a n -> p (a n)"),
                             inp["W_edge"].partition_broadcast(P)).then_inc(loaded, 16)
                sp.dma_start(w.records[:, :, :].rearrange("p c f -> p (c f)"), inp["edges"]).then_inc(loaded, 16)

            @block.tensor
            def _(pe):
                pe.wait_ge(counted, 1)
                pe.matmul(p_ea[:, :], k.ones[:, :], ea_sum[:, :], start=True, stop=True).then_inc(summed, 1)

            @block.vector
            def _(dve):
                c = Chain(dve, own)
                dve.memset(k.eps_ln[:, :], EPS_LN)
                dve.memset(k.eps_bn[:, :], EPS_BN)
                c.run(dve.memset(blank[:, :], 0.0))
                dve.memset(blank[:, :].rearrange("p (t f) -> p t f", f=REC)[:, :, R_LOCAL], -1.0)
                dve.wait_ge(loaded, 96)
                dve.tensor_reduce(ea_sum[:, :], w.records[:, :, R_EA:R_EA + 4].rearrange("p c f -> p f c"),
                                  AX.X, ALU.add).then_inc(counted, 1)
                for i in range(2):
                    c.run(dve.tensor_tensor(prod[:, :, :], w0[:, :, :], att[:, i, :].unsqueeze(1).broadcast_to(
                        [P, F // P, F]), ALU.mult))
                    c.run(dve.tensor_reduce(
                        w.w_ext[:, :, i * HEADS:(i + 1) * HEADS],
                        prod[:, :, :].rearrange("p t (h c) -> p t h c", h=HEADS), AX.X, ALU.add))
                c.run(dve.tensor_tensor(prod[:, :, :], w_edge[:, :, :], att[:, 2, :].unsqueeze(1).broadcast_to(
                    [P, 4, F]), ALU.mult))
                c.run(dve.tensor_reduce(w.v_edge[:, :, :], prod[:, :, :].rearrange(
                    "p a (h c) -> p a h c", h=HEADS), AX.X, ALU.add))
                dve.wait_ge(summed, 1)
                c.run(dve.tensor_scalar(mean_ea[:, :], p_ea[:, :], 1.0 / N_EDGES, None, ALU.mult))
                c.run(dve.tensor_tensor(tmp[:, :, :], w.v_edge[:, :, :].rearrange("p a h -> p h a"),
                                        mean_ea[:, :].unsqueeze(1).broadcast_to([P, HEADS, 4]), ALU.mult))
                c.run(dve.tensor_reduce(w.mean_logit[:, :], tmp[:, :, :], AX.X, ALU.add))


def node_pass(nc, k, s, kt, constants, weights, banks, loads, stores, prepare, n_prepare, finish,
              n_finish, act_steps):
    s.a_t = s.sb("a_t", [P, 2, kt * P])
    p_t = [s.ps(f"p_t{i}", [P, kt * P]) for i in range(2)]
    constant = s.sem("constant")
    loaded = [s.sem(f"loaded{q}") for q in range(4)]
    stored, saved = s.sem("stored"), s.sem("saved")
    prepared, turned, copied, multiplied = (s.sem(n) for n in ("prepared", "turned", "copied", "multiplied"))
    finished, own_p, own_f = s.sem("finished"), s.sem("own_p"), s.sem("own_f")
    asked, answered = s.sem("asked"), s.sem("answered")
    n_loads, n_stores = len(loads(0, 0)), len(stores(0, 0))
    n_steps = len(act_steps)

    with nc.Block() as block:
        @block.sync
        def _(sp):
            for to, of in constants:
                sp.dma_start(to, of).then_inc(constant, 16)

            def load(t, q):
                sp.wait_ge(finished, t + 1)
                for to, of in loads(t, q):
                    sp.dma_start(to, of).then_inc(loaded[q], 16)

            if n_loads:
                with sp.Fori(0, (NT - 1) // 4) as i:
                    t = i * 4
                    for q in range(4):
                        load(t + q, q)
                load(NT - 1, 0)

        @block.vector
        def _(dve):
            dve.wait_ge(constant, 16 * len(constants))

            def first(t, q):
                if n_loads:
                    dve.wait_ge(loaded[q], uses4(t, q, 16 * n_loads))
                if prepare is None:
                    dve.sem_inc(prepared, 1)
                    return
                dve.wait_ge(turned, t + 1)
                c = Chain(dve, own_p, t * n_prepare)
                prepare(dve, c, t, q).then_inc(prepared, 1)
                assert c.n == n_prepare

            def second(t, q):
                dve.wait_ge(multiplied, t + 3)
                dve.wait_ge(saved, t + 1)

                def through_act(i, instruction):
                    instruction.then_inc(asked, 1)
                    dve.wait_ge(answered, t * n_steps + (i + 1))

                c = Chain(dve, own_f, t * n_finish)
                finish(dve, c, through_act, t, q).then_inc(finished, 1)
                assert c.n == n_finish

            tiles_ahead(dve, first, second)

        @block.tensor
        def _(pe):
            pe.sem_inc(turned, 2)
            pe.sem_inc(copied, 2)
            pe.sem_inc(multiplied, 2)
            pe.sem_inc(finished, 4)
            pe.wait_ge(constant, 16 * len(constants))

            def first(t, q):
                pe.wait_ge(prepared, t + 1)
                pe.wait_ge(copied, t + 1)
                for i in range(kt):
                    last = pe.transpose(p_t[q % 2][:, i * P:(i + 1) * P], s.a[:, q % s.a_slots, i * P:(i + 1) * P],
                                        k.ident[:, :])
                last.then_inc(turned, 1)

            def second(t, q):
                pe.wait_ge(copied, t + 3)
                pe.wait_ge(finished, t + 3)
                for bank, n, weight in weights:
                    for i in range(kt):
                        last = pe.matmul(banks[q % 2][:, bank:bank + n], s.a_t[:, q % 2, i * P:(i + 1) * P],
                                         weight[:, i, :], start=(i == 0), stop=(i == kt - 1))
                last.then_inc(multiplied, 1)

            tiles_ahead(pe, first, second)

        @block.scalar
        def _(act):
            def first(t, q):
                act.wait_ge(turned, t + 3)
                act.wait_ge(multiplied, t + 1)
                act.copy(s.a_t[:, q % 2, :], p_t[q % 2][:, :]).then_inc(copied, 1)

            def second(t, q):
                for i, step in enumerate(act_steps):
                    act.wait_ge(asked, t * n_steps + (i + 1))
                    step(act, t, q).then_inc(answered, 1)

            tiles_ahead(act, first, second)

        @block.gpsimd
        def _(pool):
            def store(t, q):
                pool.wait_ge(finished, t + 5)
                for to, of in stores(t, q):
                    pool.dma_start(to, of).then_inc(stored, 16)
                pool.wait_ge(stored, (t + 1) * (16 * n_stores))
                pool.sem_inc(saved, 1)

            pool.sem_inc(saved, 2)
            tiles_ahead(pool, nothing, store)


class Norm:
    CHAINED = 3

    def __init__(self, k, s):
        self.k = k
        self.st, self.mv = s.sb("ln_st", [P, 6]), s.sb("ln_mv", [P, 2])
        self.passed = s.sem("ln_passed")
        self.std, self.rstd = s.sb("ln_std", [P, 1]), s.sb("ln_rstd", [P, 1])

    def act_step(self, act, t, q):
        return act.activation(self.std[:, :], self.mv[:, 1:2], ACT.Sqrt, bias=self.k.eps_ln[:, :])

    def apply(self, dve, c, through_act, i, y, out):
        c.run(dve.bn_stats(self.st[:, :], y))
        dve.sem_inc(self.passed, 1)
        through_act(i, dve.bn_aggr(self.mv[:, :], self.st[:, :]))
        c.run(dve.reciprocal(self.rstd[:, :], self.std[:, :]))
        return dve.tensor_scalar(out, y, self.mv[:, 0:1], self.rstd[:, :], ALU.subtract, ALU.mult)


def rows_of(table, t):
    return table[bass.ds(t * P, P), :]


def gat_projection(nc, k, w, inp, x0, h_table, src_table):
    with Scope(nc, "n0") as s:
        s.a, s.a_slots = s.sb("a", [P, 4, F]), 4
        w0 = s.sb("w0", [P, F // P, F])
        h = s.sb("h", [P, 2, F])
        banks = [s.ps(f"bank{i}", [P, 2 * F]) for i in range(2)]

        def finish(dve, c, through_act, t, q):
            dve.tensor_copy(col(w.node_logit, t * 2 * HEADS, 2 * HEADS), banks[q % 2][:, F:F + 2 * HEADS])
            return dve.tensor_copy(h[:, q % 2, :], banks[q % 2][:, 0:F])

        node_pass(nc, k, s, F // P,
                  [(w0[:, :, :], inp["W0"].rearrange("(t p) n -> p t n", p=P))],
                  [(0, F, w0), (F, 2 * HEADS, w.w_ext)], banks,
                  lambda t, q: [(s.a[:, q, :], rows_of(x0, t))],
                  lambda t, q: [(rows_of(h_table, t), h[:, q % 2, :]),
                                (rows_of(src_table, t), col(w.node_logit, t * 2 * HEADS, HEADS))],
                  None, 0, finish, 0, [])


def edge_logits(nc, k, w, rec):
    with Scope(nc, "lg") as s:
        pad = s.sb("pad", [P, TILES_PAD])
        both = s.sb("both", [P, NT, HEADS])
        own = s.sem("own")
        with nc.Block() as block:
            @block.vector
            def _(dve):
                c = Chain(dve, own)
                c.run(dve.tensor_scalar(pad[:, :], rec[:, :, R_LOCAL], 0.0, MASKED, ALU.is_lt, ALU.mult))
                for a in range(4):
                    for h in range(HEADS):
                        before = pad[:, :] if a == 0 else w.attr_logit[:, :, h]
                        last = dve.scalar_tensor_tensor(
                            w.attr_logit[:, :, h], rec[:, :, R_EA + a], w.v_edge[:, a, h:h + 1], before,
                            ALU.mult, ALU.add)
                    c.run(last)
                node = w.node_logit[:, :].rearrange("p (t h) -> p t h", h=2 * HEADS)
                c.run(dve.tensor_tensor(both[:, :, :], node[:, :, 0:HEADS], node[:, :, HEADS:2 * HEADS], ALU.add))
                c.run(dve.tensor_tensor(both[:, :, :], both[:, :, :], w.mean_logit[:, :].unsqueeze(1).broadcast_to(
                    [P, NT, HEADS]), ALU.add))
                dve.tensor_copy(w.dst_own[:, :, 0:HEADS], node[:, :, HEADS:2 * HEADS])
                dve.scalar_tensor_tensor(w.dst_own[:, :, HEADS:2 * HEADS], both[:, :, :], NEG_SLOPE, both[:, :, :],
                                         ALU.mult, ALU.max)
                c.run(dve.memset(w.above[:, :, :], 0.0))


def attention_maxima(nc, k, w, rec, buckets, src_table):
    DR = 4
    with Scope(nc, "mx") as s:
        index = s.sb("index", [P, 2, BT], I32)
        src = s.sb("src", [P, 2, BT, HEADS])
        hot = s.sb("hot", [P, 2, BT, P])
        hot_t = s.sb("hot_t", [P, BT, P])
        over = s.sb("over", [P, 2, BT, HEADS])
        raw = s.sb("raw", [P, BT, HEADS])
        diag = s.sb("diag", [P, DR, HEADS, P])
        top = s.sb("top", [P, BT, HEADS])
        p_hot = s.ps("p_hot", [P, BT * P])
        p_node = s.ps("p_node", [P, BT, 2 * HEADS])
        p_top = [s.ps(f"p_top{i}", [P, HEADS, P]) for i in range(DR)]
        indexed, granted, hot_ready, turned, copied = (
            s.sem(n) for n in ("indexed", "granted", "hot_ready", "turned", "copied"))
        gathered = [s.sem(f"gathered{h}") for h in range(2)]
        by_node, logits, own, diag_dve, diag_act = (
            s.sem(n) for n in ("by_node", "logits", "own", "diag_dve", "diag_act"))
        masked, reduced, raised = s.sem("masked"), s.sem("reduced"), s.sem("raised")
        other = rec[:, :, R_OTHER].bitcast(I32)
        with nc.Block() as block:
            @block.scalar
            def _(act):
                def first(g, h):
                    act.wait_ge(logits, g + 1)
                    act.copy(index[:, h, :], col(other, g * BT, BT)).then_inc(indexed, 1)
                    act.wait_ge(by_node, g)
                    for i in range(2):
                        act.wait_ge(turned, g * 2 + (i + 1))
                        act.copy(hot_t[:, 4 * i:4 * i + 4, :].rearrange("p n e -> p (n e)"),
                                 p_hot[:, 4 * i * P:4 * (i + 1) * P]).then_inc(copied, 1)

                def second(g, h):
                    act.wait_ge(logits, g + 3)
                    for n in range(BT):
                        act.wait_ge(masked, g * BT + (n + 1 + 2 * BT - DR))
                        for hd in (2, 3):
                            last = act.activation(diag[:, n % DR, hd, :], k.ident[:, :], ACT.Copy,
                                                  scale=over[:, h, n, hd:hd + 1])
                        last.then_inc(diag_act, 1)

                batches_ahead(act, first, second, nothing)

            @block.gpsimd
            def _(pool):
                def gather(g, h):
                    pool.wait_ge(indexed, g + 1)
                    pool.sem_inc(granted, 1)
                    for n in range(BT):
                        pool.indirect_dma_start(
                            src[:, h, n, :], None, src_table,
                            bass.IndirectOffsetOnAxis(index[:, h, n:n + 1], 0)).then_inc(gathered[h], 16)

                batches_ahead(pool, gather, nothing, nothing)
                pool.wait_ge(gathered[0], (TILES // BT + 2) // 2 * BT * 16)

            @block.tensor
            def _(pe):
                pe.sem_inc(logits, 2)
                pe.sem_inc(masked, 2 * BT)
                pe.sem_inc(reduced, DR)
                pe.sem_inc(raised, 1)

                def first(g, h):
                    tile = bucket_registers(nc, mybir.EngineType.PE, buckets, g * BT)
                    pe.wait_ge(hot_ready, g + 1)
                    pe.wait_ge(copied, g * 2)
                    for n in range(BT):
                        last = pe.transpose(p_hot[:, n * P:(n + 1) * P], hot[:, h, n, :], k.ident[:, :])
                        if n % 4 == 3:
                            last.then_inc(turned, 1)
                    pe.wait_ge(copied, g * 2 + 2)
                    pe.wait_ge(logits, g + 2)
                    for n in range(BT):
                        last = pe.matmul(p_node[:, n, :], hot_t[:, n, :],
                                         w.dst_own[:, bass.ds(tile[n], 1), :], start=True, stop=True)
                    last.then_inc(by_node, 1)

                def second(g, h):
                    for n in range(BT):
                        pe.wait_ge(diag_dve, g * BT + (n + 1))
                        pe.wait_ge(diag_act, g * BT + (n + 1))
                        pe.wait_ge(reduced, g * BT + (n + 1))
                        pe.matmul(p_top[n % DR][:, :, :], hot[:, h, n, :], diag[:, n % DR, :, :],
                                  start=True, stop=True).then_inc(masked, 1)

                batches_ahead(pe, first, second, nothing)

            @block.vector
            def _(dve):
                def first(g, h):
                    dve.wait_ge(masked, g * BT + BT)
                    for n in range(BT):
                        last = dve.tensor_scalar(hot[:, h, n, :], k.columns[:, 0:P],
                                                 col(rec[:, :, R_LOCAL], g * BT + n), None, ALU.is_equal)
                    last.then_inc(hot_ready, 1)

                def third(g, h):
                    c = Chain(dve, own, g * 3)
                    dve.wait_ge(gathered[h], (g - h) * (BT * 8) + BT * 16)
                    dve.wait_ge(by_node, g + 1)
                    logit = w.logit[:, bass.ds(g * BT, BT), :]
                    c.run(dve.tensor_tensor(raw[:, :, :], src[:, h, :, :], p_node[:, :, 0:HEADS], ALU.add))
                    c.run(dve.tensor_tensor(raw[:, :, :], raw[:, :, :],
                                            w.attr_logit[:, bass.ds(g * BT, BT), :], ALU.add))
                    c.run(dve.scalar_tensor_tensor(logit, raw[:, :, :], NEG_SLOPE, raw[:, :, :], ALU.mult, ALU.max))
                    dve.tensor_tensor(over[:, h, :, :], logit, p_node[:, :, HEADS:2 * HEADS],
                                      ALU.subtract).then_inc(logits, 1)

                def second(g, h):
                    tile = bucket_registers(nc, mybir.EngineType.DVE, buckets, g * BT)
                    dve.wait_ge(logits, g + 3)

                    def spread(n):
                        dve.wait_ge(masked, g * BT + (n + 1 + 2 * BT - DR))
                        dve.tensor_tensor(
                            diag[:, n % DR, 0:2, :], k.ident[:, :].unsqueeze(1).broadcast_to([P, 2, P]),
                            over[:, h, n, 0:2].unsqueeze(2).broadcast_to([P, 2, P]), ALU.mult).then_inc(diag_dve, 1)

                    def raise_node(n):
                        dve.wait_ge(reduced, g * BT + (n + 1 + DR))
                        dve.wait_ge(raised, g * BT + (n + 1))
                        here = w.above[:, bass.ds(tile[n], 1), :]
                        dve.tensor_tensor(here, here, top[:, n, :].unsqueeze(1), ALU.max).then_inc(raised, 1)

                    spread(0)
                    spread(1)
                    for n in range(BT):
                        if n + 2 < BT:
                            spread(n + 2)
                        dve.wait_ge(masked, g * BT + (n + 1 + 2 * BT))
                        dve.tensor_reduce(top[:, n, :], p_top[n % DR][:, :, :], AX.X, ALU.max).then_inc(reduced, 1)
                        if n > 0:
                            raise_node(n - 1)
                    raise_node(BT - 1)

                batches_ahead(dve, first, second, third)


def self_loops(nc, k, w, h_table, acc):
    with Scope(nc, "sl") as s:
        h = s.sb("h", [P, 4, F])
        loaded = [s.sem(f"loaded{q}") for q in range(4)]
        own, under, exped, used = s.sem("own"), s.sem("under"), s.sem("exped"), s.sem("used")
        with nc.Block() as block:
            @block.sync
            def _(sp):
                sp.sem_inc(used, 4)

                def load(t, q):
                    sp.wait_ge(used, t + 1)
                    sp.dma_start(h[:, q, :], rows_of(h_table, t)).then_inc(loaded[q], 16)

                tiles_ahead(sp, nothing, load)

            @block.scalar
            def _(act):
                act.wait_ge(under, 1)
                act.activation(w.self_weight[:, :, :], w.above[:, :, :], ACT.Exp, scale=-1.0).then_inc(exped, 1)

            @block.vector
            def _(dve):
                c = Chain(dve, own)
                dve.tensor_tensor(w.maximum[:, :, :], w.above[:, :, :], w.dst_own[:, :, HEADS:2 * HEADS],
                                  ALU.add).then_inc(under, 1)
                dve.memset(acc[:, :, F:ACCW], 0.0).then_inc(own, 1)
                dve.wait_ge(exped, 1)
                dve.wait_ge(own, 1)
                dve.tensor_copy(acc[:, :, DEN:DEN + HEADS], w.self_weight[:, :, :])

                def scale(t, q):
                    dve.wait_ge(loaded[q], uses4(t, q, 16))
                    dve.tensor_tensor(
                        acc[:, bass.ds(t, 1), 0:F].rearrange("p o (h c) -> p (o h) c", h=HEADS),
                        h[:, q, :].rearrange("p (h c) -> p h c", h=HEADS),
                        w.self_weight[:, bass.ds(t, 1), :].rearrange("p o h -> p (o h)").unsqueeze(2).broadcast_to(
                            [P, HEADS, C]), ALU.mult).then_inc(used, 1)

                tiles_ahead(dve, nothing, scale)


def attention_sums(nc, k, w, rec, buckets, h_table, acc):
    RING = 2
    with Scope(nc, "at") as s:
        index = s.sb("index", [P, 2, BT], I32)
        rows = s.sb("rows", [P, BT, F])
        hot = s.sb("hot", [P, 2, BT, P])
        hot_t = s.sb("hot_t", [P, BT, P])
        below = s.sb("below", [P, BT, HEADS])
        att = s.sb("att", [P, 2, BT, HEADS + 1])
        p_hot = s.ps("p_hot", [P, BT * P])
        p_max = s.ps("p_max", [P, BT, HEADS])
        part = [s.ps(f"part{i}", [P, 2 * F]) for i in range(RING)]
        gathered = [s.sem(f"gathered{n}") for n in range(BT)]
        indexed, granted, hot_ready, turned, copied = (
            s.sem(n) for n in ("indexed", "granted", "hot_ready", "turned", "copied"))
        by_node, shifted, exped = s.sem("by_node"), s.sem("shifted"), s.sem("exped")
        scaled_dve, scaled_act, summed, added = (
            s.sem(n) for n in ("scaled_dve", "scaled_act", "summed", "added"))
        other = rec[:, :, R_OTHER].bitcast(I32)
        with nc.Block() as block:
            @block.scalar
            def _(act):
                def first(g, h):
                    act.wait_ge(summed, g * BT)
                    act.copy(index[:, h, :], col(other, g * BT, BT)).then_inc(indexed, 1)
                    act.wait_ge(by_node, g)
                    for i in range(2):
                        act.wait_ge(turned, g * 2 + (i + 1))
                        act.copy(hot_t[:, 4 * i:4 * i + 4, :].rearrange("p n e -> p (n e)"),
                                 p_hot[:, 4 * i * P:4 * (i + 1) * P]).then_inc(copied, 1)

                def second(g, h):
                    act.wait_ge(exped, g + 1)
                    for n in range(BT):
                        act.wait_ge(gathered[n], g * 16 + 16)
                        for hd in (2, 3):
                            part_row = rows[:, n, hd * C:(hd + 1) * C]
                            last = act.activation(part_row, part_row, ACT.Copy, scale=att[:, h, n, hd:hd + 1])
                        last.then_inc(scaled_act, 1)

                def third(g, h):
                    act.wait_ge(shifted, g + 1)
                    act.activation(att[:, h, :, 0:HEADS], below[:, :, :], ACT.Exp).then_inc(exped, 1)

                batches_ahead(act, first, second, third)

            @block.gpsimd
            def _(pool):
                def gather(g, h):
                    pool.wait_ge(indexed, g + 1)
                    for n in range(BT):
                        pool.wait_ge(summed, g * BT + (n + 1))
                        pool.sem_inc(granted, 1)
                        pool.indirect_dma_start(
                            rows[:, n, :], None, h_table,
                            bass.IndirectOffsetOnAxis(index[:, h, n:n + 1], 0)).then_inc(gathered[n], 16)

                with pool.Fori(0, TILES // BT // 2) as i:
                    g = i * 2
                    gather(g, 0)
                    gather(g + 1, 1)

            @block.tensor
            def _(pe):
                pe.sem_inc(summed, BT)
                pe.sem_inc(added, RING)

                def first(g, h):
                    tile = bucket_registers(nc, mybir.EngineType.PE, buckets, g * BT)
                    pe.wait_ge(hot_ready, g + 1)
                    pe.wait_ge(copied, g * 2)
                    for n in range(BT):
                        last = pe.transpose(p_hot[:, n * P:(n + 1) * P], hot[:, h, n, :], k.ident[:, :])
                        if n % 4 == 3:
                            last.then_inc(turned, 1)
                    pe.wait_ge(copied, g * 2 + 2)
                    pe.wait_ge(shifted, g)
                    for n in range(BT):
                        last = pe.matmul(p_max[:, n, :], hot_t[:, n, :],
                                         w.maximum[:, bass.ds(tile[n], 1), :], start=True, stop=True)
                    last.then_inc(by_node, 1)

                def second(g, h):
                    for n in range(BT):
                        pe.wait_ge(scaled_dve, g * BT + (n + 1))
                        pe.wait_ge(scaled_act, g * BT + (n + 1))
                        pe.wait_ge(added, g * BT + (n + 1))
                        pe.matmul(part[n % RING][:, 0:F], hot[:, h, n, :], rows[:, n, :], start=True, stop=True)
                        pe.matmul(part[n % RING][:, F:F + HEADS + 1], hot[:, h, n, :], att[:, h, n, :],
                                  start=True, stop=True).then_inc(summed, 1)

                batches_ahead(pe, first, second, nothing)

            @block.vector
            def _(dve):
                def first(g, h):
                    dve.wait_ge(summed, g * BT)
                    for n in range(BT):
                        last = dve.tensor_scalar(hot[:, h, n, :], k.columns[:, 0:P],
                                                 col(rec[:, :, R_LOCAL], g * BT + n), None, ALU.is_equal)
                    last.then_inc(hot_ready, 1)

                def third(g, h):
                    dve.wait_ge(by_node, g + 1)
                    dve.wait_ge(exped, g)
                    dve.tensor_copy(att[:, h, :, HEADS], col(rec[:, :, R_W], g * BT, BT))
                    dve.tensor_tensor(below[:, :, :], w.logit[:, bass.ds(g * BT, BT), :], p_max[:, :, :],
                                      ALU.subtract).then_inc(shifted, 1)

                def second(g, h):
                    tile = bucket_registers(nc, mybir.EngineType.DVE, buckets, g * BT)
                    dve.wait_ge(exped, g + 1)

                    def scale(n):
                        dve.wait_ge(gathered[n], g * 16 + 16)
                        heads = rows[:, n, 0:2 * C].rearrange("p (h c) -> p h c", h=2)
                        dve.tensor_tensor(heads, heads, att[:, h, n, 0:2].unsqueeze(2).broadcast_to([P, 2, C]),
                                          ALU.mult).then_inc(scaled_dve, 1)

                    scale(0)
                    for n in range(BT):
                        if n + 1 < BT:
                            scale(n + 1)
                        dve.wait_ge(summed, g * BT + (n + 1 + BT))
                        dve.wait_ge(added, g * BT + (n + RING))
                        here = acc[:, bass.ds(tile[n], 1), 0:F + HEADS + 1]
                        dve.tensor_tensor(here, here, part[n % RING][:, 0:F + HEADS + 1].unsqueeze(1),
                                          ALU.add).then_inc(added, 1)

                batches_ahead(dve, first, second, third)


def batch_norm(nc, k, w, inp, acc):
    with Scope(nc, "bn") as s:
        bias, gamma = s.sb("bias", [P, F]), s.sb("gamma", [P, F])
        rden, deg, has = s.sb("rden", [P, NT, HEADS]), s.sb("deg", [P, NT]), s.sb("has", [P, NT])
        mean, std = s.sb("mean", [P, F]), s.sb("std", [P, F])
        square = s.sb("square", [P, 2, F])
        p_sum, p_var = s.ps("p_sum", [P, F]), s.ps("p_var", [P, F])
        loaded, own, ready, summed, centred = (s.sem(n) for n in ("loaded", "own", "ready", "summed", "centred"))
        squared, added, rooted, asked = s.sem("squared"), s.sem("added"), s.sem("rooted"), s.sem("asked")
        GROUP = 5
        with nc.Block() as block:
            @block.sync
            def _(sp):
                sp.dma_start(bias[:, :], inp["bias"].partition_broadcast(P)).then_inc(loaded, 16)
                sp.dma_start(gamma[:, :], inp["gamma"].partition_broadcast(P)).then_inc(loaded, 16)

            @block.tensor
            def _(pe):
                for t in range(NT):
                    pe.wait_ge(ready, t // GROUP + 1)
                    last = pe.matmul(p_sum[:, :], (k.ones if t < NT - 1 else k.last_rows)[:, :],
                                     acc[:, t, 0:F], start=(t == 0), stop=(t == NT - 1))
                last.then_inc(summed, 1)
                for t in range(NT):
                    pe.wait_ge(squared, t + 1)
                    pe.matmul(p_var[:, :], (k.ones if t < NT - 1 else k.last_rows)[:, :],
                              square[:, t % 2, :], start=(t == 0), stop=(t == NT - 1)).then_inc(added, 1)

            @block.scalar
            def _(act):
                act.wait_ge(asked, 1)
                act.activation(w.dinv[:, :], deg[:, :], ACT.Sqrt).then_inc(rooted, 1)
                for t in range(NT):
                    act.wait_ge(centred, t // GROUP + 1)
                    if t >= 2:
                        act.wait_ge(added, t - 1)
                    act.activation(square[:, t % 2, :], acc[:, t, 0:F], ACT.Square).then_inc(squared, 1)
                act.wait_ge(added, NT)
                act.activation(std[:, :], p_var[:, :], ACT.Sqrt, bias=k.eps_bn[:, :],
                               scale=1.0 / N_NODES).then_inc(rooted, 1)

            @block.vector
            def _(dve):
                c = Chain(dve, own)
                c.run(dve.tensor_scalar(rden[:, :, :], acc[:, :, DEN:DEN + HEADS], EPS_DEN, None, ALU.add))
                c.run(dve.reciprocal(rden[:, :, :], rden[:, :, :]))
                dve.wait_ge(loaded, 32)
                for g in range(0, NT, GROUP):
                    here = acc[:, g:g + GROUP, 0:F]
                    by_head = here.rearrange("p t (h c) -> p t h c", h=HEADS)
                    c.run(dve.tensor_tensor(by_head, by_head, rden[:, g:g + GROUP, :].unsqueeze(3).broadcast_to(
                        [P, GROUP, HEADS, C]), ALU.mult))
                    dve.tensor_tensor(here, here, bias[:, :].unsqueeze(1).broadcast_to([P, GROUP, F]),
                                      ALU.add).then_inc(ready, 1)
                c.run(dve.tensor_scalar(w.rdeg[:, :], acc[:, :, DEG], 1.0, None, ALU.max))
                c.run(dve.reciprocal(w.rdeg[:, :], w.rdeg[:, :]))
                c.run(dve.tensor_scalar(deg[:, :], acc[:, :, DEG], 1.0, None, ALU.add))
                dve.tensor_scalar(has[:, :], deg[:, :], 0.0, None, ALU.is_gt)
                dve.tensor_scalar(deg[:, :], deg[:, :], TINY, None, ALU.max).then_inc(asked, 1)
                dve.wait_ge(rooted, 1)
                c.run(dve.reciprocal(w.dinv[:, :], w.dinv[:, :]))
                c.run(dve.tensor_tensor(w.dinv[:, :], w.dinv[:, :], has[:, :], ALU.mult))
                dve.wait_ge(ready, NT // GROUP)
                dve.wait_ge(summed, 1)
                c.run(dve.tensor_scalar(mean[:, :], p_sum[:, :], 1.0 / N_NODES, None, ALU.mult))
                for g in range(0, NT, GROUP):
                    here = acc[:, g:g + GROUP, 0:F]
                    dve.tensor_tensor(here, here, mean[:, :].unsqueeze(1).broadcast_to([P, GROUP, F]),
                                      ALU.subtract).then_inc(centred, 1)
                dve.wait_ge(rooted, 2)
                c.run(dve.reciprocal(std[:, :], std[:, :]))
                dve.tensor_tensor(w.bn_scale[:, :], std[:, :], gamma[:, :], ALU.mult)


def gat_output(nc, k, w, inp, x0, x1, scaled, acc):
    with Scope(nc, "n1") as s:
        beta = s.sb("beta", [P, F])
        x = s.sb("x", [P, 4, F])
        y = s.sb("y", [P, 2, F])
        out = s.sb("out", [P, 2, F])
        norm = Norm(k, s)
        constant = s.sem("constant")
        loaded = [s.sem(f"loaded{q}") for q in range(4)]
        stored, saved = s.sem("stored"), s.sem("saved")
        own, asked, answered, finished = (s.sem(n) for n in ("own", "asked", "answered", "finished"))
        CHAINED = 5
        with nc.Block() as block:
            @block.sync
            def _(sp):
                sp.dma_start(beta[:, :], inp["beta"].partition_broadcast(P)).then_inc(constant, 16)
                sp.sem_inc(finished, 4)

                def load(t, q):
                    sp.wait_ge(finished, t + 1)
                    sp.dma_start(x[:, q, :], rows_of(x0, t)).then_inc(loaded[q], 16)

                tiles_ahead(sp, nothing, load)

            @block.vector
            def _(dve):
                dve.wait_ge(constant, 16)

                def tile(t, q):
                    c = Chain(dve, own, t * CHAINED)
                    here = acc[:, bass.ds(t, 1), 0:F].rearrange("p o f -> p (o f)")
                    dve.wait_ge(loaded[q], uses4(t, q, 16))
                    dve.tensor_tensor(x[:, q, :], x[:, q, :], beta[:, :], ALU.add)
                    c.run(dve.tensor_tensor(y[:, q % 2, :], here, w.bn_scale[:, :], ALU.mult))
                    c.run(dve.tensor_tensor(y[:, q % 2, :], y[:, q % 2, :], x[:, q, :], ALU.add))

                    def through_act(i, instruction):
                        instruction.then_inc(asked, 1)
                        dve.wait_ge(answered, t + 1)

                    dve.wait_ge(saved, t + 1)
                    c.run(norm.apply(dve, c, through_act, 0, y[:, q % 2, :], out[:, q % 2, :]))
                    dve.tensor_scalar(here, out[:, q % 2, :], col(w.dinv, t), None, ALU.mult).then_inc(finished, 1)
                    assert c.n == CHAINED

                tiles_ahead(dve, nothing, tile)

            @block.scalar
            def _(act):
                def root(t, q):
                    act.wait_ge(asked, t + 1)
                    norm.act_step(act, t, q).then_inc(answered, 1)

                tiles_ahead(act, nothing, root)

            @block.gpsimd
            def _(pool):
                def store(t, q):
                    pool.wait_ge(finished, t + 5)
                    pool.dma_start(rows_of(x1, t), out[:, q % 2, :]).then_inc(stored, 16)
                    pool.dma_start(rows_of(scaled, t), acc[:, bass.ds(t, 1), 0:F]).then_inc(stored, 16)
                    pool.wait_ge(stored, (t + 1) * 32)
                    pool.sem_inc(saved, 1)

                pool.sem_inc(saved, 2)
                tiles_ahead(pool, nothing, store)


def gcn_hidden(nc, k, w, inp, scaled_hid, acc):
    with Scope(nc, "n2") as s:
        s.a, s.a_slots = s.sb("a", [P, 2, F]), 2
        w1, b1 = s.sb("w1", [P, F // P, HID]), s.sb("b1", [P, HID])
        hid = s.sb("hid", [P, 2, HID])
        banks = [s.ps(f"bank{i}", [P, HID]) for i in range(2)]

        def prepare(dve, c, t, q):
            return dve.tensor_scalar(s.a[:, q % 2, :].unsqueeze(1), acc[:, bass.ds(t, 1), 0:F],
                                     col(w.dinv, t), None, ALU.mult)

        def finish(dve, c, through_act, t, q):
            c.run(dve.tensor_tensor(hid[:, q % 2, :], banks[q % 2][:, :], b1[:, :], ALU.add))
            return dve.tensor_scalar(acc[:, bass.ds(t, 1), 0:HID], hid[:, q % 2, :].unsqueeze(1), 0.0,
                                     col(w.dinv, t), ALU.max, ALU.mult)

        node_pass(nc, k, s, F // P,
                  [(w1[:, :, :], inp["W1"].rearrange("(t p) n -> p t n", p=P)),
                   (b1[:, :], inp["b1"].partition_broadcast(P))],
                  [(0, HID, w1)], banks, lambda t, q: [],
                  lambda t, q: [(rows_of(scaled_hid, t), acc[:, bass.ds(t, 1), 0:HID])],
                  prepare, 0, finish, 1, [])


def gcn_output(nc, k, w, inp, x1, x2, acc):
    with Scope(nc, "n3") as s:
        s.a, s.a_slots = s.sb("a", [P, 2, HID]), 2
        w2, b2 = s.sb("w2", [P, HID // P, F]), s.sb("b2", [P, F])
        x = s.sb("x", [P, 4, F])
        y, out = s.sb("y", [P, 2, F]), s.sb("out", [P, 2, F])
        st, mv, ms = s.sb("st", [P, 6]), s.sb("mv", [P, 2]), s.sb("ms", [P, 1])
        length, rlen = s.sb("length", [P, 1]), s.sb("rlen", [P, 1])
        norm = Norm(k, s)
        banks = [s.ps(f"bank{i}", [P, F]) for i in range(2)]

        def prepare(dve, c, t, q):
            return dve.tensor_scalar(s.a[:, q % 2, :].unsqueeze(1), acc[:, bass.ds(t, 1), 0:HID],
                                     col(w.dinv, t), None, ALU.mult)

        def finish(dve, c, through_act, t, q):
            here = y[:, q % 2, :]
            c.run(dve.tensor_tensor(here, banks[q % 2][:, :], b2[:, :], ALU.add))
            c.run(dve.bn_stats(st[:, :], here))
            dve.sem_inc(norm.passed, 1)
            c.run(dve.bn_aggr(mv[:, :], st[:, :]))
            through_act(0, dve.scalar_tensor_tensor(ms[:, :], mv[:, 0:1], mv[:, 0:1], mv[:, 1:2], ALU.mult, ALU.add))
            c.run(dve.tensor_scalar(length[:, :], length[:, :], EPS_NORM, None, ALU.max))
            c.run(dve.reciprocal(rlen[:, :], length[:, :]))
            c.run(dve.scalar_tensor_tensor(here, here, rlen[:, :], x[:, q, :], ALU.mult, ALU.add))
            return norm.apply(dve, c, through_act, 1, here, out[:, q % 2, :])

        def root(act, t, q):
            return act.activation(length[:, :], ms[:, :], ACT.Sqrt, scale=float(F))

        node_pass(nc, k, s, HID // P,
                  [(w2[:, :, :], inp["W2"].rearrange("(t p) n -> p t n", p=P)),
                   (b2[:, :], inp["b2"].partition_broadcast(P))],
                  [(0, F, w2)], banks, lambda t, q: [(x[:, q, :], rows_of(x1, t))],
                  lambda t, q: [(rows_of(x2, t), out[:, q % 2, :])],
                  prepare, 0, finish, 8, [root, norm.act_step])


def sage_output(nc, k, w, inp, x2, x3, acc):
    with Scope(nc, "n4") as s:
        s.a, s.a_slots = s.sb("a", [P, 2, 2 * F]), 2
        wt = s.sb("wt", [P, 2 * F // P, F])
        b = s.sb("b", [P, 2, F])
        x = s.sb("x", [P, 4, F])
        y, out = s.sb("y", [P, 2, F]), s.sb("out", [P, 2, F])
        norm = Norm(k, s)
        banks = [s.ps(f"bank{i}", [P, F]) for i in range(2)]

        def prepare(dve, c, t, q):
            dve.tensor_copy(s.a[:, q % 2, 0:F], x[:, q, :])
            return dve.tensor_scalar(s.a[:, q % 2, F:2 * F].unsqueeze(1), acc[:, bass.ds(t, 1), 0:F],
                                     col(w.rdeg, t), None, ALU.mult)

        def finish(dve, c, through_act, t, q):
            here = y[:, q % 2, :]
            c.run(dve.tensor_tensor(here, banks[q % 2][:, :], b[:, 0, :], ALU.add))
            c.run(dve.tensor_tensor(here, here, b[:, 1, :], ALU.add))
            c.run(dve.tensor_tensor(here, here, x[:, q, :], ALU.add))
            return norm.apply(dve, c, through_act, 0, here, out[:, q % 2, :])

        node_pass(nc, k, s, 2 * F // P,
                  [(wt[:, 0:F // P, :], inp["W_self_t"].rearrange("(t p) n -> p t n", p=P)),
                   (wt[:, F // P:2 * F // P, :], inp["W_neigh_t"].rearrange("(t p) n -> p t n", p=P)),
                   (b[:, 0, :], inp["b_self"].partition_broadcast(P)),
                   (b[:, 1, :], inp["b_neigh"].partition_broadcast(P))],
                  [(0, F, wt)], banks, lambda t, q: [(x[:, q, :], rows_of(x2, t))],
                  lambda t, q: [(rows_of(x3, t), out[:, q % 2, :])],
                  prepare, 0, finish, 5, [norm.act_step])


def conv_output(nc, k, w, inp, x3, result, acc):
    with Scope(nc, "n5") as s:
        s.a, s.a_slots = s.sb("a", [P, 2, F]), 2
        w3, b3 = s.sb("w3", [P, F // P, F]), s.sb("b3", [P, F])
        x = s.sb("x", [P, 4, F])
        y, out = s.sb("y", [P, 2, F]), s.sb("out", [P, 2, F])
        norm = Norm(k, s)
        banks = [s.ps(f"bank{i}", [P, F]) for i in range(2)]

        def prepare(dve, c, t, q):
            return dve.tensor_copy(s.a[:, q % 2, :].unsqueeze(1), acc[:, bass.ds(t, 1), 0:F])

        def finish(dve, c, through_act, t, q):
            here = y[:, q % 2, :]
            c.run(dve.tensor_tensor(here, banks[q % 2][:, :], b3[:, :], ALU.add))
            c.run(dve.tensor_tensor(here, here, x[:, q, :], ALU.add))
            return norm.apply(dve, c, through_act, 0, here, out[:, q % 2, :])

        def store(t, q):
            rows = P if not isinstance(t, int) or t < NT - 1 else LAST_ROWS
            return [(result[bass.ds(t * P, rows), :], out[0:rows, q % 2, :])]

        node_pass(nc, k, s, F // P,
                  [(w3[:, :, :], inp["W3"].rearrange("(t p) n -> p t n", p=P)),
                   (b3[:, :], inp["b3"].partition_broadcast(P))],
                  [(0, F, w3)], banks, lambda t, q: [(x[:, q, :], rows_of(x3, t))], store,
                  prepare, 0, finish, 4, [norm.act_step])


def build(nc, inp, result):
    class Held:
        pass

    def dram(name, shape):
        return nc.dram_tensor(name, shape, FP).ap()

    by_dst, by_src = dram("edges_by_dst", [P * TC, REC]), dram("edges_by_src", [P * TC, REC])
    h_table, src_table = dram("h_table", [NODES_PAD, F]), dram("src_table", [NODES_PAD, HEADS])
    scaled, scaled_hid = dram("x1_scaled", [NODES_PAD, F]), dram("hidden_scaled", [NODES_PAD, HID])
    x0 = inp["x"]
    x1, x2, x3 = (dram(n, [NODES_PAD, F]) for n in ("x1", "x2", "x3"))

    with Scope(nc, "k") as held:
        k, w = Held(), Held()
        k.ident, k.before = held.sb("ident", [P, P]), held.sb("before", [P, P])
        k.ones, k.last_rows = held.sb("ones", [P, P]), held.sb("last_rows", [P, P])
        k.columns, k.pad_slot = held.sb("columns", [P, TILES_PAD]), held.sb("pad_slot", [P, EC])
        k.eps_ln, k.eps_bn = held.sb("eps_ln", [P, 1]), held.sb("eps_bn", [P, 1])
        w.w_ext = held.sb("w_ext", [P, F // P, 2 * HEADS])
        w.v_edge, w.mean_logit = held.sb("v_edge", [P, 4, HEADS]), held.sb("mean_logit", [P, HEADS])
        w.node_logit = held.sb("node_logit", [P, NT * 2 * HEADS])
        w.dst_own = held.sb("dst_own", [P, NT, 2 * HEADS])
        w.above, w.maximum = held.sb("above", [P, NT, HEADS]), held.sb("maximum", [P, NT, HEADS])
        w.self_weight = held.sb("self_weight", [P, NT, HEADS])
        w.bn_scale = held.sb("bn_scale", [P, F])
        w.dinv, w.rdeg = held.sb("dinv", [P, NT]), held.sb("rdeg", [P, NT])
        dst_tiles, src_tiles = (held.sb(n, [P, TILES_PAD], I32) for n in ("dst_tiles", "src_tiles"))

        constants(nc, k)
        with Scope(nc, "sort") as srt:
            w.records = srt.sb("records", [P, EC, REC])
            slots = srt.sb("slots", [P, EC], I32)
            blank = srt.sb("blank", [P, TC * REC])
            setup(nc, k, inp, w, blank)
            for name, key, other, table, tiles in (("pd", "dst", "src", by_dst, dst_tiles),
                                                   ("ps", "src", "dst", by_src, src_tiles)):
                place(nc, k, name, inp[key], slots, tiles, w.records, inp[other])
                scatter_records(nc, name + "s", w.records, slots, table, blank)

        gat_projection(nc, k, w, inp, x0, h_table, src_table)
        rec = held.sb("rec", [P, TILES_PAD, REC])
        acc = held.sb("acc", [P, NT, ACCW])
        load_records(nc, "ld", by_dst, rec)
        with Scope(nc, "gat") as gat:
            w.attr_logit = gat.sb("attr_logit", [P, TILES_PAD, HEADS])
            w.logit = gat.sb("logit", [P, TILES_PAD, HEADS])
            edge_logits(nc, k, w, rec)
            attention_maxima(nc, k, w, rec, dst_tiles, src_table)
            self_loops(nc, k, w, h_table, acc)
            attention_sums(nc, k, w, rec, dst_tiles, h_table, acc)
        batch_norm(nc, k, w, inp, acc)
        gat_output(nc, k, w, inp, x0, x1, scaled, acc)
        aggregate(nc, k, "g1", rec, dst_tiles, scaled, F, acc, clear=False)
        gcn_hidden(nc, k, w, inp, scaled_hid, acc)
        aggregate(nc, k, "g2", rec, dst_tiles, scaled_hid, HID, acc, clear=False)
        gcn_output(nc, k, w, inp, x1, x2, acc)
        aggregate(nc, k, "g3", rec, dst_tiles, x2, F, acc, clear=True)
        sage_output(nc, k, w, inp, x2, x3, acc)
        load_records(nc, "ld2", by_src, rec)
        aggregate(nc, k, "g4", rec, src_tiles, x3, F, acc, clear=True)
        conv_output(nc, k, w, inp, x3, result, acc)


def kernel(x, src, dst, edge_attr_4, edge_weight, L0_gnn_W, L0_gnn_W_edge, L0_gnn_att_src, L0_gnn_att_dst,
           L0_gnn_att_edge, L0_gnn_bias, L0_gnn_gamma, L0_gnn_beta, L1_gnn_W1, L1_gnn_b1, L1_gnn_W2, L1_gnn_b2,
           L2_gnn_W_self, L2_gnn_b_self, L2_gnn_W_neigh, L2_gnn_b_neigh, L3_gnn_weight, L3_gnn_bias):
    import numpy as np
    import concourse.bacc as bacc
    from concourse.bass_utils import run_bass_kernel_spmd

    arrays = laid_out(np, locals())
    nc = bacc.Bacc("TRN2", target_bir_lowering=False, num_devices=1)
    inp = {name: nc.dram_tensor("in_" + name, a.shape, mybir.dt.from_np(a.dtype), kind="ExternalInput").ap()
           for name, a in arrays.items()}
    result = nc.dram_tensor("out_x", (N_NODES, F), FP, kind="ExternalOutput").ap()
    build(nc, inp, result)
    r = run_bass_kernel_spmd(nc, [{"in_" + name: a for name, a in arrays.items()}], core_ids=[0])
    return r.results[0]["out_x"]


def laid_out(np, a):
    x = np.zeros((NODES_PAD, F), np.float32)
    x[:N_NODES] = np.asarray(a["x"])
    edges = np.zeros((EDGES_PAD, REC), np.float32)
    edges[:N_EDGES, R_W] = np.asarray(a["edge_weight"])
    edges[:N_EDGES, R_EA:R_EA + 4] = np.asarray(a["edge_attr_4"])

    def padded(index):
        out = np.full(EDGES_PAD, NODES_PAD, np.int32)
        out[:N_EDGES] = np.asarray(index)
        return out.reshape(P, EC)

    def flat(name):
        return np.ascontiguousarray(np.asarray(a[name])).reshape(-1)

    def rows(name):
        return np.ascontiguousarray(np.asarray(a[name]))

    def turned(name):
        return np.ascontiguousarray(np.asarray(a[name]).T)

    return {
        "x": x, "edges": edges.reshape(P, EC * REC), "src": padded(a["src"]), "dst": padded(a["dst"]),
        "W0": rows("L0_gnn_W"), "W_edge": flat("L0_gnn_W_edge"), "att_src": flat("L0_gnn_att_src"),
        "att_dst": flat("L0_gnn_att_dst"), "att_edge": flat("L0_gnn_att_edge"), "bias": flat("L0_gnn_bias"),
        "gamma": flat("L0_gnn_gamma"), "beta": flat("L0_gnn_beta"), "W1": rows("L1_gnn_W1"),
        "b1": flat("L1_gnn_b1"), "W2": rows("L1_gnn_W2"), "b2": flat("L1_gnn_b2"),
        "W_self_t": turned("L2_gnn_W_self"), "b_self": flat("L2_gnn_b_self"),
        "W_neigh_t": turned("L2_gnn_W_neigh"), "b_neigh": flat("L2_gnn_b_neigh"),
        "W3": rows("L3_gnn_weight"), "b3": flat("L3_gnn_bias"),
    }
```

```python
from contextlib import ExitStack

import concourse.bass as bass
from concourse import mybir

FP = mybir.dt.float32
I32 = mybir.dt.int32
BF = mybir.dt.bfloat16
ALU = mybir.AluOpType
ACT = mybir.ActivationFunctionType
AX = mybir.AxisListType

P = 128
N_NODES, F, HEADS, N_EDGES, HID = 3125, 512, 4, 50000, 256
C = F // HEADS
NT = -(-N_NODES // P)
NODES_PAD = NT * P
LAST_ROWS = N_NODES - (NT - 1) * P
BT = 8
EC = -(-N_EDGES // (P * BT)) * BT
EDGES_PAD = P * EC
TILES_USED = (N_EDGES + NT * (P - 1)) // P
TILES = -(-TILES_USED // (4 * BT)) * 4 * BT
TILES_PAD = TILES + 3 * BT
TC = TILES_PAD + -(-(EDGES_PAD - N_EDGES) // P)
REC = 8
R_LOCAL, R_OTHER, R_W, R_EA = 0, 1, 2, 4
NEG_SLOPE, EPS_BN, EPS_LN, EPS_DEN, EPS_NORM = 0.2, 1e-5, 1e-5, 1e-16, 1e-12
MASKED = -1e30
ACCW = F + BT
DEN, DEG = F, F + HEADS
TINY = 1e-30


class Chain:

    def __init__(self, eng, sem, base=0):
        self.eng, self.sem, self.base, self.n = eng, sem, base, 0

    def run(self, instruction):
        instruction.then_inc(self.sem, 1)
        self.n += 1
        self.eng.wait_ge(self.sem, self.base + self.n)


def tiles_ahead(eng, first, second, ahead=1):
    for t in range(ahead):
        first(t, t % 4)
    looped = (NT - ahead) // 4 * 4
    with eng.Fori(0, looped // 4) as i:
        for q in range(4):
            first(i * 4 + (q + ahead), (q + ahead) % 4)
            second(i * 4 + q, q)
    for t in range(looped, NT):
        if t + ahead < NT:
            first(t + ahead, (t + ahead) % 4)
        second(t, t % 4)


def edge_steps(eng, begin, step):
    begin()
    with eng.Fori(0, TILES // BT // 4) as i:
        for q in range(4):
            for n in range(BT):
                step(i * 4 + q, q, n)


def later(g, q, n, by):
    return g + (n + by) // BT, (q + (n + by) // BT) % 4, (n + by) % BT


def nothing(t, q):
    pass


def uses4(t, q, each):
    return (t - q) * (each // 4) + each


def col(ap, j, n=1):
    return ap[:, bass.ds(j, n)]


def bucket_registers(nc, engine, buckets, j):
    _, values = nc.values_load_multi_w_load_instructions(
        buckets[0:1, bass.ds(j, BT)], engines=[engine], min_val=0, max_val=NT - 1,
        skip_runtime_bounds_check_because="the node tile numbers are clamped")
    return values


class Scope:

    def __init__(self, nc, name):
        self.nc, self.name, self.ctx, self.sems = nc, name, ExitStack(), []

    def __enter__(self):
        return self

    def __exit__(self, *exc):
        if self.sems and exc[0] is None:
            self.nc.clear_and_free_semaphores(self.sems)
            self.nc.all_engine_barrier(sem_only=True)
        self.ctx.close()

    def sb(self, name, shape, dt=FP):
        return self.ctx.enter_context(self.nc.sbuf_tensor(f"{self.name}_{name}", shape, dt))

    def ps(self, name, shape):
        return self.ctx.enter_context(self.nc.psum_tensor(f"{self.name}_{name}", shape, FP))

    def sem(self, name):
        self.sems.append(self.nc.alloc_semaphore(f"{self.name}_{name}"))
        return self.sems[-1]


def constants(nc, k):
    with Scope(nc, "cst") as s:
        ii = s.sb("ii", [P, P], I32)
        ic = s.sb("ic", [P, TILES_PAD], I32)
        ie = s.sb("ie", [P, EC], I32)
        pf = s.sb("pf", [P, P])
        ef = s.sb("ef", [P, EC])
        made = s.sem("made")
        own = s.sem("own")
        with nc.Block() as block:
            @block.gpsimd
            def _(pool):
                pool.iota(ii[:, :], [[0, P]], base=0, channel_multiplier=1).then_inc(made, 1)
                pool.iota(ic[:, :], [[1, TILES_PAD]], base=0, channel_multiplier=0).then_inc(made, 1)
                pool.iota(ie[:, :], [[1, EC]], base=0, channel_multiplier=EC).then_inc(made, 1)

            @block.vector
            def _(dve):
                own_chain = Chain(dve, own)
                dve.wait_ge(made, 3)
                dve.tensor_copy(pf[:, :], ii[:, :])
                dve.tensor_copy(ef[:, :], ie[:, :])
                own_chain.run(dve.tensor_copy(k.columns[:, :], ic[:, :]))
                dve.tensor_tensor(k.ident[:, :], k.columns[:, 0:P], pf[:, :], ALU.is_equal)
                dve.tensor_tensor(k.before[:, :], k.columns[:, 0:P], pf[:, :], ALU.is_gt)
                dve.memset(k.ones[:, :], 1.0)
                dve.tensor_scalar(k.last_rows[:, :], pf[:, :], float(LAST_ROWS), None, ALU.is_lt)
                own_chain.run(dve.tensor_scalar(k.pad_slot[:, :], ef[:, :], float(N_EDGES), None, ALU.is_ge))
                own_chain.run(dve.tensor_scalar(ef[:, :], ef[:, :], float(TILES_PAD * P - N_EDGES), None, ALU.add))
                dve.tensor_tensor(k.pad_slot[:, :], k.pad_slot[:, :], ef[:, :], ALU.mult)
    return


def place(nc, k, name, key_dram, slots, buckets, records, other_dram):
    with Scope(nc, name) as s:
        key, other = s.sb("key", [P, EC], I32), s.sb("other", [P, EC], I32)
        key_i, key_f, low_f = s.sb("key_i", [P, EC], I32), s.sb("key_f", [P, EC]), s.sb("low_f", [P, EC])
        ohot = s.sb("ohot", [P, NT, EC], BF)
        seen = s.sb("seen", [P, TILES_PAD * NT])
        ends, cnt = s.sb("ends", [P, NT + 1]), s.sb("cnt", [P, NT])
        tiles_i, tiles_f = s.sb("tiles_i", [P, NT], I32), s.sb("tiles_f", [P, NT])
        last, start, off = s.sb("last", [P, NT]), s.sb("start", [P, NT]), s.sb("off", [P, NT])
        tile_f = s.sb("tile_f", [P, TILES_PAD])
        p_cnt = s.ps("p_cnt", [P, 2 * NT])
        loaded, own, counted, summed = s.sem("loaded"), s.sem("own"), s.sem("counted"), s.sem("summed")
        with nc.Block() as block:
            @block.sync
            def _(sp):
                sp.dma_start(key[:, :], key_dram).then_inc(loaded, 16)
                sp.dma_start(other[:, :], other_dram).then_inc(loaded, 16)

            @block.tensor
            def _(pe):
                pe.wait_ge(counted, 1)
                pe.matmul(p_cnt[:, 0:NT], k.before[:, :], cnt[:, :], start=True, stop=True)
                pe.matmul(p_cnt[:, NT:2 * NT], k.ones[:, :], cnt[:, :], start=True, stop=True).then_inc(summed, 1)

            @block.vector
            def _(dve):
                c = Chain(dve, own)
                dve.wait_ge(loaded, 32)
                dve.tensor_copy(records[:, :, R_OTHER].bitcast(I32), other[:, :])
                c.run(dve.tensor_scalar(key_i[:, :], key[:, :], 7, None, ALU.arith_shift_right))
                c.run(dve.tensor_copy(key_f[:, :], key_i[:, :]))
                c.run(dve.tensor_scalar(key_i[:, :], key[:, :], P - 1, None, ALU.bitwise_and))
                dve.tensor_copy(records[:, :, R_LOCAL], key_i[:, :])
                c.run(dve.tensor_tensor(
                    ohot[:, :, :], key_f[:, :].unsqueeze(1).broadcast_to([P, NT, EC]),
                    k.columns[:, 0:NT].unsqueeze(2).broadcast_to([P, NT, EC]), ALU.is_equal))
                flat = ohot[:, :, :].rearrange("p b c -> p (b c)")
                c.run(dve.tensor_tensor_scan(seen[:, 0:NT * EC], flat, flat, 0.0, ALU.add, ALU.max))
                seen_bc = seen[:, 0:NT * EC].rearrange("p (b c) -> p b c", b=NT)
                dve.memset(ends[:, 0:1], 0.0)
                c.run(dve.tensor_copy(ends[:, 1:NT + 1], seen_bc[:, :, EC - 1]))
                dve.tensor_tensor(cnt[:, :], ends[:, 1:NT + 1], ends[:, 0:NT], ALU.subtract).then_inc(counted, 1)
                dve.wait_ge(summed, 1)
                c.run(dve.tensor_scalar(tiles_i[:, :], p_cnt[:, NT:2 * NT], float(P - 1), None, ALU.add))
                c.run(dve.tensor_scalar(tiles_i[:, :], tiles_i[:, :], 7, None, ALU.arith_shift_right))
                c.run(dve.tensor_copy(tiles_f[:, :], tiles_i[:, :]))
                c.run(dve.tensor_tensor_scan(last[:, :], tiles_f[:, :], tiles_f[:, :], 0.0, ALU.add, ALU.max))
                c.run(dve.tensor_tensor(start[:, :], last[:, :], tiles_f[:, :], ALU.subtract))
                c.run(dve.scalar_tensor_tensor(off[:, :], start[:, :], float(P), p_cnt[:, 0:NT], ALU.mult, ALU.add))
                c.run(dve.scalar_tensor_tensor(off[:, :], off[:, :], -1.0, ends[:, 0:NT], ALU.add, ALU.subtract))
                c.run(dve.tensor_tensor(seen_bc, seen_bc, off[:, :].unsqueeze(2).broadcast_to([P, NT, EC]), ALU.add))
                c.run(dve.tensor_tensor(seen_bc, seen_bc, ohot[:, :, :], ALU.mult))
                c.run(dve.tensor_reduce(key_f[:, :], seen_bc.rearrange("p b c -> p c b"), AX.X, ALU.add))
                c.run(dve.tensor_tensor(key_f[:, :], key_f[:, :], k.pad_slot[:, :], ALU.add))
                c.run(dve.tensor_copy(slots[:, :], key_f[:, :]))
                c.run(dve.tensor_scalar(key_i[:, :], slots[:, :], 7, None, ALU.arith_shift_right))
                c.run(dve.tensor_copy(key_f[:, :], key_i[:, :]))
                c.run(dve.tensor_scalar(slots[:, :], slots[:, :], P - 1, None, ALU.bitwise_and))
                c.run(dve.tensor_copy(low_f[:, :], slots[:, :]))
                c.run(dve.scalar_tensor_tensor(slots[:, :], low_f[:, :], float(TC), key_f[:, :], ALU.mult, ALU.add))
                ended = seen[:, 0:TILES_PAD * NT].rearrange("p (j b) -> p j b", b=NT)
                c.run(dve.tensor_tensor(
                    ended, last[:, :].unsqueeze(1).broadcast_to([P, TILES_PAD, NT]),
                    k.columns[:, :].unsqueeze(2).broadcast_to([P, TILES_PAD, NT]), ALU.is_le))
                c.run(dve.tensor_reduce(tile_f[:, :], ended, AX.X, ALU.add))
                c.run(dve.tensor_scalar(buckets[:, :], tile_f[:, :], float(NT - 1), None, ALU.min))


def scatter_records(nc, name, records, slots, table, blank):
    with Scope(nc, name) as s:
        rec = s.sb("rec", [P, 2, BT, REC])
        row = s.sb("row", [P, 2, BT], I32)
        blanked, staged = s.sem("blanked"), s.sem("staged")
        written = [s.sem(f"written{h}") for h in range(2)]
        issued = s.sem("issued")
        batches = EC // BT
        with nc.Block() as block:
            @block.sync
            def _(sp):
                sp.dma_start(table.rearrange("(l t) f -> l (t f)", l=P), blank[:, :]).then_inc(blanked, 16)

            @block.scalar
            def _(act):
                def stage(g, h, reused=True):
                    if reused:
                        act.wait_ge(written[h], (g - h) * (BT * 16 // 2))
                    act.copy(row[:, h, :], col(slots, g * BT, BT))
                    act.copy(rec[:, h, :, :], col(records, g * BT, BT)).then_inc(staged, 1)

                stage(0, 0, reused=False)
                stage(1, 1, reused=False)
                with act.Fori(1, (batches - 1) // 2) as i:
                    g = i * 2
                    stage(g, 0)
                    stage(g + 1, 1)
                stage(batches - 1, 0)

            @block.gpsimd
            def _(pool):
                pool.wait_ge(blanked, 16)

                def scatter(g, h):
                    pool.wait_ge(staged, g + 1)
                    pool.sem_inc(issued, 1)
                    for n in range(BT):
                        pool.indirect_dma_start(
                            table, bass.IndirectOffsetOnAxis(row[:, h, n:n + 1], 0),
                            rec[:, h, n, :], None).then_inc(written[h], 16)

                with pool.Fori(0, (batches - 1) // 2) as i:
                    g = i * 2
                    scatter(g, 0)
                    scatter(g + 1, 1)
                scatter(batches - 1, 0)
                pool.wait_ge(written[0], (batches + 1) // 2 * BT * 16)
                pool.wait_ge(written[1], batches // 2 * BT * 16)


def load_records(nc, name, table, rec):
    with Scope(nc, name) as s:
        loaded = s.sem("loaded")
        with nc.Block() as block:
            @block.sync
            def _(sp):
                sp.dma_start(rec[:, :, :].rearrange("p t f -> p (t f)"),
                             table.rearrange("(l t) f -> l (t f)", l=P)[:, 0:TILES_PAD * REC]).then_inc(loaded, 16)
                sp.wait_ge(loaded, 16)


def aggregate(nc, k, name, rec, buckets, table, width, acc, clear):
    RING, AHEAD = 4, 2
    with Scope(nc, name) as s:
        rows = s.sb("rows", [P, BT, width])
        index = s.sb("index", [P, 2, BT], I32)
        hot = s.sb("hot", [P, RING, P])
        part = [s.ps(f"part{i}", [P, F]) for i in range(RING)]
        gathered = [s.sem(f"gathered{n}") for n in range(BT)]
        indexed, granted, hot_ready = s.sem("indexed"), s.sem("granted"), s.sem("hot_ready")
        summed, added, cleared = s.sem("summed"), s.sem("added"), s.sem("cleared")
        other = rec[:, :, R_OTHER].bitcast(I32)
        with nc.Block() as block:
            @block.scalar
            def _(act):
                with act.Fori(0, TILES // BT // 2) as i:
                    g = i * 2
                    for h in range(2):
                        act.wait_ge(summed, g * BT + BT * (h + 1))
                        act.copy(index[:, h, :], col(other, g * BT + BT * h, BT)).then_inc(indexed, 1)

            @block.gpsimd
            def _(pool):
                with pool.Fori(0, TILES // BT // 2) as i:
                    g = i * 2
                    for h in range(2):
                        pool.wait_ge(indexed, g + (h + 1))
                        for n in range(BT):
                            pool.wait_ge(summed, g * BT + (h * BT + n + 1 + BT))
                            pool.sem_inc(granted, 1)
                            pool.indirect_dma_start(
                                rows[:, n, :], None, table,
                                bass.IndirectOffsetOnAxis(index[:, h, n:n + 1], 0)).then_inc(gathered[n], 16)

            @block.vector
            def _(dve):
                def weigh(j, n):
                    dve.tensor_scalar(hot[:, n % RING, :], k.columns[:, 0:P], col(rec[:, :, R_LOCAL], j),
                                      col(rec[:, :, R_W], j), ALU.is_equal, ALU.mult).then_inc(hot_ready, 1)

                if clear:
                    dve.memset(acc[:, :, 0:width], 0.0).then_inc(cleared, 1)
                    dve.wait_ge(cleared, 1)
                for n in range(AHEAD):
                    weigh(n, n)
                with dve.Fori(0, TILES // BT // 2) as i:
                    g = i * 2
                    for h in range(2):
                        tile = bucket_registers(nc, mybir.EngineType.DVE, buckets, g * BT + h * BT)
                        for n in range(BT):
                            u = h * BT + n
                            dve.wait_ge(summed, g * BT + (u + AHEAD - RING + 2 * BT + 1))
                            weigh(g * BT + (u + AHEAD), u + AHEAD)
                            dve.wait_ge(summed, g * BT + (u + 2 * BT + 1))
                            dve.wait_ge(added, g * BT + (u + RING))
                            here = acc[:, bass.ds(tile[n], 1), 0:width]
                            dve.tensor_tensor(here, here, part[n % RING][:, 0:width].unsqueeze(1),
                                              ALU.add).then_inc(added, 1)

            @block.tensor
            def _(pe):
                pe.sem_inc(summed, 2 * BT)
                pe.sem_inc(added, RING)
                with pe.Fori(0, TILES // BT // 2) as i:
                    g = i * 2
                    for u in range(2 * BT):
                        pe.wait_ge(hot_ready, g * BT + (u + 1))
                        pe.wait_ge(gathered[u % BT], g * 16 + (u // BT + 1) * 16)
                        pe.wait_ge(added, g * BT + (u + 1))
                        pe.matmul(part[u % RING][:, 0:width], hot[:, u % RING, :], rows[:, u % BT, :],
                                  start=True, stop=True).then_inc(summed, 1)


def setup(nc, k, inp, w, blank):
    with Scope(nc, "set") as s:
        w0 = s.sb("w0", [P, F // P, F])
        att = s.sb("att", [P, 3, F])
        w_edge = s.sb("w_edge", [P, 4, F])
        prod = s.sb("prod", [P, F // P, F])
        ea_sum, mean_ea = s.sb("ea_sum", [P, 4]), s.sb("mean_ea", [P, 4])
        tmp = s.sb("tmp", [P, HEADS, 4])
        p_ea = s.ps("p_ea", [P, 4])
        loaded, own, counted, summed = s.sem("loaded"), s.sem("own"), s.sem("counted"), s.sem("summed")
        with nc.Block() as block:
            @block.sync
            def _(sp):
                sp.dma_start(w0[:, :, :], inp["W0"].rearrange("(t p) n -> p t n", p=P)).then_inc(loaded, 16)
                for i, n in enumerate(("att_src", "att_dst", "att_edge")):
                    sp.dma_start(att[:, i, :], inp[n].partition_broadcast(P)).then_inc(loaded, 16)
                sp.dma_start(w_edge[:, :, :].rearrange("p a n -> p (a n)"),
                             inp["W_edge"].partition_broadcast(P)).then_inc(loaded, 16)
                sp.dma_start(w.records[:, :, :].rearrange("p c f -> p (c f)"), inp["edges"]).then_inc(loaded, 16)

            @block.tensor
            def _(pe):
                pe.wait_ge(counted, 1)
                pe.matmul(p_ea[:, :], k.ones[:, :], ea_sum[:, :], start=True, stop=True).then_inc(summed, 1)

            @block.vector
            def _(dve):
                c = Chain(dve, own)
                dve.memset(k.eps_ln[:, :], EPS_LN)
                dve.memset(k.eps_bn[:, :], EPS_BN)
                c.run(dve.memset(blank[:, :], 0.0))
                dve.memset(blank[:, :].rearrange("p (t f) -> p t f", f=REC)[:, :, R_LOCAL], -1.0)
                dve.wait_ge(loaded, 96)
                dve.tensor_reduce(ea_sum[:, :], w.records[:, :, R_EA:R_EA + 4].rearrange("p c f -> p f c"),
                                  AX.X, ALU.add).then_inc(counted, 1)
                for i in range(2):
                    c.run(dve.tensor_tensor(prod[:, :, :], w0[:, :, :], att[:, i, :].unsqueeze(1).broadcast_to(
                        [P, F // P, F]), ALU.mult))
                    c.run(dve.tensor_reduce(
                        w.w_ext[:, :, i * HEADS:(i + 1) * HEADS],
                        prod[:, :, :].rearrange("p t (h c) -> p t h c", h=HEADS), AX.X, ALU.add))
                c.run(dve.tensor_tensor(prod[:, :, :], w_edge[:, :, :], att[:, 2, :].unsqueeze(1).broadcast_to(
                    [P, 4, F]), ALU.mult))
                c.run(dve.tensor_reduce(w.v_edge[:, :, :], prod[:, :, :].rearrange(
                    "p a (h c) -> p a h c", h=HEADS), AX.X, ALU.add))
                dve.wait_ge(summed, 1)
                c.run(dve.tensor_scalar(mean_ea[:, :], p_ea[:, :], 1.0 / N_EDGES, None, ALU.mult))
                c.run(dve.tensor_tensor(tmp[:, :, :], w.v_edge[:, :, :].rearrange("p a h -> p h a"),
                                        mean_ea[:, :].unsqueeze(1).broadcast_to([P, HEADS, 4]), ALU.mult))
                c.run(dve.tensor_reduce(w.mean_logit[:, :], tmp[:, :, :], AX.X, ALU.add))


def node_pass(nc, k, s, kt, constants, weights, banks, loads, stores, prepare, n_prepare, finish,
              n_finish, act_steps):
    s.a_t = s.sb("a_t", [P, 2, kt * P])
    p_t = [s.ps(f"p_t{i}", [P, kt * P]) for i in range(2)]
    constant = s.sem("constant")
    loaded = [s.sem(f"loaded{q}") for q in range(4)]
    stored, saved = s.sem("stored"), s.sem("saved")
    prepared, turned, copied, multiplied = (s.sem(n) for n in ("prepared", "turned", "copied", "multiplied"))
    finished, own_p, own_f = s.sem("finished"), s.sem("own_p"), s.sem("own_f")
    asked, answered = s.sem("asked"), s.sem("answered")
    n_loads, n_stores = len(loads(0, 0)), len(stores(0, 0))
    n_steps = len(act_steps)

    with nc.Block() as block:
        @block.sync
        def _(sp):
            for to, of in constants:
                sp.dma_start(to, of).then_inc(constant, 16)

            def load(t, q):
                sp.wait_ge(finished, t + 1)
                for to, of in loads(t, q):
                    sp.dma_start(to, of).then_inc(loaded[q], 16)

            if n_loads:
                with sp.Fori(0, (NT - 1) // 4) as i:
                    t = i * 4
                    for q in range(4):
                        load(t + q, q)
                load(NT - 1, 0)

        @block.vector
        def _(dve):
            dve.wait_ge(constant, 16 * len(constants))

            def first(t, q):
                if prepare is None:
                    return
                if n_loads:
                    dve.wait_ge(loaded[q], uses4(t, q, 16 * n_loads))
                dve.wait_ge(turned, t + 1)
                c = Chain(dve, own_p, t * n_prepare)
                prepare(dve, c, t, q).then_inc(prepared, 1)
                assert c.n == n_prepare

            def second(t, q):
                dve.wait_ge(multiplied, t + 3)
                dve.wait_ge(saved, t + 1)

                def through_act(i, instruction):
                    instruction.then_inc(asked, 1)
                    dve.wait_ge(answered, t * n_steps + (i + 1))

                c = Chain(dve, own_f, t * n_finish)
                finish(dve, c, through_act, t, q).then_inc(finished, 1)
                assert c.n == n_finish

            tiles_ahead(dve, first, second, ahead=2)

        @block.tensor
        def _(pe):
            pe.sem_inc(turned, 4)
            pe.sem_inc(copied, 2)
            pe.sem_inc(multiplied, 2)
            pe.sem_inc(finished, 4)
            pe.wait_ge(constant, 16 * len(constants))

            def first(t, q):
                if prepare is None:
                    pe.wait_ge(loaded[q], uses4(t, q, 16 * n_loads))
                else:
                    pe.wait_ge(prepared, t + 1)
                pe.wait_ge(copied, t + 1)
                for i in range(kt):
                    last = pe.transpose(p_t[q % 2][:, i * P:(i + 1) * P], s.a[:, q, i * P:(i + 1) * P],
                                        k.ident[:, :])
                last.then_inc(turned, 1)

            def second(t, q):
                pe.wait_ge(copied, t + 3)
                pe.wait_ge(finished, t + 3)
                for bank, n, weight in weights:
                    for i in range(kt):
                        last = pe.matmul(banks[q % 2][:, bank:bank + n], s.a_t[:, q % 2, i * P:(i + 1) * P],
                                         weight[:, i, :], start=(i == 0), stop=(i == kt - 1))
                last.then_inc(multiplied, 1)

            tiles_ahead(pe, first, second)

        @block.scalar
        def _(act):
            def first(t, q):
                act.wait_ge(turned, t + 5)
                act.wait_ge(multiplied, t + 1)
                act.copy(s.a_t[:, q % 2, :], p_t[q % 2][:, :]).then_inc(copied, 1)

            def second(t, q):
                for i, step in enumerate(act_steps):
                    act.wait_ge(asked, t * n_steps + (i + 1))
                    step(act, t, q).then_inc(answered, 1)

            tiles_ahead(act, first, second)

        @block.gpsimd
        def _(pool):
            def store(t, q):
                pool.wait_ge(finished, t + 5)
                for to, of in stores(t, q):
                    pool.dma_start(to, of).then_inc(stored, 16)
                pool.wait_ge(stored, (t + 1) * (16 * n_stores))
                pool.sem_inc(saved, 1)

            pool.sem_inc(saved, 2)
            tiles_ahead(pool, nothing, store)


class Norm:
    CHAINED = 3

    def __init__(self, k, s):
        self.k = k
        self.st, self.mv = s.sb("ln_st", [P, 6]), s.sb("ln_mv", [P, 2])
        self.passed = s.sem("ln_passed")
        self.std, self.rstd = s.sb("ln_std", [P, 1]), s.sb("ln_rstd", [P, 1])

    def act_step(self, act, t, q):
        return act.activation(self.std[:, :], self.mv[:, 1:2], ACT.Sqrt, bias=self.k.eps_ln[:, :])

    def apply(self, dve, c, through_act, i, y, out):
        c.run(dve.bn_stats(self.st[:, :], y))
        dve.sem_inc(self.passed, 1)
        through_act(i, dve.bn_aggr(self.mv[:, :], self.st[:, :]))
        c.run(dve.reciprocal(self.rstd[:, :], self.std[:, :]))
        return dve.tensor_scalar(out, y, self.mv[:, 0:1], self.rstd[:, :], ALU.subtract, ALU.mult)


def rows_of(table, t):
    return table[bass.ds(t * P, P), :]


def gat_projection(nc, k, w, inp, x0, h_table, src_table):
    with Scope(nc, "n0") as s:
        s.a = s.sb("a", [P, 4, F])
        w0 = s.sb("w0", [P, F // P, F])
        h = s.sb("h", [P, 2, F])
        banks = [s.ps(f"bank{i}", [P, 2 * F]) for i in range(2)]

        def finish(dve, c, through_act, t, q):
            dve.tensor_copy(col(w.node_logit, t * 2 * HEADS, 2 * HEADS), banks[q % 2][:, F:F + 2 * HEADS])
            return dve.tensor_copy(h[:, q % 2, :], banks[q % 2][:, 0:F])

        node_pass(nc, k, s, F // P,
                  [(w0[:, :, :], inp["W0"].rearrange("(t p) n -> p t n", p=P))],
                  [(0, F, w0), (F, 2 * HEADS, w.w_ext)], banks,
                  lambda t, q: [(s.a[:, q, :], rows_of(x0, t))],
                  lambda t, q: [(rows_of(h_table, t), h[:, q % 2, :]),
                                (rows_of(src_table, t), col(w.node_logit, t * 2 * HEADS, HEADS))],
                  None, 0, finish, 0, [])


def edge_logits(nc, k, w, rec):
    with Scope(nc, "lg") as s:
        pad = s.sb("pad", [P, TILES_PAD])
        both = s.sb("both", [P, NT, HEADS])
        own = s.sem("own")
        with nc.Block() as block:
            @block.vector
            def _(dve):
                c = Chain(dve, own)
                c.run(dve.tensor_scalar(pad[:, :], rec[:, :, R_LOCAL], 0.0, MASKED, ALU.is_lt, ALU.mult))
                for a in range(4):
                    for h in range(HEADS):
                        before = pad[:, :] if a == 0 else w.attr_logit[:, :, h]
                        last = dve.scalar_tensor_tensor(
                            w.attr_logit[:, :, h], rec[:, :, R_EA + a], w.v_edge[:, a, h:h + 1], before,
                            ALU.mult, ALU.add)
                    c.run(last)
                node = w.node_logit[:, :].rearrange("p (t h) -> p t h", h=2 * HEADS)
                c.run(dve.tensor_tensor(both[:, :, :], node[:, :, 0:HEADS], node[:, :, HEADS:2 * HEADS], ALU.add))
                c.run(dve.tensor_tensor(both[:, :, :], both[:, :, :], w.mean_logit[:, :].unsqueeze(1).broadcast_to(
                    [P, NT, HEADS]), ALU.add))
                dve.tensor_copy(w.dst_own[:, :, 0:HEADS], node[:, :, HEADS:2 * HEADS])
                dve.scalar_tensor_tensor(w.dst_own[:, :, HEADS:2 * HEADS], both[:, :, :], NEG_SLOPE, both[:, :, :],
                                         ALU.mult, ALU.max)
                c.run(dve.memset(w.above[:, :, :], 0.0))


class ByNode:

    def __init__(self, nc, k, s, rec, buckets, values, width):
        self.nc, self.k, self.rec, self.buckets, self.values = nc, k, rec, buckets, values
        self.index = s.sb("index", [P, 4, BT], I32)
        self.hot = s.sb("hot", [P, 4, BT, P])
        self.hot_t = s.sb("hot_t", [P, BT, P])
        self.near = s.sb("near", [P, BT, width])
        self.p_hot = s.ps("p_hot", [P, BT * P])
        self.p_node = s.ps("p_node", [P, BT, width])
        self.indexed, self.hot_ready, self.turned, self.copied, self.by_node = (
            s.sem(n) for n in ("indexed", "hot_ready", "turned", "copied", "by_node"))

    def stage_index(self, act, b, q):
        act.copy(self.index[:, q, :], col(self.rec[:, :, R_OTHER].bitcast(I32), b * BT, BT)).then_inc(self.indexed, 1)

    def make_hot(self, dve, b, q, n):
        dve.tensor_scalar(self.hot[:, q, n, :], self.k.columns[:, 0:P], col(self.rec[:, :, R_LOCAL], b * BT + n),
                          None, ALU.is_equal).then_inc(self.hot_ready, 1)

    def turn(self, pe, b, q, n):
        pe.wait_ge(self.hot_ready, b * BT + (n + 1))
        if n % 4 == 0:
            pe.wait_ge(self.copied, b * 2 + n // 4)
        pe.transpose(self.p_hot[:, n * P:(n + 1) * P], self.hot[:, q, n, :],
                     self.k.ident[:, :]).then_inc(self.turned, 1)

    def copy_near(self, act, b, n):
        if n == 0:
            self.tile = bucket_registers(self.nc, mybir.EngineType.Activation, self.buckets, b * BT)
            act.wait_ge(self.by_node, b)
        for m in (n, n + 1):
            act.copy(self.near[:, m:m + 1, :], self.values[:, bass.ds(self.tile[m], 1), :])

    def copy_turned(self, act, b, half):
        act.wait_ge(self.turned, b * BT + 4 * (half + 1))
        act.wait_ge(self.by_node, b)
        act.copy(self.hot_t[:, 4 * half:4 * half + 4, :].rearrange("p n e -> p (n e)"),
                 self.p_hot[:, 4 * half * P:4 * (half + 1) * P]).then_inc(self.copied, 1)

    def find(self, pe, b):
        pe.wait_ge(self.copied, b * 2 + 2)
        for n in range(BT):
            last = pe.matmul(self.p_node[:, n, :], self.hot_t[:, n, :], self.near[:, n, :], start=True, stop=True)
        last.then_inc(self.by_node, 1)

    def dve_step(self, dve, g, q, n):
        self.make_hot(dve, g + 2, (q + 2) % 4, n)

    def pe_step(self, pe, g, q, n):
        self.turn(pe, g + 2, (q + 2) % 4, n)

    def act_step(self, act, g, q, n):
        if n == 0:
            self.copy_turned(act, g + 1, 1)
        if n == 4:
            self.copy_turned(act, g + 2, 0)
        if n >= 4:
            self.copy_near(act, g + 2, (n - 4) * 2)

    def dve_begin(self, dve):
        for b in range(2):
            for n in range(BT):
                self.make_hot(dve, b, b, n)

    def pe_begin(self, pe):
        for b in range(2):
            for n in range(BT):
                self.turn(pe, b, b, n)
            if b == 0:
                self.find(pe, 0)

    def act_begin(self, act):
        for n in range(0, BT, 2):
            self.copy_near(act, 0, n)
        self.copy_turned(act, 0, 0)
        self.copy_turned(act, 0, 1)
        for n in range(0, BT, 2):
            self.copy_near(act, 1, n)
        self.copy_turned(act, 1, 0)


def attention_maxima(nc, k, w, rec, buckets, src_table):
    DR, BANKS, AHEAD, DVE_HEADS = 6, 4, 4, 1
    with Scope(nc, "mx") as s:
        pre = ByNode(nc, k, s, rec, buckets, w.dst_own, 2 * HEADS)
        src = s.sb("src", [P, 4, BT, HEADS])
        over = s.sb("over", [P, 2, BT, HEADS])
        raw = s.sb("raw", [P, BT, HEADS])
        diag = s.sb("diag", [P, BT, HEADS, P])
        top = s.sb("top", [P, BT, HEADS])
        p_top = [s.ps(f"p_top{i}", [P, HEADS, P]) for i in range(BANKS)]
        gathered = [s.sem(f"gathered{q}") for q in range(4)]
        granted, logits, own, diag_dve, diag_act = (
            s.sem(n) for n in ("granted", "logits", "own", "diag_dve", "diag_act"))
        masked, reduced, raised = s.sem("masked"), s.sem("reduced"), s.sem("raised")

        with nc.Block() as block:
            @block.scalar
            def _(act):
                def spread(b, q, n):
                    act.wait_ge(logits, b + 3)
                    act.wait_ge(masked, b * BT + (n + 1 + BT))
                    for hd in range(DVE_HEADS, HEADS):
                        last = act.activation(diag[:, n, hd, :], k.ident[:, :], ACT.Copy,
                                              scale=over[:, q % 2, n, hd:hd + 1])
                    last.then_inc(diag_act, 1)

                def begin():
                    for b in range(3):
                        pre.stage_index(act, b, b)
                    pre.act_begin(act)
                    for n in range(AHEAD):
                        spread(0, 0, n)

                def step(g, q, n):
                    pre.act_step(act, g, q, n)
                    if n == 3:
                        act.wait_ge(logits, g + 2)
                        pre.stage_index(act, g + 3, (q + 3) % 4)
                    spread(*later(g, q, n, AHEAD))

                edge_steps(act, begin, step)

            @block.gpsimd
            def _(pool):
                def gather(b, q):
                    pool.wait_ge(pre.indexed, b + 1)
                    pool.sem_inc(granted, 1)
                    for n in range(BT):
                        pool.indirect_dma_start(
                            src[:, q, n, :], None, src_table,
                            bass.IndirectOffsetOnAxis(pre.index[:, q, n:n + 1], 0)).then_inc(gathered[q], 16)

                for b in range(3):
                    gather(b, b)
                with pool.Fori(0, TILES // BT // 4) as i:
                    for q in range(4):
                        gather(i * 4 + (q + 3), (q + 3) % 4)
                for q in range(4):
                    pool.wait_ge(gathered[q], (TILES // BT // 4 + (q < 3)) * BT * 16)

            @block.tensor
            def _(pe):
                def begin():
                    pe.sem_inc(masked, 2 * BT)
                    pe.sem_inc(reduced, BANKS)
                    pe.sem_inc(raised, 1)
                    pe.sem_inc(logits, 2)
                    pre.pe_begin(pe)

                def step(g, q, n):
                    pe.wait_ge(diag_dve, g * BT + (n + 1))
                    pe.wait_ge(diag_act, g * BT + (n + 1))
                    pe.wait_ge(reduced, g * BT + (n + 1))
                    pe.matmul(p_top[n % BANKS][:, :, :], pre.hot[:, q, n, :], diag[:, n, :, :],
                              start=True, stop=True).then_inc(masked, 1)
                    pre.pe_step(pe, g, q, n)
                    if n == 1:
                        pe.wait_ge(logits, g + 3)
                        pre.find(pe, g + 1)

                edge_steps(pe, begin, step)

            @block.vector
            def _(dve):
                def make_logits(b, q):
                    c = Chain(dve, own, b * 3)
                    dve.wait_ge(gathered[q], (b - q) * (BT * 4) + BT * 16)
                    dve.wait_ge(pre.by_node, b + 1)
                    logit = w.logit[:, bass.ds(b * BT, BT), :]
                    c.run(dve.tensor_tensor(raw[:, :, :], src[:, q, :, :], pre.p_node[:, :, 0:HEADS], ALU.add))
                    c.run(dve.tensor_tensor(raw[:, :, :], raw[:, :, :],
                                            w.attr_logit[:, bass.ds(b * BT, BT), :], ALU.add))
                    c.run(dve.scalar_tensor_tensor(logit, raw[:, :, :], NEG_SLOPE, raw[:, :, :], ALU.mult, ALU.max))
                    dve.tensor_tensor(over[:, q % 2, :, :], logit, pre.p_node[:, :, HEADS:2 * HEADS],
                                      ALU.subtract).then_inc(logits, 1)

                def spread(b, q, n):
                    dve.wait_ge(logits, b + 3)
                    dve.wait_ge(masked, b * BT + (n + 1 + BT))
                    dve.tensor_scalar(diag[:, n, 0, :], k.ident[:, :], over[:, q % 2, n, 0:1], None,
                                      ALU.mult).then_inc(diag_dve, 1)

                def begin():
                    pre.dve_begin(dve)
                    make_logits(0, 0)
                    for n in range(AHEAD):
                        spread(0, 0, n)

                def step(g, q, n):
                    if n == 0:
                        step.tile = bucket_registers(nc, mybir.EngineType.DVE, buckets, g * BT)
                    if n == 2:
                        make_logits(g + 1, (q + 1) % 4)
                    pre.dve_step(dve, g, q, n)
                    spread(*later(g, q, n, AHEAD))
                    dve.wait_ge(masked, g * BT + (n + 1 + 2 * BT))
                    dve.tensor_reduce(top[:, n, :], p_top[n % BANKS][:, :, :], AX.X, ALU.max).then_inc(reduced, 1)
                    for m in (n - 1, n)[n == 0:] if n == BT - 1 else (n - 1,)[n == 0:]:
                        dve.wait_ge(reduced, g * BT + (m + 1 + BANKS))
                        dve.wait_ge(raised, g * BT + (m + 1))
                        here = w.above[:, bass.ds(step.tile[m], 1), :]
                        dve.tensor_tensor(here, here, top[:, m, :].unsqueeze(1), ALU.max).then_inc(raised, 1)

                edge_steps(dve, begin, step)


def self_loops(nc, k, w, h_table, acc):
    with Scope(nc, "sl") as s:
        h = s.sb("h", [P, 4, F])
        loaded = [s.sem(f"loaded{q}") for q in range(4)]
        own, under, exped, used = s.sem("own"), s.sem("under"), s.sem("exped"), s.sem("used")
        with nc.Block() as block:
            @block.sync
            def _(sp):
                sp.sem_inc(used, 4)

                def load(t, q):
                    sp.wait_ge(used, t + 1)
                    sp.dma_start(h[:, q, :], rows_of(h_table, t)).then_inc(loaded[q], 16)

                tiles_ahead(sp, nothing, load)

            @block.scalar
            def _(act):
                act.wait_ge(under, 1)
                act.activation(w.self_weight[:, :, :], w.above[:, :, :], ACT.Exp, scale=-1.0).then_inc(exped, 1)

            @block.vector
            def _(dve):
                c = Chain(dve, own)
                dve.tensor_tensor(w.maximum[:, :, :], w.above[:, :, :], w.dst_own[:, :, HEADS:2 * HEADS],
                                  ALU.add).then_inc(under, 1)
                dve.memset(acc[:, :, F:ACCW], 0.0).then_inc(own, 1)
                dve.wait_ge(exped, 1)
                dve.wait_ge(own, 1)
                dve.tensor_copy(acc[:, :, DEN:DEN + HEADS], w.self_weight[:, :, :])

                def scale(t, q):
                    dve.wait_ge(loaded[q], uses4(t, q, 16))
                    dve.tensor_tensor(
                        acc[:, bass.ds(t, 1), 0:F].rearrange("p o (h c) -> p (o h) c", h=HEADS),
                        h[:, q, :].rearrange("p (h c) -> p h c", h=HEADS),
                        w.self_weight[:, bass.ds(t, 1), :].rearrange("p o h -> p (o h)").unsqueeze(2).broadcast_to(
                            [P, HEADS, C]), ALU.mult).then_inc(used, 1)

                tiles_ahead(dve, nothing, scale)


def attention_sums(nc, k, w, rec, buckets, h_table, acc):
    RING, AHEAD, DVE_HEADS = 2, 3, 1
    with Scope(nc, "at") as s:
        pre = ByNode(nc, k, s, rec, buckets, w.maximum, HEADS)
        rows = s.sb("rows", [P, BT, F])
        below = s.sb("below", [P, BT, HEADS])
        att = s.sb("att", [P, 2, BT, HEADS + 1])
        part = [s.ps(f"part{i}", [P, 2 * F]) for i in range(RING)]
        gathered = [s.sem(f"gathered{n}") for n in range(BT)]
        granted, shifted, exped = s.sem("granted"), s.sem("shifted"), s.sem("exped")
        scaled_dve, scaled_act, summed, added = (
            s.sem(n) for n in ("scaled_dve", "scaled_act", "summed", "added"))

        with nc.Block() as block:
            @block.scalar
            def _(act):
                def scale(b, q, n):
                    act.wait_ge(exped, b + 1)
                    act.wait_ge(gathered[n], b * 16 + 16)
                    for hd in range(DVE_HEADS, HEADS):
                        head = rows[:, n, hd * C:(hd + 1) * C]
                        last = act.activation(head, head, ACT.Copy, scale=att[:, q % 2, n, hd:hd + 1])
                    last.then_inc(scaled_act, 1)

                def exponentials(b, q):
                    act.wait_ge(shifted, b + 1)
                    act.activation(att[:, q % 2, :, 0:HEADS], below[:, :, :], ACT.Exp).then_inc(exped, 1)

                def begin():
                    pre.stage_index(act, 0, 0)
                    pre.stage_index(act, 1, 1)
                    pre.act_begin(act)
                    exponentials(0, 0)
                    for n in range(AHEAD):
                        scale(0, 0, n)

                def step(g, q, n):
                    pre.act_step(act, g, q, n)
                    if n == 3:
                        exponentials(g + 1, (q + 1) % 4)
                        pre.stage_index(act, g + 2, (q + 2) % 4)
                    scale(*later(g, q, n, AHEAD))

                edge_steps(act, begin, step)

            @block.gpsimd
            def _(pool):
                def gather(b, q):
                    pool.wait_ge(pre.indexed, b + 1)
                    for n in range(BT):
                        pool.wait_ge(summed, b * BT + (n + 1 + BT))
                        pool.sem_inc(granted, 1)
                        pool.indirect_dma_start(
                            rows[:, n, :], None, h_table,
                            bass.IndirectOffsetOnAxis(pre.index[:, q, n:n + 1], 0)).then_inc(gathered[n], 16)

                gather(0, 0)
                with pool.Fori(0, TILES // BT // 4) as i:
                    for q in range(4):
                        gather(i * 4 + (q + 1), (q + 1) % 4)
                for n in range(BT):
                    pool.wait_ge(gathered[n], (TILES // BT + 1) * 16)

            @block.tensor
            def _(pe):
                def begin():
                    pe.sem_inc(summed, 2 * BT)
                    pe.sem_inc(added, RING)
                    pre.pe_begin(pe)

                def step(g, q, n):
                    pe.wait_ge(scaled_dve, g * BT + (n + 1))
                    pe.wait_ge(scaled_act, g * BT + (n + 1))
                    pe.wait_ge(added, g * BT + (n + 1))
                    pe.matmul(part[n % RING][:, 0:F], pre.hot[:, q, n, :], rows[:, n, :], start=True, stop=True)
                    pe.matmul(part[n % RING][:, F:F + HEADS + 1], pre.hot[:, q, n, :], att[:, q % 2, n, :],
                              start=True, stop=True).then_inc(summed, 1)
                    pre.pe_step(pe, g, q, n)
                    if n == 1:
                        pe.wait_ge(shifted, g + 1)
                        pre.find(pe, g + 1)

                edge_steps(pe, begin, step)

            @block.vector
            def _(dve):
                def shift(b, q, waits=True):
                    dve.wait_ge(pre.by_node, b + 1)
                    if waits:
                        dve.wait_ge(exped, b)
                    dve.tensor_copy(att[:, q % 2, :, HEADS], col(rec[:, :, R_W], b * BT, BT))
                    dve.tensor_tensor(below[:, :, :], w.logit[:, bass.ds(b * BT, BT), :], pre.p_node[:, :, :],
                                      ALU.subtract).then_inc(shifted, 1)

                def scale(b, q, n):
                    dve.wait_ge(exped, b + 1)
                    dve.wait_ge(gathered[n], b * 16 + 16)
                    heads = rows[:, n, 0:DVE_HEADS * C]
                    dve.tensor_scalar(heads, heads, att[:, q % 2, n, 0:1], None, ALU.mult).then_inc(scaled_dve, 1)

                def begin():
                    pre.dve_begin(dve)
                    shift(0, 0, waits=False)
                    for n in range(AHEAD):
                        scale(0, 0, n)

                def step(g, q, n):
                    if n == 0:
                        step.tile = bucket_registers(nc, mybir.EngineType.DVE, buckets, g * BT)
                    if n == 2:
                        shift(g + 1, (q + 1) % 4)
                    pre.dve_step(dve, g, q, n)
                    scale(*later(g, q, n, AHEAD))
                    dve.wait_ge(summed, g * BT + (n + 1 + 2 * BT))
                    dve.wait_ge(added, g * BT + (n + RING))
                    here = acc[:, bass.ds(step.tile[n], 1), 0:F + HEADS + 1]
                    dve.tensor_tensor(here, here, part[n % RING][:, 0:F + HEADS + 1].unsqueeze(1),
                                      ALU.add).then_inc(added, 1)

                edge_steps(dve, begin, step)


def batch_norm(nc, k, w, inp, acc):
    with Scope(nc, "bn") as s:
        bias, gamma = s.sb("bias", [P, F]), s.sb("gamma", [P, F])
        rden, deg, has = s.sb("rden", [P, NT, HEADS]), s.sb("deg", [P, NT]), s.sb("has", [P, NT])
        mean, std = s.sb("mean", [P, F]), s.sb("std", [P, F])
        square = s.sb("square", [P, 2, F])
        p_sum, p_var = s.ps("p_sum", [P, F]), s.ps("p_var", [P, F])
        loaded, own, ready, summed, centred = (s.sem(n) for n in ("loaded", "own", "ready", "summed", "centred"))
        squared, added, rooted, asked = s.sem("squared"), s.sem("added"), s.sem("rooted"), s.sem("asked")
        GROUP = 5
        with nc.Block() as block:
            @block.sync
            def _(sp):
                sp.dma_start(bias[:, :], inp["bias"].partition_broadcast(P)).then_inc(loaded, 16)
                sp.dma_start(gamma[:, :], inp["gamma"].partition_broadcast(P)).then_inc(loaded, 16)

            @block.tensor
            def _(pe):
                for t in range(NT):
                    pe.wait_ge(ready, t // GROUP + 1)
                    last = pe.matmul(p_sum[:, :], (k.ones if t < NT - 1 else k.last_rows)[:, :],
                                     acc[:, t, 0:F], start=(t == 0), stop=(t == NT - 1))
                last.then_inc(summed, 1)
                for t in range(NT):
                    pe.wait_ge(squared, t + 1)
                    pe.matmul(p_var[:, :], (k.ones if t < NT - 1 else k.last_rows)[:, :],
                              square[:, t % 2, :], start=(t == 0), stop=(t == NT - 1)).then_inc(added, 1)

            @block.scalar
            def _(act):
                act.wait_ge(asked, 1)
                act.activation(w.dinv[:, :], deg[:, :], ACT.Sqrt).then_inc(rooted, 1)
                for t in range(NT):
                    act.wait_ge(centred, t // GROUP + 1)
                    if t >= 2:
                        act.wait_ge(added, t - 1)
                    act.activation(square[:, t % 2, :], acc[:, t, 0:F], ACT.Square).then_inc(squared, 1)
                act.wait_ge(added, NT)
                act.activation(std[:, :], p_var[:, :], ACT.Sqrt, bias=k.eps_bn[:, :],
                               scale=1.0 / N_NODES).then_inc(rooted, 1)

            @block.vector
            def _(dve):
                c = Chain(dve, own)
                c.run(dve.tensor_scalar(rden[:, :, :], acc[:, :, DEN:DEN + HEADS], EPS_DEN, None, ALU.add))
                c.run(dve.reciprocal(rden[:, :, :], rden[:, :, :]))
                dve.wait_ge(loaded, 32)
                for g in range(0, NT, GROUP):
                    here = acc[:, g:g + GROUP, 0:F]
                    by_head = here.rearrange("p t (h c) -> p t h c", h=HEADS)
                    c.run(dve.tensor_tensor(by_head, by_head, rden[:, g:g + GROUP, :].unsqueeze(3).broadcast_to(
                        [P, GROUP, HEADS, C]), ALU.mult))
                    dve.tensor_tensor(here, here, bias[:, :].unsqueeze(1).broadcast_to([P, GROUP, F]),
                                      ALU.add).then_inc(ready, 1)
                c.run(dve.tensor_scalar(w.rdeg[:, :], acc[:, :, DEG], 1.0, None, ALU.max))
                c.run(dve.reciprocal(w.rdeg[:, :], w.rdeg[:, :]))
                c.run(dve.tensor_scalar(deg[:, :], acc[:, :, DEG], 1.0, None, ALU.add))
                dve.tensor_scalar(has[:, :], deg[:, :], 0.0, None, ALU.is_gt)
                dve.tensor_scalar(deg[:, :], deg[:, :], TINY, None, ALU.max).then_inc(asked, 1)
                dve.wait_ge(rooted, 1)
                c.run(dve.reciprocal(w.dinv[:, :], w.dinv[:, :]))
                c.run(dve.tensor_tensor(w.dinv[:, :], w.dinv[:, :], has[:, :], ALU.mult))
                dve.wait_ge(ready, NT // GROUP)
                dve.wait_ge(summed, 1)
                c.run(dve.tensor_scalar(mean[:, :], p_sum[:, :], 1.0 / N_NODES, None, ALU.mult))
                for g in range(0, NT, GROUP):
                    here = acc[:, g:g + GROUP, 0:F]
                    dve.tensor_tensor(here, here, mean[:, :].unsqueeze(1).broadcast_to([P, GROUP, F]),
                                      ALU.subtract).then_inc(centred, 1)
                dve.wait_ge(rooted, 2)
                c.run(dve.reciprocal(std[:, :], std[:, :]))
                dve.tensor_tensor(w.bn_scale[:, :], std[:, :], gamma[:, :], ALU.mult)


def gat_output(nc, k, w, inp, x0, x1, scaled, acc):
    with Scope(nc, "n1") as s:
        beta = s.sb("beta", [P, F])
        x = s.sb("x", [P, 4, F])
        y = s.sb("y", [P, 2, F])
        out = s.sb("out", [P, 2, F])
        norm = Norm(k, s)
        constant = s.sem("constant")
        loaded = [s.sem(f"loaded{q}") for q in range(4)]
        stored, saved = s.sem("stored"), s.sem("saved")
        own, asked, answered, finished = (s.sem(n) for n in ("own", "asked", "answered", "finished"))
        CHAINED = 5
        with nc.Block() as block:
            @block.sync
            def _(sp):
                sp.dma_start(beta[:, :], inp["beta"].partition_broadcast(P)).then_inc(constant, 16)
                sp.sem_inc(finished, 4)

                def load(t, q):
                    sp.wait_ge(finished, t + 1)
                    sp.dma_start(x[:, q, :], rows_of(x0, t)).then_inc(loaded[q], 16)

                tiles_ahead(sp, nothing, load)

            @block.vector
            def _(dve):
                dve.wait_ge(constant, 16)

                def tile(t, q):
                    c = Chain(dve, own, t * CHAINED)
                    here = acc[:, bass.ds(t, 1), 0:F].rearrange("p o f -> p (o f)")
                    dve.wait_ge(loaded[q], uses4(t, q, 16))
                    dve.tensor_tensor(x[:, q, :], x[:, q, :], beta[:, :], ALU.add)
                    c.run(dve.tensor_tensor(y[:, q % 2, :], here, w.bn_scale[:, :], ALU.mult))
                    c.run(dve.tensor_tensor(y[:, q % 2, :], y[:, q % 2, :], x[:, q, :], ALU.add))

                    def through_act(i, instruction):
                        instruction.then_inc(asked, 1)
                        dve.wait_ge(answered, t + 1)

                    dve.wait_ge(saved, t + 1)
                    c.run(norm.apply(dve, c, through_act, 0, y[:, q % 2, :], out[:, q % 2, :]))
                    dve.tensor_scalar(here, out[:, q % 2, :], col(w.dinv, t), None, ALU.mult).then_inc(finished, 1)
                    assert c.n == CHAINED

                tiles_ahead(dve, nothing, tile)

            @block.scalar
            def _(act):
                def root(t, q):
                    act.wait_ge(asked, t + 1)
                    norm.act_step(act, t, q).then_inc(answered, 1)

                tiles_ahead(act, nothing, root)

            @block.gpsimd
            def _(pool):
                def store(t, q):
                    pool.wait_ge(finished, t + 5)
                    pool.dma_start(rows_of(x1, t), out[:, q % 2, :]).then_inc(stored, 16)
                    pool.dma_start(rows_of(scaled, t), acc[:, bass.ds(t, 1), 0:F]).then_inc(stored, 16)
                    pool.wait_ge(stored, (t + 1) * 32)
                    pool.sem_inc(saved, 1)

                pool.sem_inc(saved, 2)
                tiles_ahead(pool, nothing, store)


def gcn_hidden(nc, k, w, inp, scaled_hid, acc):
    with Scope(nc, "n2") as s:
        s.a = s.sb("a", [P, 4, F])
        w1, b1 = s.sb("w1", [P, F // P, HID]), s.sb("b1", [P, HID])
        hid = s.sb("hid", [P, 2, HID])
        banks = [s.ps(f"bank{i}", [P, HID]) for i in range(2)]

        def prepare(dve, c, t, q):
            return dve.tensor_scalar(s.a[:, q, :].unsqueeze(1), acc[:, bass.ds(t, 1), 0:F],
                                     col(w.dinv, t), None, ALU.mult)

        def finish(dve, c, through_act, t, q):
            c.run(dve.tensor_tensor(hid[:, q % 2, :], banks[q % 2][:, :], b1[:, :], ALU.add))
            return dve.tensor_scalar(acc[:, bass.ds(t, 1), 0:HID], hid[:, q % 2, :].unsqueeze(1), 0.0,
                                     col(w.dinv, t), ALU.max, ALU.mult)

        node_pass(nc, k, s, F // P,
                  [(w1[:, :, :], inp["W1"].rearrange("(t p) n -> p t n", p=P)),
                   (b1[:, :], inp["b1"].partition_broadcast(P))],
                  [(0, HID, w1)], banks, lambda t, q: [],
                  lambda t, q: [(rows_of(scaled_hid, t), acc[:, bass.ds(t, 1), 0:HID])],
                  prepare, 0, finish, 1, [])


def gcn_output(nc, k, w, inp, x1, x2, acc):
    with Scope(nc, "n3") as s:
        s.a = s.sb("a", [P, 4, HID])
        w2, b2 = s.sb("w2", [P, HID // P, F]), s.sb("b2", [P, F])
        x = s.sb("x", [P, 4, F])
        y, out = s.sb("y", [P, 2, F]), s.sb("out", [P, 2, F])
        st, mv, ms = s.sb("st", [P, 6]), s.sb("mv", [P, 2]), s.sb("ms", [P, 1])
        length, rlen = s.sb("length", [P, 1]), s.sb("rlen", [P, 1])
        norm = Norm(k, s)
        banks = [s.ps(f"bank{i}", [P, F]) for i in range(2)]

        def prepare(dve, c, t, q):
            return dve.tensor_scalar(s.a[:, q, :].unsqueeze(1), acc[:, bass.ds(t, 1), 0:HID],
                                     col(w.dinv, t), None, ALU.mult)

        def finish(dve, c, through_act, t, q):
            here = y[:, q % 2, :]
            c.run(dve.tensor_tensor(here, banks[q % 2][:, :], b2[:, :], ALU.add))
            c.run(dve.bn_stats(st[:, :], here))
            dve.sem_inc(norm.passed, 1)
            c.run(dve.bn_aggr(mv[:, :], st[:, :]))
            through_act(0, dve.scalar_tensor_tensor(ms[:, :], mv[:, 0:1], mv[:, 0:1], mv[:, 1:2], ALU.mult, ALU.add))
            c.run(dve.tensor_scalar(length[:, :], length[:, :], EPS_NORM, None, ALU.max))
            c.run(dve.reciprocal(rlen[:, :], length[:, :]))
            c.run(dve.scalar_tensor_tensor(here, here, rlen[:, :], x[:, q, :], ALU.mult, ALU.add))
            return norm.apply(dve, c, through_act, 1, here, out[:, q % 2, :])

        def root(act, t, q):
            return act.activation(length[:, :], ms[:, :], ACT.Sqrt, scale=float(F))

        node_pass(nc, k, s, HID // P,
                  [(w2[:, :, :], inp["W2"].rearrange("(t p) n -> p t n", p=P)),
                   (b2[:, :], inp["b2"].partition_broadcast(P))],
                  [(0, F, w2)], banks, lambda t, q: [(x[:, q, :], rows_of(x1, t))],
                  lambda t, q: [(rows_of(x2, t), out[:, q % 2, :])],
                  prepare, 0, finish, 8, [root, norm.act_step])


def sage_output(nc, k, w, inp, x2, x3, acc):
    with Scope(nc, "n4") as s:
        s.a = s.sb("a", [P, 4, 2 * F])
        wt = s.sb("wt", [P, 2 * F // P, F])
        b = s.sb("b", [P, 2, F])
        x = s.sb("x", [P, 4, F])
        y, out = s.sb("y", [P, 2, F]), s.sb("out", [P, 2, F])
        norm = Norm(k, s)
        banks = [s.ps(f"bank{i}", [P, F]) for i in range(2)]

        def prepare(dve, c, t, q):
            dve.tensor_copy(s.a[:, q, 0:F], x[:, q, :])
            return dve.tensor_scalar(s.a[:, q, F:2 * F].unsqueeze(1), acc[:, bass.ds(t, 1), 0:F],
                                     col(w.rdeg, t), None, ALU.mult)

        def finish(dve, c, through_act, t, q):
            here = y[:, q % 2, :]
            c.run(dve.tensor_tensor(here, banks[q % 2][:, :], b[:, 0, :], ALU.add))
            c.run(dve.tensor_tensor(here, here, b[:, 1, :], ALU.add))
            c.run(dve.tensor_tensor(here, here, x[:, q, :], ALU.add))
            return norm.apply(dve, c, through_act, 0, here, out[:, q % 2, :])

        node_pass(nc, k, s, 2 * F // P,
                  [(wt[:, 0:F // P, :], inp["W_self_t"].rearrange("(t p) n -> p t n", p=P)),
                   (wt[:, F // P:2 * F // P, :], inp["W_neigh_t"].rearrange("(t p) n -> p t n", p=P)),
                   (b[:, 0, :], inp["b_self"].partition_broadcast(P)),
                   (b[:, 1, :], inp["b_neigh"].partition_broadcast(P))],
                  [(0, F, wt)], banks, lambda t, q: [(x[:, q, :], rows_of(x2, t))],
                  lambda t, q: [(rows_of(x3, t), out[:, q % 2, :])],
                  prepare, 0, finish, 5, [norm.act_step])


def conv_output(nc, k, w, inp, x3, result, acc):
    with Scope(nc, "n5") as s:
        s.a = s.sb("a", [P, 4, F])
        w3, b3 = s.sb("w3", [P, F // P, F]), s.sb("b3", [P, F])
        x = s.sb("x", [P, 4, F])
        y, out = s.sb("y", [P, 2, F]), s.sb("out", [P, 2, F])
        norm = Norm(k, s)
        banks = [s.ps(f"bank{i}", [P, F]) for i in range(2)]

        def prepare(dve, c, t, q):
            return dve.tensor_copy(s.a[:, q, :].unsqueeze(1), acc[:, bass.ds(t, 1), 0:F])

        def finish(dve, c, through_act, t, q):
            here = y[:, q % 2, :]
            c.run(dve.tensor_tensor(here, banks[q % 2][:, :], b3[:, :], ALU.add))
            c.run(dve.tensor_tensor(here, here, x[:, q, :], ALU.add))
            return norm.apply(dve, c, through_act, 0, here, out[:, q % 2, :])

        def store(t, q):
            rows = P if not isinstance(t, int) or t < NT - 1 else LAST_ROWS
            return [(result[bass.ds(t * P, rows), :], out[0:rows, q % 2, :])]

        node_pass(nc, k, s, F // P,
                  [(w3[:, :, :], inp["W3"].rearrange("(t p) n -> p t n", p=P)),
                   (b3[:, :], inp["b3"].partition_broadcast(P))],
                  [(0, F, w3)], banks, lambda t, q: [(x[:, q, :], rows_of(x3, t))], store,
                  prepare, 0, finish, 4, [norm.act_step])


def build(nc, inp, result):
    class Held:
        pass

    def dram(name, shape):
        return nc.dram_tensor(name, shape, FP).ap()

    by_dst, by_src = dram("edges_by_dst", [P * TC, REC]), dram("edges_by_src", [P * TC, REC])
    h_table, src_table = dram("h_table", [NODES_PAD, F]), dram("src_table", [NODES_PAD, HEADS])
    scaled, scaled_hid = dram("x1_scaled", [NODES_PAD, F]), dram("hidden_scaled", [NODES_PAD, HID])
    x0 = inp["x"]
    x1, x2, x3 = (dram(n, [NODES_PAD, F]) for n in ("x1", "x2", "x3"))

    with Scope(nc, "k") as held:
        k, w = Held(), Held()
        k.ident, k.before = held.sb("ident", [P, P]), held.sb("before", [P, P])
        k.ones, k.last_rows = held.sb("ones", [P, P]), held.sb("last_rows", [P, P])
        k.columns, k.pad_slot = held.sb("columns", [P, TILES_PAD]), held.sb("pad_slot", [P, EC])
        k.eps_ln, k.eps_bn = held.sb("eps_ln", [P, 1]), held.sb("eps_bn", [P, 1])
        w.w_ext = held.sb("w_ext", [P, F // P, 2 * HEADS])
        w.v_edge, w.mean_logit = held.sb("v_edge", [P, 4, HEADS]), held.sb("mean_logit", [P, HEADS])
        w.node_logit = held.sb("node_logit", [P, NT * 2 * HEADS])
        w.dst_own = held.sb("dst_own", [P, NT, 2 * HEADS])
        w.above, w.maximum = held.sb("above", [P, NT, HEADS]), held.sb("maximum", [P, NT, HEADS])
        w.self_weight = held.sb("self_weight", [P, NT, HEADS])
        w.bn_scale = held.sb("bn_scale", [P, F])
        w.dinv, w.rdeg = held.sb("dinv", [P, NT]), held.sb("rdeg", [P, NT])
        dst_tiles, src_tiles = (held.sb(n, [P, TILES_PAD], I32) for n in ("dst_tiles", "src_tiles"))

        constants(nc, k)
        with Scope(nc, "sort") as srt:
            w.records = srt.sb("records", [P, EC, REC])
            slots = srt.sb("slots", [P, EC], I32)
            blank = srt.sb("blank", [P, TC * REC])
            setup(nc, k, inp, w, blank)
            for name, key, other, table, tiles in (("pd", "dst", "src", by_dst, dst_tiles),
                                                   ("ps", "src", "dst", by_src, src_tiles)):
                place(nc, k, name, inp[key], slots, tiles, w.records, inp[other])
                scatter_records(nc, name + "s", w.records, slots, table, blank)

        gat_projection(nc, k, w, inp, x0, h_table, src_table)
        rec = held.sb("rec", [P, TILES_PAD, REC])
        acc = held.sb("acc", [P, NT, ACCW])
        load_records(nc, "ld", by_dst, rec)
        with Scope(nc, "gat") as gat:
            w.attr_logit = gat.sb("attr_logit", [P, TILES_PAD, HEADS])
            w.logit = gat.sb("logit", [P, TILES_PAD, HEADS])
            edge_logits(nc, k, w, rec)
            attention_maxima(nc, k, w, rec, dst_tiles, src_table)
            self_loops(nc, k, w, h_table, acc)
            attention_sums(nc, k, w, rec, dst_tiles, h_table, acc)
        batch_norm(nc, k, w, inp, acc)
        gat_output(nc, k, w, inp, x0, x1, scaled, acc)
        aggregate(nc, k, "g1", rec, dst_tiles, scaled, F, acc, clear=False)
        gcn_hidden(nc, k, w, inp, scaled_hid, acc)
        aggregate(nc, k, "g2", rec, dst_tiles, scaled_hid, HID, acc, clear=False)
        gcn_output(nc, k, w, inp, x1, x2, acc)
        aggregate(nc, k, "g3", rec, dst_tiles, x2, F, acc, clear=True)
        sage_output(nc, k, w, inp, x2, x3, acc)
        load_records(nc, "ld2", by_src, rec)
        aggregate(nc, k, "g4", rec, src_tiles, x3, F, acc, clear=True)
        conv_output(nc, k, w, inp, x3, result, acc)


def kernel(x, src, dst, edge_attr_4, edge_weight, L0_gnn_W, L0_gnn_W_edge, L0_gnn_att_src, L0_gnn_att_dst,
           L0_gnn_att_edge, L0_gnn_bias, L0_gnn_gamma, L0_gnn_beta, L1_gnn_W1, L1_gnn_b1, L1_gnn_W2, L1_gnn_b2,
           L2_gnn_W_self, L2_gnn_b_self, L2_gnn_W_neigh, L2_gnn_b_neigh, L3_gnn_weight, L3_gnn_bias):
    import numpy as np
    import concourse.bacc as bacc
    from concourse.bass_utils import run_bass_kernel_spmd

    arrays = laid_out(np, locals())
    nc = bacc.Bacc("TRN2", target_bir_lowering=False, num_devices=1)
    inp = {name: nc.dram_tensor("in_" + name, a.shape, mybir.dt.from_np(a.dtype), kind="ExternalInput").ap()
           for name, a in arrays.items()}
    result = nc.dram_tensor("out_x", (N_NODES, F), FP, kind="ExternalOutput").ap()
    build(nc, inp, result)
    r = run_bass_kernel_spmd(nc, [{"in_" + name: a for name, a in arrays.items()}], core_ids=[0])
    return r.results[0]["out_x"]


def laid_out(np, a):
    x = np.zeros((NODES_PAD, F), np.float32)
    x[:N_NODES] = np.asarray(a["x"])
    edges = np.zeros((EDGES_PAD, REC), np.float32)
    edges[:N_EDGES, R_W] = np.asarray(a["edge_weight"])
    edges[:N_EDGES, R_EA:R_EA + 4] = np.asarray(a["edge_attr_4"])

    def padded(index):
        out = np.full(EDGES_PAD, NODES_PAD, np.int32)
        out[:N_EDGES] = np.asarray(index)
        return out.reshape(P, EC)

    def flat(name):
        return np.ascontiguousarray(np.asarray(a[name])).reshape(-1)

    def rows(name):
        return np.ascontiguousarray(np.asarray(a[name]))

    def turned(name):
        return np.ascontiguousarray(np.asarray(a[name]).T)

    return {
        "x": x, "edges": edges.reshape(P, EC * REC), "src": padded(a["src"]), "dst": padded(a["dst"]),
        "W0": rows("L0_gnn_W"), "W_edge": flat("L0_gnn_W_edge"), "att_src": flat("L0_gnn_att_src"),
        "att_dst": flat("L0_gnn_att_dst"), "att_edge": flat("L0_gnn_att_edge"), "bias": flat("L0_gnn_bias"),
        "gamma": flat("L0_gnn_gamma"), "beta": flat("L0_gnn_beta"), "W1": rows("L1_gnn_W1"),
        "b1": flat("L1_gnn_b1"), "W2": rows("L1_gnn_W2"), "b2": flat("L1_gnn_b2"),
        "W_self_t": turned("L2_gnn_W_self"), "b_self": flat("L2_gnn_b_self"),
        "W_neigh_t": turned("L2_gnn_W_neigh"), "b_neigh": flat("L2_gnn_b_neigh"),
        "W3": rows("L3_gnn_weight"), "b3": flat("L3_gnn_bias"),
    }
```

```python
from contextlib import ExitStack

import concourse.bass as bass
from concourse import mybir

FP = mybir.dt.float32
I32 = mybir.dt.int32
BF = mybir.dt.bfloat16
ALU = mybir.AluOpType
ACT = mybir.ActivationFunctionType
AX = mybir.AxisListType

P = 128
N_NODES, F, HEADS, N_EDGES, HID = 3125, 512, 4, 50000, 256
C = F // HEADS
NT = -(-N_NODES // P)
NODES_PAD = NT * P
LAST_ROWS = N_NODES - (NT - 1) * P
BT = 8
EC = -(-N_EDGES // (P * NT * BT)) * NT * BT
EDGES_PAD = P * EC
TILES_USED = (N_EDGES + NT * (P - 1)) // P
TILES = -(-TILES_USED // (4 * BT)) * 4 * BT
TILES_PAD = TILES + 3 * BT
TC = TILES_PAD + -(-(EDGES_PAD - N_EDGES) // P)
REC, REC_SRC = 8, 4
R_LOCAL, R_OTHER, R_W, R_EA = 0, 1, 2, 4
NEG_SLOPE, EPS_BN, EPS_LN, EPS_DEN, EPS_NORM = 0.2, 1e-5, 1e-5, 1e-16, 1e-12
MASKED = -1e30
ACCW = F + BT
DEN, DEG = F, F + HEADS
TINY = 1e-30


class Chain:

    def __init__(self, eng, sem, base=0):
        self.eng, self.sem, self.base, self.n = eng, sem, base, 0

    def run(self, instruction):
        instruction.then_inc(self.sem, 1)
        self.n += 1
        self.eng.wait_ge(self.sem, self.base + self.n)


def in_turn(eng, *stages, peel=0):
    leads = [lead for _, lead in stages]
    start, stop = max(peel, -min(leads)), NT - max(0, max(leads))
    steps = (stop - start) // 4 * 4

    def straight(first, last):
        for u in range(first, last):
            for do, lead in stages:
                if 0 <= u + lead < NT:
                    do(u + lead, (u + lead) % 4)

    straight(-max(0, max(leads)), start)
    with eng.Fori(0, steps // 4) as i:
        for r in range(start, start + 4):
            for do, lead in stages:
                do(i * 4 + (r + lead), (r + lead) % 4)
    straight(start + steps, NT + start)


def edge_steps(eng, begin, step):
    begin()
    with eng.Fori(0, TILES // BT // 4) as i:
        for q in range(4):
            for n in range(BT):
                step(i * 4 + q, q, n)


def later(g, q, n, by):
    return g + (n + by) // BT, (q + (n + by) // BT) % 4, (n + by) % BT


def uses4(t, q, each):
    return (t - q) * (each // 4) + each


def col(ap, j, n=1):
    return ap[:, bass.ds(j, n)]


def bucket_registers(nc, engine, buckets, j):
    _, values = nc.values_load_multi_w_load_instructions(
        buckets[0:1, bass.ds(j, BT)], engines=[engine], min_val=0, max_val=NT - 1,
        skip_runtime_bounds_check_because="the node tile numbers are clamped")
    return values


class Scope:

    def __init__(self, nc, name):
        self.nc, self.name, self.ctx, self.sems = nc, name, ExitStack(), []

    def __enter__(self):
        return self

    def __exit__(self, *exc):
        if self.sems and exc[0] is None:
            self.nc.clear_and_free_semaphores(self.sems)
            self.nc.all_engine_barrier(sem_only=True)
        self.ctx.close()

    def sb(self, name, shape, dt=FP):
        return self.ctx.enter_context(self.nc.sbuf_tensor(f"{self.name}_{name}", shape, dt))

    def ps(self, name, shape):
        return self.ctx.enter_context(self.nc.psum_tensor(f"{self.name}_{name}", shape, FP))

    def sem(self, name):
        self.sems.append(self.nc.alloc_semaphore(f"{self.name}_{name}"))
        return self.sems[-1]


def constants(nc, k, blank):
    with Scope(nc, "cst") as s:
        ii = s.sb("ii", [P, P], I32)
        ic = s.sb("ic", [P, TILES_PAD], I32)
        ie = s.sb("ie", [P, EC], I32)
        pf = s.sb("pf", [P, P])
        ef = s.sb("ef", [P, EC])
        made = s.sem("made")
        own = s.sem("own")
        with nc.Block() as block:
            @block.gpsimd
            def _(pool):
                pool.iota(ii[:, :], [[0, P]], base=0, channel_multiplier=1).then_inc(made, 1)
                pool.iota(ic[:, :], [[1, TILES_PAD]], base=0, channel_multiplier=0).then_inc(made, 1)
                pool.iota(ie[:, :], [[1, EC]], base=0, channel_multiplier=EC).then_inc(made, 1)

            @block.vector
            def _(dve):
                own_chain = Chain(dve, own)
                own_chain.run(dve.memset(blank[:, :], 0.0))
                dve.memset(blank[:, :].rearrange("p (t f) -> p t f", f=REC)[:, :, R_LOCAL], -1.0)
                dve.wait_ge(made, 3)
                dve.tensor_copy(pf[:, :], ii[:, :])
                dve.tensor_copy(ef[:, :], ie[:, :])
                own_chain.run(dve.tensor_copy(k.columns[:, :], ic[:, :]))
                dve.tensor_tensor(k.ident[:, :], k.columns[:, 0:P], pf[:, :], ALU.is_equal)
                dve.tensor_tensor(k.before[:, :], k.columns[:, 0:P], pf[:, :], ALU.is_gt)
                dve.memset(k.ones[:, :], 1.0)
                dve.tensor_scalar(k.last_rows[:, :], pf[:, :], float(LAST_ROWS), None, ALU.is_lt)
                own_chain.run(dve.tensor_scalar(k.pad_slot[:, :], ef[:, :], float(N_EDGES), None, ALU.is_ge))
                own_chain.run(dve.tensor_scalar(ef[:, :], ef[:, :], float(TILES_PAD * P - N_EDGES), None, ALU.add))
                dve.tensor_tensor(k.pad_slot[:, :], k.pad_slot[:, :], ef[:, :], ALU.mult)
    return


def place(nc, k, name, key_dram, slots, buckets, records, other_dram, fill, weighted, loads,
          background=None):
    with Scope(nc, name) as s:
        key, other = s.sb("key", [P, EC], I32), s.sb("other", [P, EC], I32)
        key_i, key_f, low_f = s.sb("key_i", [P, EC], I32), s.sb("key_f", [P, EC]), s.sb("low_f", [P, EC])
        ohot = s.sb("ohot", [P, NT, EC], BF)
        seen = s.sb("seen", [P, TILES_PAD * NT])
        ends, cnt = s.sb("ends", [P, NT + 1]), s.sb("cnt", [P, NT])
        tiles_i, tiles_f = s.sb("tiles_i", [P, NT], I32), s.sb("tiles_f", [P, NT])
        last, start, off = s.sb("last", [P, NT]), s.sb("start", [P, NT]), s.sb("off", [P, NT])
        tile_f = s.sb("tile_f", [P, TILES_PAD])
        p_cnt = s.ps("p_cnt", [P, 2 * NT])
        loaded, own, counted, summed = s.sem("loaded"), s.sem("own"), s.sem("counted"), s.sem("summed")
        moved, filled, s.placed = s.sem("moved"), s.sem("filled"), s.sem("placed")
        with nc.Block() as block:
            @block.sync
            def _(sp):
                sp.dma_start(key[:, :], key_dram).then_inc(loaded, 16)
                sp.dma_start(other[:, :], other_dram).then_inc(loaded, 16)
                if fill is not None:
                    sp.dma_start(*fill).then_inc(filled, 16)
                for to, of in loads:
                    sp.dma_start(to, of).then_inc(moved, 16)
                if loads:
                    sp.wait_ge(moved, 16 * len(loads))
                    sp.sem_inc(s.placed, 1)

            if background is not None:
                block.gpsimd(background(s))

            @block.tensor
            def _(pe):
                pe.wait_ge(counted, 1)
                pe.matmul(p_cnt[:, 0:NT], k.before[:, :], cnt[:, :], start=True, stop=True)
                pe.matmul(p_cnt[:, NT:2 * NT], k.ones[:, :], cnt[:, :], start=True, stop=True).then_inc(summed, 1)

            @block.vector
            def _(dve):
                c = Chain(dve, own)
                dve.wait_ge(loaded, 32)
                c.run(dve.tensor_scalar(key_i[:, :], key[:, :], 7, None, ALU.arith_shift_right))
                c.run(dve.tensor_copy(key_f[:, :], key_i[:, :]))
                c.run(dve.tensor_scalar(key_i[:, :], key[:, :], P - 1, None, ALU.bitwise_and))
                c.run(dve.tensor_tensor(
                    ohot[:, :, :], key_f[:, :].unsqueeze(1).broadcast_to([P, NT, EC]),
                    k.columns[:, 0:NT].unsqueeze(2).broadcast_to([P, NT, EC]), ALU.is_equal))
                flat = ohot[:, :, :].rearrange("p b c -> p (b c)")
                c.run(dve.tensor_tensor_scan(seen[:, 0:NT * EC], flat, flat, 0.0, ALU.add, ALU.max))
                if fill is None:
                    dve.tensor_copy(records[:, :, R_W:REC_SRC], weighted[:, :, R_W:REC_SRC])
                else:
                    dve.wait_ge(filled, 16)
                dve.tensor_copy(records[:, :, R_OTHER].bitcast(I32), other[:, :])
                dve.tensor_copy(records[:, :, R_LOCAL], key_i[:, :])
                seen_bc = seen[:, 0:NT * EC].rearrange("p (b c) -> p b c", b=NT)
                dve.memset(ends[:, 0:1], 0.0)
                c.run(dve.tensor_copy(ends[:, 1:NT + 1], seen_bc[:, :, EC - 1]))
                dve.tensor_tensor(cnt[:, :], ends[:, 1:NT + 1], ends[:, 0:NT], ALU.subtract).then_inc(counted, 1)
                dve.wait_ge(summed, 1)
                c.run(dve.tensor_scalar(tiles_i[:, :], p_cnt[:, NT:2 * NT], float(P - 1), None, ALU.add))
                c.run(dve.tensor_scalar(tiles_i[:, :], tiles_i[:, :], 7, None, ALU.arith_shift_right))
                c.run(dve.tensor_copy(tiles_f[:, :], tiles_i[:, :]))
                c.run(dve.tensor_tensor_scan(last[:, :], tiles_f[:, :], tiles_f[:, :], 0.0, ALU.add, ALU.max))
                c.run(dve.tensor_tensor(start[:, :], last[:, :], tiles_f[:, :], ALU.subtract))
                c.run(dve.scalar_tensor_tensor(off[:, :], start[:, :], float(P), p_cnt[:, 0:NT], ALU.mult, ALU.add))
                c.run(dve.scalar_tensor_tensor(off[:, :], off[:, :], -1.0, ends[:, 0:NT], ALU.add, ALU.subtract))
                c.run(dve.tensor_tensor(seen_bc, seen_bc, off[:, :].unsqueeze(2).broadcast_to([P, NT, EC]), ALU.add))
                c.run(dve.tensor_tensor(seen_bc, seen_bc, ohot[:, :, :], ALU.mult))
                c.run(dve.tensor_reduce(key_f[:, :], seen_bc.rearrange("p b c -> p c b"), AX.X, ALU.add))
                c.run(dve.tensor_tensor(key_f[:, :], key_f[:, :], k.pad_slot[:, :], ALU.add))
                c.run(dve.tensor_copy(slots[:, :], key_f[:, :]))
                c.run(dve.tensor_scalar(key_i[:, :], slots[:, :], 7, None, ALU.arith_shift_right))
                c.run(dve.tensor_copy(key_f[:, :], key_i[:, :]))
                c.run(dve.tensor_scalar(slots[:, :], slots[:, :], P - 1, None, ALU.bitwise_and))
                c.run(dve.tensor_copy(low_f[:, :], slots[:, :]))
                c.run(dve.scalar_tensor_tensor(slots[:, :], low_f[:, :], float(TC), key_f[:, :], ALU.mult, ALU.add))
                dve.sem_inc(s.placed, 1)
                ended = seen[:, 0:TILES_PAD * NT].rearrange("p (j b) -> p j b", b=NT)
                c.run(dve.tensor_tensor(
                    ended, last[:, :].unsqueeze(1).broadcast_to([P, TILES_PAD, NT]),
                    k.columns[:, :].unsqueeze(2).broadcast_to([P, TILES_PAD, NT]), ALU.is_le))
                c.run(dve.tensor_reduce(tile_f[:, :], ended, AX.X, ALU.add))
                c.run(dve.tensor_scalar(buckets[:, :], tile_f[:, :], float(NT - 1), None, ALU.min))


class Scatter:

    def __init__(self, nc, s, each, records, slots, table, words):
        self.each, self.records, self.slots, self.table = each, records, slots, table
        self.rec = s.sb("sc_rec", [P, 2, each, words])
        self.row = s.sb("sc_row", [P, 2, each], I32)
        self.written = [s.sem(f"sc_written{h}") for h in range(2)]
        self.staged, self.issued = s.sem("sc_staged"), s.sem("sc_issued")

    def step(self, pool, g, h, column):
        if not isinstance(g, int) or g >= 2:
            pool.wait_ge(self.written[h], (g - h) * (self.each * 8))
        pool.tensor_copy(self.row[:, h, :], col(self.slots, column, self.each))
        pool.tensor_copy(self.rec[:, h, :, :], col(self.records, column, self.each)).then_inc(self.staged, 1)
        pool.wait_ge(self.staged, g + 1)
        pool.sem_inc(self.issued, 1)
        for n in range(self.each):
            pool.indirect_dma_start(
                self.table, bass.IndirectOffsetOnAxis(self.row[:, h, n:n + 1], 0),
                self.rec[:, h, n, :], None).then_inc(self.written[h], 16)

    def end(self, pool, steps):
        for h in range(2):
            pool.wait_ge(self.written[h], (steps + 1 - h) // 2 * self.each * 16)


def scatter_steps(nc, s, first, steps, *where):
    def program(pool):
        scatter = Scatter(nc, s, BT, *where)
        if first == 0:
            pool.wait_ge(s.placed, 2)
        for g in range(2):
            scatter.step(pool, g, g, (first + g) * BT)
        if steps > 2:
            with pool.Fori(1, steps // 2) as i:
                for h in range(2):
                    scatter.step(pool, i * 2 + h, h, i * 2 * BT + (first + h) * BT)
        scatter.end(pool, steps)
    return program


def scatter_by_tile(nc, s, first, each, *where):
    def program(pool):
        scatter = Scatter(nc, s, each, *where)
        in_turn(pool, (lambda t, q: scatter.step(pool, t, q % 2, t * each + first), 0), peel=2)
        scatter.end(pool, NT)
    return program


def scatter_by_batch(nc, s, pool, gather, first, *where):
    scatter = Scatter(nc, s, 1, *where)
    steps = 2 * NT

    def step(g, q):
        gather(g, q)
        if not isinstance(g, int) or g < steps:
            scatter.step(pool, g, q % 2, g + first)

    for g in range(4):
        step(g, g)
    with pool.Fori(1, steps // 4) as i:
        for q in range(4):
            step(i * 4 + q, q)
    for g in range(steps // 4 * 4, TILES // BT):
        step(g, g % 4)
    scatter.end(pool, steps)


def load_records(nc, name, table, rec, words):
    with Scope(nc, name) as s:
        loaded = s.sem("loaded")
        with nc.Block() as block:
            @block.sync
            def _(sp):
                sp.dma_start(rec[:, :, :].rearrange("p t f -> p (t f)"),
                             table.rearrange("(l t) f -> l (t f)", l=P)[:, 0:TILES_PAD * words]).then_inc(loaded, 16)
                sp.wait_ge(loaded, 16)


def aggregate(nc, k, name, rec, buckets, table, width, acc, clear, fetch=()):
    RING, AHEAD = 4, 2
    with Scope(nc, name) as s:
        rows = s.sb("rows", [P, BT, width])
        index = s.sb("index", [P, 2, BT], I32)
        hot = s.sb("hot", [P, RING, P])
        part = [s.ps(f"part{i}", [P, F]) for i in range(RING)]
        gathered = [s.sem(f"gathered{n}") for n in range(BT)]
        indexed, granted, hot_ready = s.sem("indexed"), s.sem("granted"), s.sem("hot_ready")
        summed, added, cleared = s.sem("summed"), s.sem("added"), s.sem("cleared")
        other = rec[:, :, R_OTHER].bitcast(I32)
        fetched = s.sem("fetched")
        with nc.Block() as block:
            @block.sync
            def _(sp):
                for to, of in fetch:
                    sp.dma_start(to, of).then_inc(fetched, 16)
                if fetch:
                    sp.wait_ge(fetched, 16 * len(fetch))

            @block.scalar
            def _(act):
                with act.Fori(0, TILES // BT // 2) as i:
                    g = i * 2
                    for h in range(2):
                        act.wait_ge(summed, g * BT + BT * (h + 1))
                        act.copy(index[:, h, :], col(other, g * BT + BT * h, BT)).then_inc(indexed, 1)

            @block.gpsimd
            def _(pool):
                with pool.Fori(0, TILES // BT // 2) as i:
                    g = i * 2
                    for h in range(2):
                        pool.wait_ge(indexed, g + (h + 1))
                        for n in range(BT):
                            pool.wait_ge(summed, g * BT + (h * BT + n + 1 + BT))
                            pool.sem_inc(granted, 1)
                            pool.indirect_dma_start(
                                rows[:, n, :], None, table,
                                bass.IndirectOffsetOnAxis(index[:, h, n:n + 1], 0)).then_inc(gathered[n], 16)

            @block.vector
            def _(dve):
                def weigh(j, n):
                    dve.tensor_scalar(hot[:, n % RING, :], k.columns[:, 0:P], col(rec[:, :, R_LOCAL], j),
                                      col(rec[:, :, R_W], j), ALU.is_equal, ALU.mult).then_inc(hot_ready, 1)

                if clear:
                    dve.memset(acc[:, :, 0:width], 0.0).then_inc(cleared, 1)
                    dve.wait_ge(cleared, 1)
                for n in range(AHEAD):
                    weigh(n, n)
                with dve.Fori(0, TILES // BT // 2) as i:
                    g = i * 2
                    for h in range(2):
                        tile = bucket_registers(nc, mybir.EngineType.DVE, buckets, g * BT + h * BT)
                        for n in range(BT):
                            u = h * BT + n
                            dve.wait_ge(summed, g * BT + (u + AHEAD - RING + 2 * BT + 1))
                            weigh(g * BT + (u + AHEAD), u + AHEAD)
                            dve.wait_ge(summed, g * BT + (u + 2 * BT + 1))
                            dve.wait_ge(added, g * BT + (u + RING))
                            here = acc[:, bass.ds(tile[n], 1), 0:width]
                            dve.tensor_tensor(here, here, part[n % RING][:, 0:width].unsqueeze(1),
                                              ALU.add).then_inc(added, 1)

            @block.tensor
            def _(pe):
                pe.sem_inc(summed, 2 * BT)
                pe.sem_inc(added, RING)
                with pe.Fori(0, TILES // BT // 2) as i:
                    g = i * 2
                    for u in range(2 * BT):
                        pe.wait_ge(hot_ready, g * BT + (u + 1))
                        pe.wait_ge(gathered[u % BT], g * 16 + (u // BT + 1) * 16)
                        pe.wait_ge(added, g * BT + (u + 1))
                        pe.matmul(part[u % RING][:, 0:width], hot[:, u % RING, :], rows[:, u % BT, :],
                                  start=True, stop=True).then_inc(summed, 1)


def setup(nc, k, inp, w, background):
    with Scope(nc, "set") as s:
        w0 = s.sb("w0", [P, F // P, F])
        att = s.sb("att", [P, 3, F])
        w_edge = s.sb("w_edge", [P, 4, F])
        prod = s.sb("prod", [P, F // P, F])
        ea_sum, mean_ea = s.sb("ea_sum", [P, 4]), s.sb("mean_ea", [P, 4])
        tmp = s.sb("tmp", [P, HEADS, 4])
        p_ea = s.ps("p_ea", [P, 4])
        loaded, own, counted, summed = s.sem("loaded"), s.sem("own"), s.sem("counted"), s.sem("summed")
        with nc.Block() as block:
            @block.sync
            def _(sp):
                sp.dma_start(w0[:, :, :], inp["W0"].rearrange("(t p) n -> p t n", p=P)).then_inc(loaded, 16)
                for i, n in enumerate(("att_src", "att_dst", "att_edge")):
                    sp.dma_start(att[:, i, :], inp[n].partition_broadcast(P)).then_inc(loaded, 16)
                sp.dma_start(w_edge[:, :, :].rearrange("p a n -> p (a n)"),
                             inp["W_edge"].partition_broadcast(P)).then_inc(loaded, 16)

            block.gpsimd(background(s))

            @block.tensor
            def _(pe):
                pe.wait_ge(counted, 1)
                pe.matmul(p_ea[:, :], k.ones[:, :], ea_sum[:, :], start=True, stop=True).then_inc(summed, 1)

            @block.vector
            def _(dve):
                c = Chain(dve, own)
                dve.memset(k.eps_ln[:, :], EPS_LN)
                dve.memset(k.eps_bn[:, :], EPS_BN)
                dve.wait_ge(loaded, 80)
                dve.tensor_reduce(ea_sum[:, :], w.records[:, :, R_EA:R_EA + 4].rearrange("p c f -> p f c"),
                                  AX.X, ALU.add).then_inc(counted, 1)
                for i in range(2):
                    c.run(dve.tensor_tensor(prod[:, :, :], w0[:, :, :], att[:, i, :].unsqueeze(1).broadcast_to(
                        [P, F // P, F]), ALU.mult))
                    c.run(dve.tensor_reduce(
                        w.w_ext[:, :, i * HEADS:(i + 1) * HEADS],
                        prod[:, :, :].rearrange("p t (h c) -> p t h c", h=HEADS), AX.X, ALU.add))
                c.run(dve.tensor_tensor(prod[:, :, :], w_edge[:, :, :], att[:, 2, :].unsqueeze(1).broadcast_to(
                    [P, 4, F]), ALU.mult))
                c.run(dve.tensor_reduce(w.v_edge[:, :, :], prod[:, :, :].rearrange(
                    "p a (h c) -> p a h c", h=HEADS), AX.X, ALU.add))
                dve.wait_ge(summed, 1)
                c.run(dve.tensor_scalar(mean_ea[:, :], p_ea[:, :], 1.0 / N_EDGES, None, ALU.mult))
                c.run(dve.tensor_tensor(tmp[:, :, :], w.v_edge[:, :, :].rearrange("p a h -> p h a"),
                                        mean_ea[:, :].unsqueeze(1).broadcast_to([P, HEADS, 4]), ALU.mult))
                c.run(dve.tensor_reduce(w.mean_logit[:, :], tmp[:, :, :], AX.X, ALU.add))


def node_pass(nc, k, s, kt, constants, weights, banks, loads, read_in, stores, operand, prepare,
              finish, roots=(), polish=None, background=None, follow_up=None):
    s.a_t = s.sb("a_t", [P, 2, kt * P])
    p_t = [s.ps(f"p_t{i}", [P, kt * P]) for i in range(2)]
    constant = s.sem("constant")
    loaded = [s.sem(f"loaded{q}") for q in range(4)]
    stored = [s.sem(f"stored{q}") for q in range(4)]
    prepared, turned, copied, multiplied = (s.sem(n) for n in ("prepared", "turned", "copied", "multiplied"))
    finished = s.sem("finished")
    parts = range(len(finish))
    done = [finished if polish is None else s.sem(f"done{i}") for i in parts]
    own, rooted = [s.sem(f"own{i}") for i in parts], [s.sem(f"rooted{i}") for i in parts]
    n_loads, n_stores = len(loads(0, 0)), len(stores(0, 0))
    lag = len(finish) if roots else 0
    extra = None
    if follow_up is not None:
        weight, output, take = follow_up
        extra = FollowUp(k, s, F, weight, output, finished, 4)

    def output_free(eng, t, q):
        eng.wait_ge(stored[q], uses4(t, q, 16 * n_stores))

    with nc.Block() as block:
        @block.sync
        def _(sp):
            for to, of in constants:
                sp.dma_start(to, of).then_inc(constant, 16)
            for q in range(4):
                sp.sem_inc(stored[q], 16 * n_stores)

            def load(t, q):
                sp.wait_ge(done[read_in], t + 1)
                for to, of in loads(t, q):
                    sp.dma_start(to, of).then_inc(loaded[q], 16)

            def store(t, q):
                sp.wait_ge(finished, t + 5)
                for to, of in stores(t, q):
                    sp.dma_start(to, of).then_inc(stored[q], 16)

            in_turn(sp, *([(load, 4)] if n_loads else []), (store, -lag))
            for q in range(4):
                sp.wait_ge(stored[q], (1 + (NT + 3 - q) // 4) * 16 * n_stores)

        if background is not None:
            block.gpsimd(background)

        @block.vector
        def _(dve):
            if constants:
                dve.wait_ge(constant, 16 * len(constants))

            def part(i):
                def run(t, q):
                    if i == 0:
                        dve.wait_ge(multiplied, t + 3)
                        dve.wait_ge(finished, t + 1)
                    else:
                        dve.wait_ge(rooted[i - 1], t + 1)
                    if i == read_in and n_loads:
                        dve.wait_ge(loaded[q], uses4(t, q, 16 * n_loads))
                    if polish is None:
                        output_free(dve, t, q)
                    c = Chain(dve, own[i], t * finish[i][1])
                    finish[i][0](dve, c, t, q).then_inc(done[i], 1)
                    assert c.n == finish[i][1]
                return run

            def use(t, q):
                take(dve, t, q, extra.product(dve, t, q)).then_inc(extra.used, 1)

            in_turn(dve, *((part(i), -i) for i in parts), *([(use, -lag - 2)] if extra else []))

        @block.tensor
        def _(pe):
            pe.sem_inc(turned, 4)
            pe.sem_inc(copied, 2)
            pe.sem_inc(multiplied, 2)
            for sem in {id(sem): sem for sem in [finished] + done}.values():
                pe.sem_inc(sem, 4)
            if constants:
                pe.wait_ge(constant, 16 * len(constants))

            def turn(t, q):
                if n_loads:
                    pe.wait_ge(loaded[q], uses4(t, q, 16 * n_loads))
                if prepare is not None:
                    pe.wait_ge(prepared, t + 1)
                pe.wait_ge(copied, t + 1)
                for i in range(kt):
                    last = pe.transpose(p_t[q % 2][:, i * P:(i + 1) * P], operand(i, q), k.ident[:, :])
                last.then_inc(turned, 1)

            def multiply(t, q):
                pe.wait_ge(copied, t + 3)
                pe.wait_ge(done[0], t + 3)
                for bank, n, weight in weights:
                    for i in range(kt):
                        last = pe.matmul(banks[q % 2][:, bank:bank + n], s.a_t[:, q % 2, i * P:(i + 1) * P],
                                         weight[:, i, :], start=(i == 0), stop=(i == kt - 1))
                last.then_inc(multiplied, 1)

            if extra:
                extra.begin(pe)
            in_turn(pe, (turn, 1), (multiply, 0),
                    *([(lambda t, q: extra.turn(pe, t, q), -lag), (lambda t, q: extra.multiply(pe, t, q), -lag - 1)] if extra else []))

        @block.scalar
        def _(act):
            def ready(t, q):
                act.wait_ge(turned, t + 1)
                prepare(act, t, q).then_inc(prepared, 1)

            def copy(t, q):
                act.wait_ge(turned, t + 5)
                act.wait_ge(multiplied, t + 1)
                act.copy(s.a_t[:, q % 2, :], p_t[q % 2][:, :]).then_inc(copied, 1)

            def root(i):
                def run(t, q):
                    act.wait_ge(done[i], t + 5)
                    roots[i](act, q).then_inc(rooted[i], 1)
                return run

            def last(t, q):
                act.wait_ge(done[-1], t + 5)
                output_free(act, t, q)
                if extra:
                    extra.slot_free(act, t)
                polish(act, t, q).then_inc(finished, 1)

            in_turn(act, *([(lambda t, q: extra.copy(act, t, q), -lag - 1)] if extra else []), *([] if prepare is None else [(ready, 2)]), (copy, 1),
                    *((root(i), -1 - i) for i in range(len(roots))),
                    *([] if polish is None else [(last, -1 - len(roots))]))


class FollowUp:

    def __init__(self, k, s, width, weight, source, made, offset):
        self.k, self.weight, self.source, self.made, self.offset = k, weight, source, made, offset
        self.a_t = s.sb("fu_a_t", [P, 2, F])
        self.p_t = [s.ps(f"fu_p_t{i}", [P, F]) for i in range(2)]
        self.banks = [s.ps(f"fu_bank{i}", [P, width]) for i in range(2)]
        self.turned, self.copied, self.multiplied, self.used = (
            s.sem("fu_" + n) for n in ("turned", "copied", "multiplied", "used"))

    def begin(self, pe):
        for sem, n in ((self.turned, 4), (self.used, 4), (self.copied, 2), (self.multiplied, 2)):
            pe.sem_inc(sem, n)

    def slot_free(self, eng, t):
        eng.wait_ge(self.turned, t + 1)
        eng.wait_ge(self.used, t + 1)

    def turn(self, pe, t, q):
        pe.wait_ge(self.made, t + (self.offset + 1))
        pe.wait_ge(self.copied, t + 1)
        for i in range(F // P):
            last = pe.transpose(self.p_t[q % 2][:, i * P:(i + 1) * P], self.source(i, q), self.k.ident[:, :])
        last.then_inc(self.turned, 1)

    def copy(self, act, t, q):
        act.wait_ge(self.turned, t + 5)
        act.wait_ge(self.multiplied, t + 1)
        act.copy(self.a_t[:, q % 2, :], self.p_t[q % 2][:, :]).then_inc(self.copied, 1)

    def multiply(self, pe, t, q):
        pe.wait_ge(self.copied, t + 3)
        pe.wait_ge(self.used, t + 3)
        for i in range(F // P):
            last = pe.matmul(self.banks[q % 2][:, :], self.a_t[:, q % 2, i * P:(i + 1) * P],
                             self.weight[:, i, :], start=(i == 0), stop=(i == F // P - 1))
        last.then_inc(self.multiplied, 1)

    def product(self, eng, t, q):
        eng.wait_ge(self.multiplied, t + 3)
        return self.banks[q % 2][:, :]


class Norm:
    MOMENTS, FACTORS = 1, 1

    def __init__(self, k, s):
        self.k = k
        self.st, self.mv = s.sb("ln_st", [P, 6]), s.sb("ln_mv", [P, 4, 2])
        self.passed = s.sem("ln_passed")
        self.std, self.rstd, self.shift = s.sb("ln_std", [P, 4]), s.sb("ln_rstd", [P, 4]), s.sb("ln_shift", [P, 4])

    def moments(self, dve, c, y, q):
        c.run(dve.bn_stats(self.st[:, :], y))
        dve.sem_inc(self.passed, 1)
        return dve.bn_aggr(self.mv[:, q, :], self.st[:, :])

    def root(self, act, q):
        return act.activation(self.std[:, q:q + 1], self.mv[:, q, 1:2], ACT.Sqrt, bias=self.k.eps_ln[:, :])

    def factors(self, dve, c, t, q):
        rstd = self.rstd[:, q:q + 1]
        c.run(dve.reciprocal(rstd, self.std[:, q:q + 1]))
        return dve.tensor_scalar(self.shift[:, q:q + 1], self.mv[:, q, 0:1], rstd, -1.0, ALU.mult, ALU.mult)

    def apply(self, act, y, out, q):
        return act.activation(out, y, ACT.Identity, bias=self.shift[:, q:q + 1], scale=self.rstd[:, q:q + 1])


def rows_of(table, t):
    return table[bass.ds(t * P, P), :]


def gat_projection(nc, k, w, inp, x0, h_table, src_table, background):
    with Scope(nc, "n0") as s:
        a = s.sb("a", [P, 4, F])
        w0 = s.sb("w0", [P, F // P, F])
        h = s.sb("h", [P, 4, F])
        banks = [s.ps(f"bank{i}", [P, 2 * F]) for i in range(2)]

        def finish(dve, c, t, q):
            dve.tensor_copy(col(w.node_logit, t * 2 * HEADS, 2 * HEADS), banks[q % 2][:, F:F + 2 * HEADS])
            return dve.tensor_copy(h[:, q, :], banks[q % 2][:, 0:F])

        node_pass(nc, k, s, F // P,
                  [(w0[:, :, :], inp["W0"].rearrange("(t p) n -> p t n", p=P))],
                  [(0, F, w0), (F, 2 * HEADS, w.w_ext)], banks,
                  lambda t, q: [(a[:, q, :], rows_of(x0, t))], 0,
                  lambda t, q: [(rows_of(h_table, t), h[:, q, :]),
                                (rows_of(src_table, t), col(w.node_logit, t * 2 * HEADS, HEADS))],
                  lambda i, q: a[:, q, i * P:(i + 1) * P], None, [(finish, 0)],
                  background=background(s))


def edge_logits(nc, k, w, rec):
    with Scope(nc, "lg") as s:
        pad = s.sb("pad", [P, TILES_PAD])
        both = s.sb("both", [P, NT, HEADS])
        own = s.sem("own")
        with nc.Block() as block:
            @block.vector
            def _(dve):
                c = Chain(dve, own)
                c.run(dve.tensor_scalar(pad[:, :], rec[:, :, R_LOCAL], 0.0, MASKED, ALU.is_lt, ALU.mult))
                for a in range(4):
                    for h in range(HEADS):
                        before = pad[:, :] if a == 0 else w.attr_logit[:, :, h]
                        last = dve.scalar_tensor_tensor(
                            w.attr_logit[:, :, h], rec[:, :, R_EA + a], w.v_edge[:, a, h:h + 1], before,
                            ALU.mult, ALU.add)
                    c.run(last)
                node = w.node_logit[:, :].rearrange("p (t h) -> p t h", h=2 * HEADS)
                c.run(dve.tensor_tensor(both[:, :, :], node[:, :, 0:HEADS], node[:, :, HEADS:2 * HEADS], ALU.add))
                c.run(dve.tensor_tensor(both[:, :, :], both[:, :, :], w.mean_logit[:, :].unsqueeze(1).broadcast_to(
                    [P, NT, HEADS]), ALU.add))
                dve.tensor_copy(w.dst_own[:, :, 0:HEADS], node[:, :, HEADS:2 * HEADS])
                dve.scalar_tensor_tensor(w.dst_own[:, :, HEADS:2 * HEADS], both[:, :, :], NEG_SLOPE, both[:, :, :],
                                         ALU.mult, ALU.max)
                c.run(dve.memset(w.above[:, :, :], 0.0))


class ByNode:

    def __init__(self, nc, k, s, rec, buckets, values, width, dt=FP):
        self.nc, self.k, self.rec, self.buckets, self.values = nc, k, rec, buckets, values
        self.index = s.sb("index", [P, 4, BT], I32)
        self.hot = s.sb("hot", [P, 4, BT, P])
        self.hot_t = s.sb("hot_t", [P, BT, P], dt)
        self.near = s.sb("near", [P, BT, width], dt)
        self.p_hot = s.ps("p_hot", [P, BT * P])
        self.p_node = s.ps("p_node", [P, BT, width])
        self.indexed, self.hot_ready, self.turned, self.copied, self.by_node = (
            s.sem(n) for n in ("indexed", "hot_ready", "turned", "copied", "by_node"))

    def stage_index(self, act, b, q):
        act.copy(self.index[:, q, :], col(self.rec[:, :, R_OTHER].bitcast(I32), b * BT, BT)).then_inc(self.indexed, 1)

    def make_hot(self, dve, b, q, n):
        dve.tensor_scalar(self.hot[:, q, n, :], self.k.columns[:, 0:P], col(self.rec[:, :, R_LOCAL], b * BT + n),
                          None, ALU.is_equal).then_inc(self.hot_ready, 1)

    def turn(self, pe, b, q, n):
        pe.wait_ge(self.hot_ready, b * BT + (n + 1))
        if n % 4 == 0 and (not isinstance(b, int) or b > 0):
            pe.wait_ge(self.copied, b * 2 + (n // 4 - 1))
        pe.transpose(self.p_hot[:, n * P:(n + 1) * P], self.hot[:, q, n, :],
                     self.k.ident[:, :]).then_inc(self.turned, 1)

    def copy_near(self, act, b, n):
        if n == 0:
            self.tile = bucket_registers(self.nc, mybir.EngineType.Activation, self.buckets, b * BT)
        if n % 4 == 0 and (not isinstance(b, int) or b > 0):
            act.wait_ge(self.by_node, b * 2 + (n // 4 - 1))
        for m in (n, n + 1):
            act.copy(self.near[:, m:m + 1, :], self.values[:, bass.ds(self.tile[m], 1), :])

    def copy_turned(self, act, b, half):
        act.wait_ge(self.turned, b * BT + 4 * (half + 1))
        act.copy(self.hot_t[:, 4 * half:4 * half + 4, :].rearrange("p n e -> p (n e)"),
                 self.p_hot[:, 4 * half * P:4 * (half + 1) * P]).then_inc(self.copied, 1)

    def find(self, pe, b, n):
        if n % 4 == 0:
            pe.wait_ge(self.copied, b * 2 + (n // 4 + 1))
        for m in (n, n + 1):
            last = pe.matmul(self.p_node[:, m, :], self.hot_t[:, m, :], self.near[:, m, :], start=True, stop=True)
        if n % 4 == 2:
            last.then_inc(self.by_node, 1)

    def dve_step(self, dve, g, q, n):
        self.make_hot(dve, g + 3, (q + 3) % 4, n)

    def pe_step(self, pe, g, q, n, taken):
        self.turn(pe, *later(g + 2, q + 2, n, BT - 2))
        if n == 2:
            taken(g + 1)
        if n in (2, 3, 5, 6):
            self.find(pe, g + 2, {2: 0, 3: 2, 5: 4, 6: 6}[n])

    def act_step(self, act, g, q, n):
        if n in (1, 5):
            self.copy_turned(act, g + 2, n // 4)
        if n in (0, 2):
            self.copy_near(act, g + 2, 2 * n)
        if n in (0, 3):
            self.copy_near(act, g + 2, {0: 2, 3: 6}[n])

    def dve_begin(self, dve):
        for b in range(3):
            for n in range(BT):
                self.make_hot(dve, b, b, n)

    def pe_begin(self, pe, taken):
        for b in range(2):
            for n in range(BT):
                self.turn(pe, b, b, n)
            if b > 0:
                taken(b - 1)
            for n in range(0, BT, 2):
                self.find(pe, b, n)
        for n in range(BT - 2):
            self.turn(pe, 2, 2, n)

    def act_begin(self, act):
        for b in range(2):
            for n in range(0, BT, 2):
                self.copy_near(act, b, n)
                if n % 4 == 2:
                    self.copy_turned(act, b, n // 4)


def attention_maxima(nc, k, w, rec, buckets, src_table, first, *where):
    DR, BANKS, AHEAD, DVE_HEADS = 6, 4, 4, 1
    with Scope(nc, "mx") as s:
        pre = ByNode(nc, k, s, rec, buckets, w.dst_own, 2 * HEADS)
        src = s.sb("src", [P, 4, BT, HEADS])
        over = s.sb("over", [P, 2, BT, HEADS])
        raw = s.sb("raw", [P, BT, HEADS])
        diag = s.sb("diag", [P, BT, HEADS, P])
        top = s.sb("top", [P, BT, HEADS])
        p_top = [s.ps(f"p_top{i}", [P, HEADS, P]) for i in range(BANKS)]
        gathered = [s.sem(f"gathered{q}") for q in range(4)]
        granted, logits, own, diag_dve, diag_act = (
            s.sem(n) for n in ("granted", "logits", "own", "diag_dve", "diag_act"))
        masked, reduced, raised = s.sem("masked"), s.sem("reduced"), s.sem("raised")

        with nc.Block() as block:
            @block.scalar
            def _(act):
                def spread(b, q, n):
                    act.wait_ge(logits, b + 3)
                    act.wait_ge(masked, b * BT + (n + 1 + BT))
                    for hd in range(DVE_HEADS, HEADS):
                        last = act.activation(diag[:, n, hd, :], k.ident[:, :], ACT.Copy,
                                              scale=over[:, q % 2, n, hd:hd + 1])
                    last.then_inc(diag_act, 1)

                def begin():
                    for b in range(3):
                        pre.stage_index(act, b, b)
                    pre.act_begin(act)
                    for n in range(AHEAD):
                        spread(0, 0, n)

                def step(g, q, n):
                    pre.act_step(act, g, q, n)
                    if n == 3:
                        act.wait_ge(logits, g + 2)
                        pre.stage_index(act, g + 3, (q + 3) % 4)
                    spread(*later(g, q, n, AHEAD))

                edge_steps(act, begin, step)

            @block.gpsimd
            def _(pool):
                def gather(b, q):
                    pool.wait_ge(pre.indexed, b + 1)
                    pool.sem_inc(granted, 1)
                    for n in range(BT):
                        pool.indirect_dma_start(
                            src[:, q, n, :], None, src_table,
                            bass.IndirectOffsetOnAxis(pre.index[:, q, n:n + 1], 0)).then_inc(gathered[q], 16)

                for b in range(3):
                    gather(b, b)
                scatter_by_batch(nc, s, pool, lambda g, q: gather(g + 3, (q + 3) % 4), first, *where)
                for q in range(4):
                    pool.wait_ge(gathered[q], (TILES // BT // 4 + (q < 3)) * BT * 16)

            @block.tensor
            def _(pe):
                def taken(b):
                    pe.wait_ge(logits, b + 3)

                def begin():
                    pe.sem_inc(masked, 2 * BT)
                    pe.sem_inc(reduced, BANKS)
                    pe.sem_inc(raised, 1)
                    pe.sem_inc(logits, 2)
                    pre.pe_begin(pe, taken)

                def step(g, q, n):
                    pe.wait_ge(diag_dve, g * BT + (n + 1))
                    pe.wait_ge(diag_act, g * BT + (n + 1))
                    pe.wait_ge(reduced, g * BT + (n + 1))
                    pe.matmul(p_top[n % BANKS][:, :, :], pre.hot[:, q, n, :], diag[:, n, :, :],
                              start=True, stop=True).then_inc(masked, 1)
                    pre.pe_step(pe, g, q, n, taken)

                edge_steps(pe, begin, step)

            @block.vector
            def _(dve):
                def make_logits(b, q, part):
                    logit = w.logit[:, bass.ds(b * BT, BT), :]
                    if part > 0:
                        dve.wait_ge(own, b * 3 + part)
                    if part == 0:
                        dve.wait_ge(gathered[q], (b - q) * (BT * 4) + BT * 16)
                        dve.wait_ge(pre.by_node, b * 2 + 2)
                        dve.tensor_tensor(raw[:, :, :], src[:, q, :, :], pre.p_node[:, :, 0:HEADS],
                                          ALU.add).then_inc(own, 1)
                    elif part == 1:
                        dve.tensor_tensor(raw[:, :, :], raw[:, :, :], w.attr_logit[:, bass.ds(b * BT, BT), :],
                                          ALU.add).then_inc(own, 1)
                    elif part == 2:
                        dve.scalar_tensor_tensor(logit, raw[:, :, :], NEG_SLOPE, raw[:, :, :], ALU.mult,
                                                 ALU.max).then_inc(own, 1)
                    else:
                        dve.tensor_tensor(over[:, q % 2, :, :], logit, pre.p_node[:, :, HEADS:2 * HEADS],
                                          ALU.subtract).then_inc(logits, 1)

                def spread(b, q, n):
                    dve.wait_ge(logits, b + 3)
                    dve.wait_ge(masked, b * BT + (n + 1 + BT))
                    dve.tensor_scalar(diag[:, n, 0, :], k.ident[:, :], over[:, q % 2, n, 0:1], None,
                                      ALU.mult).then_inc(diag_dve, 1)

                def begin():
                    pre.dve_begin(dve)
                    for part in range(4):
                        make_logits(0, 0, part)
                    for n in range(AHEAD):
                        spread(0, 0, n)

                def step(g, q, n):
                    if n == 0:
                        step.tile = bucket_registers(nc, mybir.EngineType.DVE, buckets, g * BT)
                    if n == 0:
                        make_logits(g + 1, (q + 1) % 4, 0)
                    pre.dve_step(dve, g, q, n)
                    if n == 0:
                        make_logits(g + 1, (q + 1) % 4, 1)
                    spread(*later(g, q, n, AHEAD))
                    if n == 0:
                        make_logits(g + 1, (q + 1) % 4, 2)
                    dve.wait_ge(masked, g * BT + (n + 1 + 2 * BT))
                    dve.tensor_reduce(top[:, n, :], p_top[n % BANKS][:, :, :], AX.X, ALU.max).then_inc(reduced, 1)
                    if n == 0:
                        make_logits(g + 1, (q + 1) % 4, 3)
                    for m in (n - 1, n)[n == 0:] if n == BT - 1 else (n - 1,)[n == 0:]:
                        dve.wait_ge(reduced, g * BT + (m + 1 + BANKS))
                        dve.wait_ge(raised, g * BT + (m + 1))
                        here = w.above[:, bass.ds(step.tile[m], 1), :]
                        dve.tensor_tensor(here, here, top[:, m, :].unsqueeze(1), ALU.max).then_inc(raised, 1)

                edge_steps(dve, begin, step)


def self_loops(nc, k, w, h_table, acc):
    with Scope(nc, "sl") as s:
        h = s.sb("h", [P, 4, F])
        loaded = [s.sem(f"loaded{q}") for q in range(4)]
        rest = s.sb("rest", [P, NT, HEADS])
        own, under, exped, used, split = (s.sem(n) for n in ("own", "under", "exped", "used", "split"))
        with nc.Block() as block:
            @block.sync
            def _(sp):
                sp.sem_inc(used, 4)

                def load(t, q):
                    sp.wait_ge(used, t + 1)
                    sp.dma_start(h[:, q, :], rows_of(h_table, t)).then_inc(loaded[q], 16)

                in_turn(sp, (load, 0))

            @block.scalar
            def _(act):
                act.wait_ge(under, 1)
                act.activation(w.self_weight[:, :, :], w.above[:, :, :], ACT.Exp, scale=-1.0).then_inc(exped, 1)

            @block.vector
            def _(dve):
                c = Chain(dve, own)
                dve.tensor_tensor(w.maximum[:, :, :], w.above[:, :, :], w.dst_own[:, :, HEADS:2 * HEADS],
                                  ALU.add).then_inc(under, 1)
                dve.memset(acc[:, :, F:ACCW], 0.0).then_inc(own, 1)
                dve.wait_ge(exped, 1)
                dve.wait_ge(own, 1)
                dve.tensor_copy(acc[:, :, DEN:DEN + HEADS], w.self_weight[:, :, :])
                dve.wait_ge(under, 1)
                c = Chain(dve, split)
                left = w.maximum[:, :, :]
                for i in range(3):
                    part = w.maximum_parts[:, :, i * HEADS:(i + 1) * HEADS]
                    c.run(dve.tensor_copy(part, left))
                    if i < 2:
                        c.run(dve.tensor_tensor(rest[:, :, :], left, part, ALU.subtract))
                    left = rest[:, :, :]

                def scale(t, q):
                    dve.wait_ge(loaded[q], uses4(t, q, 16))
                    dve.tensor_tensor(
                        acc[:, bass.ds(t, 1), 0:F].rearrange("p o (h c) -> p (o h) c", h=HEADS),
                        h[:, q, :].rearrange("p (h c) -> p h c", h=HEADS),
                        w.self_weight[:, bass.ds(t, 1), :].rearrange("p o h -> p (o h)").unsqueeze(2).broadcast_to(
                            [P, HEADS, C]), ALU.mult).then_inc(used, 1)

                in_turn(dve, (scale, 0))


def attention_sums(nc, k, w, rec, buckets, h_table, acc, first, *where):
    RING, AHEAD, DVE_HEADS = 2, 3, 2
    with Scope(nc, "at") as s:
        pre = ByNode(nc, k, s, rec, buckets, w.maximum_parts, 3 * HEADS, BF)
        rows = s.sb("rows", [P, BT, F])
        below, maximum = s.sb("below", [P, BT, HEADS]), s.sb("maximum", [P, BT, HEADS])
        att = s.sb("att", [P, 2, BT, HEADS + 1])
        part = [s.ps(f"part{i}", [P, 2 * F]) for i in range(RING)]
        gathered = [s.sem(f"gathered{n}") for n in range(BT)]
        granted, joined, shifted, exped = (s.sem(n) for n in ("granted", "joined", "shifted", "exped"))
        scaled_dve, scaled_act, summed, added = (
            s.sem(n) for n in ("scaled_dve", "scaled_act", "summed", "added"))

        with nc.Block() as block:
            @block.scalar
            def _(act):
                def scale(b, q, n):
                    act.wait_ge(exped, b + 1)
                    act.wait_ge(gathered[n], b * 16 + 16)
                    for hd in range(DVE_HEADS, HEADS):
                        head = rows[:, n, hd * C:(hd + 1) * C]
                        last = act.activation(head, head, ACT.Copy, scale=att[:, q % 2, n, hd:hd + 1])
                    last.then_inc(scaled_act, 1)

                def exponentials(b, q):
                    act.wait_ge(shifted, b + 1)
                    act.activation(att[:, q % 2, :, 0:HEADS], below[:, :, :], ACT.Exp).then_inc(exped, 1)

                def begin():
                    pre.stage_index(act, 0, 0)
                    pre.stage_index(act, 1, 1)
                    pre.act_begin(act)
                    exponentials(0, 0)
                    for n in range(AHEAD):
                        scale(0, 0, n)

                def step(g, q, n):
                    pre.act_step(act, g, q, n)
                    if n == 4:
                        exponentials(g + 1, (q + 1) % 4)
                        pre.stage_index(act, g + 2, (q + 2) % 4)
                    scale(*later(g, q, n, AHEAD))

                edge_steps(act, begin, step)

            @block.gpsimd
            def _(pool):
                def gather(b, q):
                    pool.wait_ge(pre.indexed, b + 1)
                    for n in range(BT):
                        pool.wait_ge(summed, b * BT + (n + 1 + BT))
                        pool.sem_inc(granted, 1)
                        pool.indirect_dma_start(
                            rows[:, n, :], None, h_table,
                            bass.IndirectOffsetOnAxis(pre.index[:, q, n:n + 1], 0)).then_inc(gathered[n], 16)

                gather(0, 0)
                scatter_by_batch(nc, s, pool, lambda g, q: gather(g + 1, (q + 1) % 4), first, *where)
                for n in range(BT):
                    pool.wait_ge(gathered[n], (TILES // BT + 1) * 16)

            @block.tensor
            def _(pe):
                def taken(b):
                    pe.wait_ge(shifted, b + 1)

                def begin():
                    pe.sem_inc(summed, 2 * BT)
                    pe.sem_inc(added, RING)
                    pre.pe_begin(pe, taken)

                def step(g, q, n):
                    pe.wait_ge(scaled_dve, g * BT + (n + 1))
                    pe.wait_ge(scaled_act, g * BT + (n + 1))
                    pe.wait_ge(added, g * BT + (n + 1))
                    pe.matmul(part[n % RING][:, 0:F], pre.hot[:, q, n, :], rows[:, n, :], start=True, stop=True)
                    pe.matmul(part[n % RING][:, F:F + HEADS + 1], pre.hot[:, q, n, :], att[:, q % 2, n, :],
                              start=True, stop=True).then_inc(summed, 1)
                    pre.pe_step(pe, g, q, n, taken)

                edge_steps(pe, begin, step)

            @block.vector
            def _(dve):
                def shift(b, q, waits=True):
                    dve.wait_ge(pre.by_node, b * 2 + 2)
                    if waits:
                        dve.wait_ge(exped, b)
                    dve.tensor_reduce(maximum[:, :, :], pre.p_node[:, :, :].rearrange("p n (i h) -> p n h i", i=3),
                                      AX.X, ALU.add).then_inc(joined, 1)
                    dve.tensor_copy(att[:, q % 2, :, HEADS], col(rec[:, :, R_W], b * BT, BT))
                    dve.wait_ge(joined, b + 1)
                    dve.tensor_tensor(below[:, :, :], w.logit[:, bass.ds(b * BT, BT), :], maximum[:, :, :],
                                      ALU.subtract).then_inc(shifted, 1)

                def scale(b, q, n):
                    dve.wait_ge(exped, b + 1)
                    dve.wait_ge(gathered[n], b * 16 + 16)
                    heads = rows[:, n, 0:DVE_HEADS * C].rearrange("p (h c) -> p h c", h=DVE_HEADS)
                    dve.tensor_tensor(heads, heads, att[:, q % 2, n, 0:DVE_HEADS].unsqueeze(2).broadcast_to(
                        [P, DVE_HEADS, C]), ALU.mult).then_inc(scaled_dve, 1)

                def begin():
                    pre.dve_begin(dve)
                    shift(0, 0, waits=False)
                    for n in range(AHEAD):
                        scale(0, 0, n)

                def step(g, q, n):
                    if n == 0:
                        step.tile = bucket_registers(nc, mybir.EngineType.DVE, buckets, g * BT)
                    pre.dve_step(dve, g, q, n)
                    scale(*later(g, q, n, AHEAD))
                    dve.wait_ge(summed, g * BT + (n + 1 + 2 * BT))
                    dve.wait_ge(added, g * BT + (n + RING))
                    here = acc[:, bass.ds(step.tile[n], 1), 0:F + HEADS + 1]
                    dve.tensor_tensor(here, here, part[n % RING][:, 0:F + HEADS + 1].unsqueeze(1),
                                      ALU.add).then_inc(added, 1)
                    if n == 0:
                        shift(g + 1, (q + 1) % 4)

                edge_steps(dve, begin, step)


def batch_norm(nc, k, w, inp, acc):
    with Scope(nc, "bn") as s:
        bias, gamma = s.sb("bias", [P, F]), s.sb("gamma", [P, F])
        rden, deg, has = s.sb("rden", [P, NT, HEADS]), s.sb("deg", [P, NT]), s.sb("has", [P, NT])
        mean, std = s.sb("mean", [P, F]), s.sb("std", [P, F])
        square = s.sb("square", [P, 2, F])
        p_sum, p_var = s.ps("p_sum", [P, F]), s.ps("p_var", [P, F])
        loaded, own, ready, summed, centred = (s.sem(n) for n in ("loaded", "own", "ready", "summed", "centred"))
        squared, added, rooted, asked = s.sem("squared"), s.sem("added"), s.sem("rooted"), s.sem("asked")
        GROUP = 5
        with nc.Block() as block:
            @block.sync
            def _(sp):
                sp.dma_start(bias[:, :], inp["bias"].partition_broadcast(P)).then_inc(loaded, 16)
                sp.dma_start(gamma[:, :], inp["gamma"].partition_broadcast(P)).then_inc(loaded, 16)

            @block.tensor
            def _(pe):
                for t in range(NT):
                    pe.wait_ge(ready, t // GROUP + 1)
                    last = pe.matmul(p_sum[:, :], (k.ones if t < NT - 1 else k.last_rows)[:, :],
                                     acc[:, t, 0:F], start=(t == 0), stop=(t == NT - 1))
                last.then_inc(summed, 1)
                for t in range(NT):
                    pe.wait_ge(squared, t + 1)
                    pe.matmul(p_var[:, :], (k.ones if t < NT - 1 else k.last_rows)[:, :],
                              square[:, t % 2, :], start=(t == 0), stop=(t == NT - 1)).then_inc(added, 1)

            @block.scalar
            def _(act):
                act.wait_ge(asked, 1)
                act.activation(w.dinv[:, :], deg[:, :], ACT.Sqrt).then_inc(rooted, 1)
                for t in range(NT):
                    act.wait_ge(centred, t // GROUP + 1)
                    if t >= 2:
                        act.wait_ge(added, t - 1)
                    act.activation(square[:, t % 2, :], acc[:, t, 0:F], ACT.Square).then_inc(squared, 1)
                act.wait_ge(added, NT)
                act.activation(std[:, :], p_var[:, :], ACT.Sqrt, bias=k.eps_bn[:, :],
                               scale=1.0 / N_NODES).then_inc(rooted, 1)

            @block.vector
            def _(dve):
                c = Chain(dve, own)
                c.run(dve.tensor_scalar(rden[:, :, :], acc[:, :, DEN:DEN + HEADS], EPS_DEN, None, ALU.add))
                c.run(dve.reciprocal(rden[:, :, :], rden[:, :, :]))
                dve.wait_ge(loaded, 32)
                for g in range(0, NT, GROUP):
                    for t in range(g, g + GROUP):
                        for h in range(HEADS):
                            head = acc[:, t, h * C:(h + 1) * C]
                            last = dve.scalar_tensor_tensor(head, head, rden[:, t, h:h + 1],
                                                            bias[:, h * C:(h + 1) * C], ALU.mult, ALU.add)
                    last.then_inc(ready, 1)
                c.run(dve.tensor_scalar(w.rdeg[:, :], acc[:, :, DEG], 1.0, None, ALU.max))
                c.run(dve.reciprocal(w.rdeg[:, :], w.rdeg[:, :]))
                c.run(dve.tensor_scalar(deg[:, :], acc[:, :, DEG], 1.0, None, ALU.add))
                dve.tensor_scalar(has[:, :], deg[:, :], 0.0, None, ALU.is_gt)
                dve.tensor_scalar(deg[:, :], deg[:, :], TINY, None, ALU.max).then_inc(asked, 1)
                dve.wait_ge(rooted, 1)
                c.run(dve.reciprocal(w.dinv[:, :], w.dinv[:, :]))
                c.run(dve.tensor_tensor(w.dinv[:, :], w.dinv[:, :], has[:, :], ALU.mult))
                dve.wait_ge(ready, NT // GROUP)
                dve.wait_ge(summed, 1)
                c.run(dve.tensor_scalar(mean[:, :], p_sum[:, :], 1.0 / N_NODES, None, ALU.mult))
                for g in range(0, NT, GROUP):
                    here = acc[:, g:g + GROUP, 0:F]
                    dve.tensor_tensor(here, here, mean[:, :].unsqueeze(1).broadcast_to([P, GROUP, F]),
                                      ALU.subtract).then_inc(centred, 1)
                dve.wait_ge(rooted, 2)
                c.run(dve.reciprocal(std[:, :], std[:, :]))
                dve.tensor_tensor(w.bn_scale[:, :], std[:, :], gamma[:, :], ALU.mult)


def gat_output(nc, k, w, inp, x0, x1, table, acc, background):
    with Scope(nc, "n1") as s:
        beta, w1 = s.sb("beta", [P, F]), s.sb("w1", [P, F // P, HID])
        x, y, out = s.sb("x", [P, 4, F]), s.sb("y", [P, 4, F]), s.sb("out", [P, 4, F])
        scaled = s.sb("scaled", [P, 4, F])
        norm = Norm(k, s)
        constant, landed = s.sem("constant"), s.sem("landed")
        loaded = [s.sem(f"loaded{q}") for q in range(4)]
        stored = [s.sem(f"stored{q}") for q in range(4)]
        own, own_f, biased, added, rooted, normed, applied, made = (
            s.sem(n) for n in ("own", "own_f", "biased", "added", "rooted", "normed", "applied", "made"))
        product = FollowUp(k, s, HID, w1, lambda i, q: scaled[:, q, i * P:(i + 1) * P], made, 0)
        with nc.Block() as block:
            @block.sync
            def _(sp):
                sp.dma_start(beta[:, :], inp["beta"].partition_broadcast(P)).then_inc(constant, 16)
                sp.dma_start(w1[:, :, :], inp["W1"].rearrange("(t p) n -> p t n", p=P)).then_inc(constant, 16)
                for sem in (added, applied):
                    sp.sem_inc(sem, 4)
                for q in range(4):
                    sp.sem_inc(stored[q], 16)

                def load(t, q):
                    sp.wait_ge(added, t + 1)
                    sp.dma_start(x[:, q, :], rows_of(x0, t)).then_inc(loaded[q], 16)

                def store_x1(t, q):
                    sp.wait_ge(applied, t + 5)
                    sp.dma_start(rows_of(x1, t), out[:, q, :]).then_inc(stored[q], 16)

                def store_table(t, q):
                    sp.wait_ge(product.used, t + 5)
                    sp.dma_start(rows_of(table, t), acc[:, bass.ds(t, 1), 0:HID]).then_inc(landed, 16)

                in_turn(sp, (load, 4), (store_x1, -1), (store_table, -4))
                sp.wait_ge(landed, NT * 16)
                for q in range(4):
                    sp.wait_ge(stored[q], (1 + (NT + 3 - q) // 4) * 16)

            block.gpsimd(background(s))

            @block.tensor
            def _(pe):
                product.begin(pe)
                pe.wait_ge(constant, 32)
                in_turn(pe, (lambda t, q: product.turn(pe, t, q), -2), (lambda t, q: product.multiply(pe, t, q), -3))

            @block.vector
            def _(dve):
                dve.wait_ge(constant, 32)

                def bias(t, q):
                    here = acc[:, bass.ds(t, 1), 0:F].rearrange("p o f -> p (o f)")
                    dve.wait_ge(loaded[q], uses4(t, q, 16))
                    dve.wait_ge(applied, t + 1)
                    dve.tensor_tensor(x[:, q, :], x[:, q, :], beta[:, :], ALU.add)
                    dve.tensor_tensor(y[:, q, :], here, w.bn_scale[:, :], ALU.mult).then_inc(biased, 1)

                def add(t, q):
                    c = Chain(dve, own, t * (1 + norm.MOMENTS))
                    dve.wait_ge(biased, t + 1)
                    c.run(dve.tensor_tensor(y[:, q, :], y[:, q, :], x[:, q, :], ALU.add))
                    norm.moments(dve, c, y[:, q, :], q).then_inc(added, 1)

                def factors(t, q):
                    dve.wait_ge(rooted, t + 1)
                    norm.factors(dve, Chain(dve, own_f, t * norm.FACTORS), t, q).then_inc(normed, 1)

                in_turn(dve, (bias, 1), (add, 0), (factors, -1))

            @block.scalar
            def _(act):
                def root(t, q):
                    act.wait_ge(added, t + 5)
                    norm.root(act, q).then_inc(rooted, 1)

                def apply(t, q):
                    act.wait_ge(normed, t + 1)
                    act.wait_ge(stored[q], uses4(t, q, 16))
                    norm.apply(act, y[:, q, :], out[:, q, :], q).then_inc(applied, 1)

                def scale(t, q):
                    act.wait_ge(applied, t + 5)
                    product.slot_free(act, t)
                    act.activation(scaled[:, q, :], out[:, q, :], ACT.Copy, scale=col(w.dinv, t)).then_inc(made, 1)

                def take(t, q):
                    act.copy(acc[:, bass.ds(t, 1), 0:HID], product.product(act, t, q).unsqueeze(1)).then_inc(
                        product.used, 1)

                in_turn(act, (root, 0), (apply, -1), (scale, -2), (lambda t, q: product.copy(act, t, q), -3), (take, -4))


def gcn_hidden(nc, w, b1, table, acc):
    with Scope(nc, "n2") as s:
        hid = s.sb("hid", [P, 4, HID])
        biased, scaled, stored = (s.sem(n) for n in ("biased", "scaled", "stored"))
        with nc.Block() as block:
            @block.sync
            def _(sp):
                def store(t, q):
                    sp.wait_ge(scaled, t + 1)
                    sp.dma_start(rows_of(table, t), acc[:, bass.ds(t, 1), 0:HID]).then_inc(stored, 16)

                in_turn(sp, (store, 0))
                sp.wait_ge(stored, NT * 16)

            @block.vector
            def _(dve):
                def bias(t, q):
                    dve.scalar_tensor_tensor(hid[:, q, :].unsqueeze(1), acc[:, bass.ds(t, 1), 0:HID], col(w.dinv, t),
                                             b1[:, :].unsqueeze(1), ALU.mult, ALU.add).then_inc(biased, 1)

                def relu(t, q):
                    dve.wait_ge(biased, t + 1)
                    dve.tensor_scalar(acc[:, bass.ds(t, 1), 0:HID], hid[:, q, :].unsqueeze(1), 0.0, col(w.dinv, t),
                                      ALU.max, ALU.mult).then_inc(scaled, 1)

                in_turn(dve, (bias, 1), (relu, 0))


def gcn_output(nc, k, w, w2, b2, w_self, b_self, x1, x2, self_part, acc, background):
    with Scope(nc, "n3") as s:
        a = s.sb("a", [P, 4, HID])
        x = s.sb("x", [P, 4, F])
        y, out = s.sb("y", [P, 4, F]), s.sb("out", [P, 4, F])
        biased = s.sem("biased")
        ms, length, rlen = s.sb("ms", [P, 4]), s.sb("length", [P, 4]), s.sb("rlen", [P, 1])
        norm = Norm(k, s)
        banks = [s.ps(f"bank{i}", [P, F]) for i in range(2)]

        def prepare(act, t, q):
            return act.activation(a[:, q, :].unsqueeze(1), acc[:, bass.ds(t, 1), 0:HID], ACT.Copy,
                                  scale=col(w.dinv, t))

        def product(dve, c, t, q):
            here = y[:, q, :]
            c.run(dve.tensor_tensor(here, banks[q % 2][:, :], b2[:, :], ALU.add))
            c.run(norm.moments(dve, c, here, q))
            mean = norm.mv[:, q, 0:1]
            return dve.scalar_tensor_tensor(ms[:, q:q + 1], mean, mean, norm.mv[:, q, 1:2], ALU.mult, ALU.add)

        def take(dve, t, q, product):
            here = self_part[:, bass.ds(t, 1), :]
            dve.tensor_tensor(here, product.unsqueeze(1), b_self[:, :].unsqueeze(1), ALU.add).then_inc(biased, 1)
            dve.wait_ge(biased, t + 1)
            return dve.tensor_tensor(here, here, out[:, q, :].unsqueeze(1), ALU.add)

        def root(act, q):
            return act.activation(length[:, q:q + 1], ms[:, q:q + 1], ACT.Sqrt, scale=float(F))

        def add(dve, c, t, q):
            here = y[:, q, :]
            c.run(dve.tensor_scalar(length[:, q:q + 1], length[:, q:q + 1], EPS_NORM, None, ALU.max))
            c.run(dve.reciprocal(rlen[:, :], length[:, q:q + 1]))
            c.run(dve.scalar_tensor_tensor(here, here, rlen[:, :], x[:, q, :], ALU.mult, ALU.add))
            return norm.moments(dve, c, here, q)

        node_pass(nc, k, s, HID // P, [], [(0, F, w2)], banks, lambda t, q: [(x[:, q, :], rows_of(x1, t))], 1,
                  lambda t, q: [(rows_of(x2, t), out[:, q, :])],
                  lambda i, q: a[:, q, i * P:(i + 1) * P], prepare,
                  [(product, 2 + norm.MOMENTS), (add, 3 + norm.MOMENTS), (norm.factors, norm.FACTORS)],
                  [root, norm.root],
                  lambda act, t, q: norm.apply(act, y[:, q, :], out[:, q, :], q), background(s),
                  (w_self, lambda i, q: out[:, q, i * P:(i + 1) * P], take))


def sage_output(nc, k, w, w_neigh, b, self_part, x3, acc, background):
    with Scope(nc, "n4") as s:
        a = s.sb("a", [P, 4, F])
        y, out = s.sb("y", [P, 4, F]), s.sb("out", [P, 4, F])
        norm = Norm(k, s)
        banks = [s.ps(f"bank{i}", [P, F]) for i in range(2)]

        def prepare(act, t, q):
            return act.activation(a[:, q, :].unsqueeze(1), acc[:, bass.ds(t, 1), 0:F], ACT.Copy,
                                  scale=col(w.rdeg, t))

        def finish(dve, c, t, q):
            here = y[:, q, :]
            c.run(dve.tensor_tensor(here, banks[q % 2][:, :], b[:, :], ALU.add))
            c.run(dve.tensor_tensor(here.unsqueeze(1), here.unsqueeze(1), self_part[:, bass.ds(t, 1), :], ALU.add))
            return norm.moments(dve, c, here, q)

        node_pass(nc, k, s, F // P, [], [(0, F, w_neigh)], banks, lambda t, q: [], 0,
                  lambda t, q: [(rows_of(x3, t), out[:, q, :])],
                  lambda i, q: a[:, q, i * P:(i + 1) * P],
                  prepare, [(finish, 2 + norm.MOMENTS), (norm.factors, norm.FACTORS)], [norm.root],
                  lambda act, t, q: norm.apply(act, y[:, q, :], out[:, q, :], q), background(s))


def conv_output(nc, k, w3, b3, x3, result, acc):
    with Scope(nc, "n5") as s:
        a = s.sb("a", [P, 4, F])
        x = s.sb("x", [P, 4, F])
        y, out = s.sb("y", [P, 4, F]), s.sb("out", [P, 4, F])
        norm = Norm(k, s)
        banks = [s.ps(f"bank{i}", [P, F]) for i in range(2)]

        def prepare(act, t, q):
            return act.copy(a[:, q, :].unsqueeze(1), acc[:, bass.ds(t, 1), 0:F])

        def finish(dve, c, t, q):
            here = y[:, q, :]
            c.run(dve.tensor_tensor(here, banks[q % 2][:, :], b3[:, :], ALU.add))
            c.run(dve.tensor_tensor(here, here, x[:, q, :], ALU.add))
            return norm.moments(dve, c, here, q)

        def store(t, q):
            rows = P if not isinstance(t, int) or t < NT - 1 else LAST_ROWS
            return [(result[bass.ds(t * P, rows), :], out[0:rows, q, :])]

        node_pass(nc, k, s, F // P, [], [(0, F, w3)], banks, lambda t, q: [(x[:, q, :], rows_of(x3, t))], 0, store,
                  lambda i, q: a[:, q, i * P:(i + 1) * P], prepare,
                  [(finish, 2 + norm.MOMENTS), (norm.factors, norm.FACTORS)], [norm.root],
                  lambda act, t, q: norm.apply(act, y[:, q, :], out[:, q, :], q))


def build(nc, inp, result):
    class Held:
        pass

    def dram(name, shape):
        return nc.dram_tensor(name, shape, FP).ap()

    by_dst, by_src = dram("edges_by_dst", [P * TC, REC]), dram("edges_by_src", [P * TC, REC_SRC])
    h_table, src_table = dram("h_table", [NODES_PAD, F]), dram("src_table", [NODES_PAD, HEADS])
    x1_w1, scaled_hid = dram("x1_scaled_w1", [NODES_PAD, HID]), dram("hidden_scaled", [NODES_PAD, HID])
    x0 = inp["x"]
    x1, x2, x3 = (dram(n, [NODES_PAD, F]) for n in ("x1", "x2", "x3"))

    with Scope(nc, "k") as held:
        k, w = Held(), Held()
        k.ident, k.before = held.sb("ident", [P, P]), held.sb("before", [P, P])
        k.ones, k.last_rows = held.sb("ones", [P, P]), held.sb("last_rows", [P, P])
        k.columns, k.pad_slot = held.sb("columns", [P, TILES_PAD]), held.sb("pad_slot", [P, EC])
        k.eps_ln, k.eps_bn = held.sb("eps_ln", [P, 1]), held.sb("eps_bn", [P, 1])
        w.w_ext = held.sb("w_ext", [P, F // P, 2 * HEADS])
        w.v_edge, w.mean_logit = held.sb("v_edge", [P, 4, HEADS]), held.sb("mean_logit", [P, HEADS])
        w.node_logit = held.sb("node_logit", [P, NT * 2 * HEADS])
        w.dst_own = held.sb("dst_own", [P, NT, 2 * HEADS])
        w.above, w.maximum = held.sb("above", [P, NT, HEADS]), held.sb("maximum", [P, NT, HEADS])
        w.maximum_parts = held.sb("maximum_parts", [P, NT, 3 * HEADS], BF)
        w.self_weight = held.sb("self_weight", [P, NT, HEADS])
        w.bn_scale = held.sb("bn_scale", [P, F])
        w.dinv, w.rdeg = held.sb("dinv", [P, NT]), held.sb("rdeg", [P, NT])
        dst_tiles, src_tiles = (held.sb(n, [P, TILES_PAD], I32) for n in ("dst_tiles", "src_tiles"))

        src_records, src_slots = held.sb("src_records", [P, EC, REC_SRC]), held.sb("src_slots", [P, EC], I32)
        with Scope(nc, "sort") as srt:
            w.records = srt.sb("records", [P, EC, REC])
            slots = srt.sb("slots", [P, EC], I32)
            blank = srt.sb("blank", [P, TC * REC])
            to_dst = (w.records, slots, by_dst, REC)
            constants(nc, k, blank)
            cuts = (0, 4, 10, 20, EC // BT)
            behind = [lambda s, a=a, b=b: scatter_steps(nc, s, a, b - a, *to_dst)
                      for a, b in zip(cuts, cuts[1:])]
            place(nc, k, "pd", inp["dst"], slots, dst_tiles, w.records, inp["src"],
                  (w.records[:, :, :].rearrange("p c f -> p (c f)"), inp["edges"]), None,
                  [(table.rearrange("(l t) f -> l (t f)", l=P), blank[:, 0:TC * words])
                   for table, words in ((by_dst, REC), (by_src, REC_SRC))], behind[0])
            setup(nc, k, inp, w, behind[1])
            place(nc, k, "ps", inp["src"], src_slots, src_tiles, src_records, inp["dst"], None, w.records, [],
                  behind[2])
            gat_projection(nc, k, w, inp, x0, h_table, src_table, behind[3])
        rec_src = held.sb("rec_src", [P, TILES_PAD, REC_SRC])
        rec = held.sb("rec", [P, TILES_PAD, REC])
        acc = held.sb("acc", [P, NT, ACCW])
        to_src = (src_records, src_slots, by_src, REC_SRC)
        shares = (3, 6, 3)
        assert (4 + sum(shares)) * NT == EC
        behind = [lambda s, at=(4 + sum(shares[:i])) * NT, each=each: scatter_by_tile(nc, s, at, each, *to_src)
                  for i, each in enumerate(shares)]
        load_records(nc, "ld", by_dst, rec, REC)
        with Scope(nc, "gat") as gat:
            w.attr_logit = gat.sb("attr_logit", [P, TILES_PAD, HEADS])
            w.logit = gat.sb("logit", [P, TILES_PAD, HEADS])
            edge_logits(nc, k, w, rec)
            attention_maxima(nc, k, w, rec, dst_tiles, src_table, 0, *to_src)
            self_loops(nc, k, w, h_table, acc)
            attention_sums(nc, k, w, rec, dst_tiles, h_table, acc, 2 * NT, *to_src)
        batch_norm(nc, k, w, inp, acc)
        gat_output(nc, k, w, inp, x0, x1, x1_w1, acc, behind[0])

        def weight(scope, name, source, rows, width):
            to = scope.sb(name, [P, rows // P, width])
            return to, (to[:, :, :], inp[source].rearrange("(t p) n -> p t n", p=P))

        def bias(scope, name, width):
            to = scope.sb(name, [P, width])
            return to, (to[:, :], inp[name].partition_broadcast(P))

        with Scope(nc, "wb") as wb:
            b1, load_b1 = bias(wb, "b1", HID)
            aggregate(nc, k, "g1", rec, dst_tiles, x1_w1, HID, acc, clear=False, fetch=[load_b1])
            gcn_hidden(nc, w, b1, scaled_hid, acc)
        with Scope(nc, "wc") as wc:
            w2, load_w2 = weight(wc, "w2", "W2", HID, F)
            b2, load_b2 = bias(wc, "b2", F)
            w_self, load_w_self = weight(wc, "w_self", "W_self_t", F, F)
            b_self, load_b_self = bias(wc, "b_self", F)
            w_neigh, load_w_neigh = weight(wc, "w_neigh", "W_neigh_t", F, F)
            b_neigh, load_b_neigh = bias(wc, "b_neigh", F)
            self_part = wc.sb("self_part", [P, NT, F])
            aggregate(nc, k, "g2", rec, dst_tiles, scaled_hid, HID, acc, clear=False,
                      fetch=[load_w2, load_b2, load_w_self, load_b_self, load_w_neigh, load_b_neigh])
            gcn_output(nc, k, w, w2, b2, w_self, b_self, x1, x2, self_part, acc, behind[1])
            aggregate(nc, k, "g3", rec, dst_tiles, x2, F, acc, clear=True)
            sage_output(nc, k, w, w_neigh, b_neigh, self_part, x3, acc, behind[2])
        load_records(nc, "ld2", by_src, rec_src, REC_SRC)
        with Scope(nc, "wd") as wd:
            w3, load_w3 = weight(wd, "w3", "W3", F, F)
            b3, load_b3 = bias(wd, "b3", F)
            aggregate(nc, k, "g4", rec_src, src_tiles, x3, F, acc, clear=True, fetch=[load_w3, load_b3])
            conv_output(nc, k, w3, b3, x3, result, acc)


def kernel(x, src, dst, edge_attr_4, edge_weight, L0_gnn_W, L0_gnn_W_edge, L0_gnn_att_src, L0_gnn_att_dst,
           L0_gnn_att_edge, L0_gnn_bias, L0_gnn_gamma, L0_gnn_beta, L1_gnn_W1, L1_gnn_b1, L1_gnn_W2, L1_gnn_b2,
           L2_gnn_W_self, L2_gnn_b_self, L2_gnn_W_neigh, L2_gnn_b_neigh, L3_gnn_weight, L3_gnn_bias):
    import numpy as np
    import concourse.bacc as bacc
    from concourse.bass_utils import run_bass_kernel_spmd

    arrays = laid_out(np, locals())
    nc = bacc.Bacc("TRN2", target_bir_lowering=False, num_devices=1)
    inp = {name: nc.dram_tensor("in_" + name, a.shape, mybir.dt.from_np(a.dtype), kind="ExternalInput").ap()
           for name, a in arrays.items()}
    result = nc.dram_tensor("out_x", (N_NODES, F), FP, kind="ExternalOutput").ap()
    build(nc, inp, result)
    r = run_bass_kernel_spmd(nc, [{"in_" + name: a for name, a in arrays.items()}], core_ids=[0])
    return r.results[0]["out_x"]


def laid_out(np, a):
    x = np.zeros((NODES_PAD, F), np.float32)
    x[:N_NODES] = np.asarray(a["x"])
    edges = np.zeros((EDGES_PAD, REC), np.float32)
    edges[:N_EDGES, R_W] = np.asarray(a["edge_weight"])
    edges[:N_EDGES, R_EA:R_EA + 4] = np.asarray(a["edge_attr_4"])

    def padded(index):
        out = np.full(EDGES_PAD, NODES_PAD, np.int32)
        out[:N_EDGES] = np.asarray(index)
        return out.reshape(P, EC)

    def flat(name):
        return np.ascontiguousarray(np.asarray(a[name])).reshape(-1)

    def rows(name):
        return np.ascontiguousarray(np.asarray(a[name]))

    def turned(name):
        return np.ascontiguousarray(np.asarray(a[name]).T)

    return {
        "x": x, "edges": edges.reshape(P, EC * REC), "src": padded(a["src"]), "dst": padded(a["dst"]),
        "W0": rows("L0_gnn_W"), "W_edge": flat("L0_gnn_W_edge"), "att_src": flat("L0_gnn_att_src"),
        "att_dst": flat("L0_gnn_att_dst"), "att_edge": flat("L0_gnn_att_edge"), "bias": flat("L0_gnn_bias"),
        "gamma": flat("L0_gnn_gamma"), "beta": flat("L0_gnn_beta"), "W1": rows("L1_gnn_W1"),
        "b1": flat("L1_gnn_b1"), "W2": rows("L1_gnn_W2"), "b2": flat("L1_gnn_b2"),
        "W_self_t": turned("L2_gnn_W_self"), "b_self": flat("L2_gnn_b_self"),
        "W_neigh_t": turned("L2_gnn_W_neigh"), "b_neigh": flat("L2_gnn_b_neigh"),
        "W3": rows("L3_gnn_weight"), "b3": flat("L3_gnn_bias"),
    }
```
